# Optimizing a Trainium2 kernel written in Bass

```python
import numpy as np
import jax
import jax.numpy as jnp

def _softmax(x, axis=-1):
    return jax.nn.softmax(x, axis=axis)

def _gelu(x):
    return jax.nn.gelu(x, approximate=True)

def _silu(x):
    return jax.nn.silu(x)

def _sigmoid(x):
    return jax.nn.sigmoid(x)

def _layernorm(x, axis=-1, eps=1e-05):
    m = jnp.mean(x, axis=axis, keepdims=True)
    v = jnp.var(x, axis=axis, keepdims=True)
    return (x - m) / jnp.sqrt(v + eps)

def _scatter_add(tgt, idx, src, axis=0):
    return tgt.at[idx].add(src)

def _segment_sum(src, seg, n):
    return jax.ops.segment_sum(src, seg, n)
kernel_name = 'mk_gps_d1_gnn_r8_bf3e38'

def setup_inputs(seed: int=0):
    np.random.seed(seed)
    _w = jnp.asarray

    def _rec_inputs():
        import jax
        import jax.numpy as jnp
        _gk = jax.random.key(seed)
        x = -0.0001126 + 1 * jax.random.normal(jax.random.fold_in(_gk, 1), (1250, 768), jnp.float32)
        _s = jax.random.randint(jax.random.fold_in(_gk, 2), (10000,), 0, 1250, jnp.int32)
        _d = jax.random.randint(jax.random.fold_in(_gk, 3), (10000,), 0, 1250, jnp.int32)
        _loop = jnp.arange(1250, dtype=jnp.int32)
        src = jnp.concatenate([_s, _d, _loop])
        dst = jnp.concatenate([_d, _s, _loop])
        _o = jnp.argsort(dst, stable=True)
        src = src[_o]
        dst = dst[_o]
        return (x, src, dst)
    x, src, dst = _rec_inputs()

    def _L0_gnn_setup():
        import jax, jax.numpy as jnp
        import numpy as np
        N = 1250
        E = 20000
        D = 768
        H1, C1 = (4, 192)
        H2, C2 = (2, 96)
        EPS = 1e-05
        NEG_SLOPE = 0.2

        def layer_norm(x, g, b):
            mu = x.mean(-1, keepdims=True)
            var = ((x - mu) ** 2).mean(-1, keepdims=True)
            return (x - mu) * jax.lax.rsqrt(var + EPS) * g + b

        def gat_conv(x, src, dst, W, a_src, a_dst, bias, H, C, n):
            h = (x @ W).reshape(n, H, C)
            s_src = (h * a_src).sum(-1)
            s_dst = (h * a_dst).sum(-1)
            e = jax.nn.leaky_relu(s_src[src] + s_dst[dst], NEG_SLOPE)
            emax = jax.ops.segment_max(e, dst, num_segments=n)
            ee = jnp.exp(e - emax[dst])
            denom = jax.ops.segment_sum(ee, dst, num_segments=n)
            alpha = ee / denom[dst]
            out = jax.ops.segment_sum(alpha[:, :, None] * h[src], dst, num_segments=n)
            return out.reshape(n, H * C) + bias
        key = jax.random.key(seed)
        ks = jax.random.split(key, 16)
        sd = 1.0 / np.sqrt(D)
        inp = {'x': jax.random.normal(ks[0], (N, D), jnp.float32), 'edge_index': jax.random.randint(ks[1], (2, E), 0, N, jnp.int64), 'norm_g': jnp.ones((D,), jnp.float32), 'norm_b': jnp.zeros((D,), jnp.float32), 'W1': jax.random.normal(ks[2], (D, H1 * C1), jnp.float32) * sd, 'a_src1': jax.random.normal(ks[3], (H1, C1), jnp.float32) * sd, 'a_dst1': jax.random.normal(ks[4], (H1, C1), jnp.float32) * sd, 'b1': jnp.zeros((H1 * C1,), jnp.float32), 'W2': jax.random.normal(ks[5], (H1 * C1, H2 * C2), jnp.float32) * sd, 'a_src2': jax.random.normal(ks[6], (H2, C2), jnp.float32) * sd, 'a_dst2': jax.random.normal(ks[7], (H2, C2), jnp.float32) * sd, 'b2': jnp.zeros((H2 * C2,), jnp.float32), 'Wu': jax.random.normal(ks[8], (D + H2 * C2, D), jnp.float32) / np.sqrt(D + H2 * C2), 'bu': jnp.zeros((D,), jnp.float32)}
        return inp
    _L0_gnn_all = _L0_gnn_setup()
    _L0_gnn_in = {k: v for k, v in _L0_gnn_all.items() if k in ('norm_g', 'norm_b', 'W1', 'a_src1', 'a_dst1', 'b1', 'W2', 'a_src2', 'a_dst2', 'b2', 'Wu', 'bu')}
    del _L0_gnn_all

    def _L0_mix_setup():
        import jax, jax.numpy as jnp
        import numpy as np
        DIM = 768
        NUM_HEADS = 12
        HEAD_DIM = DIM // NUM_HEADS
        HIDDEN = int(DIM * 4.0)
        EPS = 1e-08

        def layer_norm(x, w, b):
            mu = jnp.mean(x, axis=-1, keepdims=True)
            var = jnp.mean(jnp.square(x - mu), axis=-1, keepdims=True)
            return (x - mu) * jax.lax.rsqrt(var + EPS) * w + b

        def linear_attention(x, qkv_w, qkv_b, proj_w, proj_b):
            B, N, C = x.shape
            qkv = (x @ qkv_w + qkv_b).reshape(B, N, 3, NUM_HEADS, HEAD_DIM)
            qkv = qkv.transpose(2, 0, 3, 1, 4)
            q, k, v = (qkv[0], qkv[1], qkv[2])
            q = jax.nn.elu(q) + 1.0
            k = jax.nn.elu(k) + 1.0
            kv = jnp.einsum('bhsd,bhse->bhde', k, v)
            z = 1.0 / jnp.einsum('bhsd,bhd->bhs', q, k.sum(axis=-2))
            out = jnp.einsum('bhde,bhsd,bhs->bhse', kv, q, z)
            out = out.transpose(0, 2, 1, 3).reshape(B, N, C)
            return out @ proj_w + proj_b
        key = jax.random.key(seed)
        ks = jax.random.split(key, 10)
        s = 0.02
        return {'x': jax.random.normal(ks[0], (16, 512, DIM), dtype=jnp.float32), 'qkv_w': jax.random.normal(ks[1], (DIM, 3 * DIM), dtype=jnp.float32) * s, 'qkv_b': jnp.zeros((3 * DIM,), dtype=jnp.float32), 'proj_w': jax.random.normal(ks[2], (DIM, DIM), dtype=jnp.float32) * s, 'proj_b': jnp.zeros((DIM,), dtype=jnp.float32), 'fc1_w': jax.random.normal(ks[3], (DIM, HIDDEN), dtype=jnp.float32) * s, 'fc1_b': jnp.zeros((HIDDEN,), dtype=jnp.float32), 'fc2_w': jax.random.normal(ks[4], (HIDDEN, DIM), dtype=jnp.float32) * s, 'fc2_b': jnp.zeros((DIM,), dtype=jnp.float32), 'ln1_w': jnp.ones((DIM,), dtype=jnp.float32), 'ln1_b': jnp.zeros((DIM,), dtype=jnp.float32), 'ln2_w': jnp.ones((DIM,), dtype=jnp.float32), 'ln2_b': jnp.zeros((DIM,), dtype=jnp.float32)}
    _L0_mix_all = _L0_mix_setup()
    _L0_mix_in = {k: v for k, v in _L0_mix_all.items() if k in ('qkv_w', 'qkv_b', 'proj_w', 'proj_b', 'fc1_w', 'fc1_b', 'fc2_w', 'fc2_b', 'ln1_w', 'ln1_b', 'ln2_w', 'ln2_b')}
    del _L0_mix_all

    def _L0_ffn_setup():
        import jax, jax.numpy as jnp
        import numpy as np
        B, L, D, E, TOP_K = (8, 1024, 768, 4, 2)
        H = 2 * D
        LN_EPS = 1e-05

        def _gelu(v):
            return jax.nn.gelu(v, approximate=False)

        def _mish(v):
            return v * jnp.tanh(jax.nn.softplus(v))
        _ACTS = [_gelu, jax.nn.silu, _mish, _gelu]
        key = jax.random.key(seed)
        ks = jax.random.split(key, 8)
        x = jax.random.normal(ks[0], (B, L, D), dtype=jnp.float32)
        router_w = jax.random.normal(ks[1], (E, D), dtype=jnp.float32) * 0.02
        router_b = jnp.zeros((E,), dtype=jnp.float32)
        w1 = jax.random.normal(ks[2], (E, D, H), dtype=jnp.float32) * (1.0 / np.sqrt(D))
        b1 = jax.random.normal(ks[3], (E, H), dtype=jnp.float32) * 0.01
        w2 = jax.random.normal(ks[4], (E, H, D), dtype=jnp.float32) * (1.0 / np.sqrt(H))
        b2 = jax.random.normal(ks[5], (E, D), dtype=jnp.float32) * 0.01
        ln_g = jnp.ones((D,), dtype=jnp.float32)
        ln_b = jnp.zeros((D,), dtype=jnp.float32)
        return {'x': x, 'router_w': router_w, 'router_b': router_b, 'w1': w1, 'b1': b1, 'w2': w2, 'b2': b2, 'ln_g': ln_g, 'ln_b': ln_b}
    _L0_ffn_all = _L0_ffn_setup()
    _L0_ffn_in = {k: v for k, v in _L0_ffn_all.items() if k in ('router_w', 'router_b', 'w1', 'b1', 'w2', 'b2', 'ln_g', 'ln_b')}
    del _L0_ffn_all
    return {'x': x, 'src': src, 'dst': dst, 'L0_gnn_norm_g': _L0_gnn_in['norm_g'], 'L0_gnn_norm_b': _L0_gnn_in['norm_b'], 'L0_gnn_W1': _L0_gnn_in['W1'], 'L0_gnn_a_src1': _L0_gnn_in['a_src1'], 'L0_gnn_a_dst1': _L0_gnn_in['a_dst1'], 'L0_gnn_b1': _L0_gnn_in['b1'], 'L0_gnn_W2': _L0_gnn_in['W2'], 'L0_gnn_a_src2': _L0_gnn_in['a_src2'], 'L0_gnn_a_dst2': _L0_gnn_in['a_dst2'], 'L0_gnn_b2': _L0_gnn_in['b2'], 'L0_gnn_Wu': _L0_gnn_in['Wu'], 'L0_gnn_bu': _L0_gnn_in['bu'], 'L0_mix_qkv_w': _L0_mix_in['qkv_w'], 'L0_mix_qkv_b': _L0_mix_in['qkv_b'], 'L0_mix_proj_w': _L0_mix_in['proj_w'], 'L0_mix_proj_b': _L0_mix_in['proj_b'], 'L0_mix_fc1_w': _L0_mix_in['fc1_w'], 'L0_mix_fc1_b': _L0_mix_in['fc1_b'], 'L0_mix_fc2_w': _L0_mix_in['fc2_w'], 'L0_mix_fc2_b': _L0_mix_in['fc2_b'], 'L0_mix_ln1_w': _L0_mix_in['ln1_w'], 'L0_mix_ln1_b': _L0_mix_in['ln1_b'], 'L0_mix_ln2_w': _L0_mix_in['ln2_w'], 'L0_mix_ln2_b': _L0_mix_in['ln2_b'], 'L0_ffn_router_w': _L0_ffn_in['router_w'], 'L0_ffn_router_b': _L0_ffn_in['router_b'], 'L0_ffn_w1': _L0_ffn_in['w1'], 'L0_ffn_b1': _L0_ffn_in['b1'], 'L0_ffn_w2': _L0_ffn_in['w2'], 'L0_ffn_b2': _L0_ffn_in['b2'], 'L0_ffn_ln_g': _L0_ffn_in['ln_g'], 'L0_ffn_ln_b': _L0_ffn_in['ln_b']}

def reference(x, src, dst, L0_gnn_norm_g, L0_gnn_norm_b, L0_gnn_W1, L0_gnn_a_src1, L0_gnn_a_dst1, L0_gnn_b1, L0_gnn_W2, L0_gnn_a_src2, L0_gnn_a_dst2, L0_gnn_b2, L0_gnn_Wu, L0_gnn_bu, L0_mix_qkv_w, L0_mix_qkv_b, L0_mix_proj_w, L0_mix_proj_b, L0_mix_fc1_w, L0_mix_fc1_b, L0_mix_fc2_w, L0_mix_fc2_b, L0_mix_ln1_w, L0_mix_ln1_b, L0_mix_ln2_w, L0_mix_ln2_b, L0_ffn_router_w, L0_ffn_router_b, L0_ffn_w1, L0_ffn_b1, L0_ffn_w2, L0_ffn_b2, L0_ffn_ln_g, L0_ffn_ln_b):
    import jax
    import jax.numpy as jnp

    def _L0_gnn_ref(x, edge_index, norm_g, norm_b, W1, a_src1, a_dst1, b1, W2, a_src2, a_dst2, b2, Wu, bu):
        import jax, jax.numpy as jnp
        import numpy as np
        N = 1250
        E = 20000
        D = 768
        H1, C1 = (4, 192)
        H2, C2 = (2, 96)
        EPS = 1e-05
        NEG_SLOPE = 0.2

        def layer_norm(x, g, b):
            mu = x.mean(-1, keepdims=True)
            var = ((x - mu) ** 2).mean(-1, keepdims=True)
            return (x - mu) * jax.lax.rsqrt(var + EPS) * g + b

        def gat_conv(x, src, dst, W, a_src, a_dst, bias, H, C, n):
            h = (x @ W).reshape(n, H, C)
            s_src = (h * a_src).sum(-1)
            s_dst = (h * a_dst).sum(-1)
            e = jax.nn.leaky_relu(s_src[src] + s_dst[dst], NEG_SLOPE)
            emax = jax.ops.segment_max(e, dst, num_segments=n)
            ee = jnp.exp(e - emax[dst])
            denom = jax.ops.segment_sum(ee, dst, num_segments=n)
            alpha = ee / denom[dst]
            out = jax.ops.segment_sum(alpha[:, :, None] * h[src], dst, num_segments=n)
            return out.reshape(n, H * C) + bias
        loops = jnp.arange(N, dtype=edge_index.dtype)
        src = jnp.concatenate([edge_index[0], loops])
        dst = jnp.concatenate([edge_index[1], loops])
        x_norm = layer_norm(x, norm_g, norm_b)
        out1 = gat_conv(x_norm, src, dst, W1, a_src1, a_dst1, b1, H1, C1, N)
        out2 = gat_conv(out1, src, dst, W2, a_src2, a_dst2, b2, H2, C2, N)
        combined = jnp.concatenate([x, out2], axis=-1)
        return combined @ Wu + bu

    def _L0_mix_ref(x, qkv_w, qkv_b, proj_w, proj_b, fc1_w, fc1_b, fc2_w, fc2_b, ln1_w, ln1_b, ln2_w, ln2_b):
        import jax, jax.numpy as jnp
        import numpy as np
        DIM = 768
        NUM_HEADS = 12
        HEAD_DIM = DIM // NUM_HEADS
        HIDDEN = int(DIM * 4.0)
        EPS = 1e-08

        def layer_norm(x, w, b):
            mu = jnp.mean(x, axis=-1, keepdims=True)
            var = jnp.mean(jnp.square(x - mu), axis=-1, keepdims=True)
            return (x - mu) * jax.lax.rsqrt(var + EPS) * w + b

        def linear_attention(x, qkv_w, qkv_b, proj_w, proj_b):
            B, N, C = x.shape
            qkv = (x @ qkv_w + qkv_b).reshape(B, N, 3, NUM_HEADS, HEAD_DIM)
            qkv = qkv.transpose(2, 0, 3, 1, 4)
            q, k, v = (qkv[0], qkv[1], qkv[2])
            q = jax.nn.elu(q) + 1.0
            k = jax.nn.elu(k) + 1.0
            kv = jnp.einsum('bhsd,bhse->bhde', k, v)
            z = 1.0 / jnp.einsum('bhsd,bhd->bhs', q, k.sum(axis=-2))
            out = jnp.einsum('bhde,bhsd,bhs->bhse', kv, q, z)
            out = out.transpose(0, 2, 1, 3).reshape(B, N, C)
            return out @ proj_w + proj_b
        y = linear_attention(layer_norm(x, ln1_w, ln1_b), qkv_w, qkv_b, proj_w, proj_b)
        x = x + y
        h = layer_norm(x, ln2_w, ln2_b)
        h = jax.nn.gelu(h @ fc1_w + fc1_b, approximate=False) @ fc2_w + fc2_b
        return x + h

    def _L0_ffn_ref(x, router_w, router_b, w1, b1, w2, b2, ln_g, ln_b):
        import jax, jax.numpy as jnp
        import numpy as np
        B, L, D, E, TOP_K = (8, 1024, 768, 4, 2)
        H = 2 * D
        LN_EPS = 1e-05

        def _gelu(v):
            return jax.nn.gelu(v, approximate=False)

        def _mish(v):
            return v * jnp.tanh(jax.nn.softplus(v))
        _ACTS = [_gelu, jax.nn.silu, _mish, _gelu]
        b, l, d = x.shape
        e = router_w.shape[0]
        pooled = x.mean(axis=1)
        logits = pooled @ router_w.T + router_b
        top_v, top_i = jax.lax.top_k(logits, TOP_K)
        gates_k = jax.nn.softmax(top_v, axis=-1)
        gate = jnp.zeros((b, e), x.dtype).at[jnp.arange(b)[:, None], top_i].add(gates_k)
        h = jnp.einsum('bld,edh->belh', x, w1) + b1[None, :, None, :]
        h = jnp.stack([_ACTS[i](h[:, i]) for i in range(e)], axis=1)
        out = jnp.einsum('belh,ehd->beld', h, w2) + b2[None, :, None, :]
        y = jnp.einsum('be,beld->bld', gate, out) + x
        mu = y.mean(axis=-1, keepdims=True)
        var = ((y - mu) ** 2).mean(axis=-1, keepdims=True)
        return (y - mu) * jax.lax.rsqrt(var + LN_EPS) * ln_g + ln_b
    edge_index = jnp.stack([src, dst])
    xn = _layernorm(x, axis=-1)
    x = x + _L0_gnn_ref(xn, edge_index, L0_gnn_norm_g, L0_gnn_norm_b, L0_gnn_W1, L0_gnn_a_src1, L0_gnn_a_dst1, L0_gnn_b1, L0_gnn_W2, L0_gnn_a_src2, L0_gnn_a_dst2, L0_gnn_b2, L0_gnn_Wu, L0_gnn_bu) + _L0_mix_ref(xn[None], L0_mix_qkv_w, L0_mix_qkv_b, L0_mix_proj_w, L0_mix_proj_b, L0_mix_fc1_w, L0_mix_fc1_b, L0_mix_fc2_w, L0_mix_fc2_b, L0_mix_ln1_w, L0_mix_ln1_b, L0_mix_ln2_w, L0_mix_ln2_b)[0]
    x = x + _L0_ffn_ref(_layernorm(x, axis=-1)[None], L0_ffn_router_w, L0_ffn_router_b, L0_ffn_w1, L0_ffn_b1, L0_ffn_w2, L0_ffn_b2, L0_ffn_ln_g, L0_ffn_ln_b)[0]
    return x

_drawn_inputs = setup_inputs


def setup_inputs(seed=0):
    import zlib

    import numpy as np

    out = dict(_drawn_inputs(seed))
    spreads = {'L0_gnn_norm_g': (1.0, 0.6),
     'L0_gnn_norm_b': (0.0, 0.438),
     'L0_gnn_b1': (0.0, 0.378),
     'L0_gnn_b2': (0.0, 0.415),
     'L0_gnn_bu': (0.0, 0.1),
     'L0_mix_qkv_b': (0.0, 0.288),
     'L0_mix_proj_b': (0.0, 0.1),
     'L0_mix_fc1_b': (0.0, 0.275),
     'L0_mix_fc2_b': (0.0, 0.1),
     'L0_mix_ln1_w': (1.0, 0.6),
     'L0_mix_ln1_b': (0.0, 0.549),
     'L0_mix_ln2_w': (1.0, 0.2),
     'L0_mix_ln2_b': (0.0, 0.491),
     'L0_ffn_router_b': (0.0, 0.8),
     'L0_ffn_ln_g': (1.0, 0.2),
     'L0_ffn_ln_b': (0.0, 0.27)}
    factors = {'L0_gnn_a_src1': 6.361,
     'L0_gnn_a_dst1': 8.0,
     'L0_gnn_a_src2': 8.0,
     'L0_gnn_a_dst2': 21.693,
     'L0_mix_qkv_w': 3.798,
     'L0_ffn_b1': 44.741,
     'L0_ffn_b2': 28.212}
    for name, (base, spread) in spreads.items():
        noise = np.random.default_rng([zlib.crc32(name.encode()), seed]).standard_normal(out[name].shape)
        drawn = base * np.exp(spread * noise) if base else spread * noise
        out[name] = jnp.asarray(drawn.astype(out[name].dtype))
    for name, factor in factors.items():
        out[name] = (out[name] * factor).astype(out[name].dtype)
    return out
```

```python
from contextlib import ExitStack

import concourse.bass as bass
from concourse import mybir

N = 1250
D = 768
TP = 125
NT = N // TP
NP = NT // 2
CH = 418
NCH = 3
NF = CH * NCH
P = 128
KT = D // P
E = 21250
EPAIR = 2 * TP
NEP = E // EPAIR
H1, C1 = 4, 192
H2, C2 = 2, 96
NEG = 0.2
NHEAD, HD = 12, 64
MLP_GROUPS = 4
EXP, TOPK, EXP_GROUPS = 4, 2, 2
EH = 2 * D
BIG = 1e30

fp32 = mybir.dt.float32
f32r = mybir.dt.float32r
bf16 = mybir.dt.bfloat16
fp16 = mybir.dt.float16
i32 = mybir.dt.int32
u32 = mybir.dt.uint32
u16 = mybir.dt.uint16
ALU = mybir.AluOpType
ACT = mybir.ActivationFunctionType
AX = mybir.AxisListType
ds = bass.ds


class Chain:

    def __init__(self, eng, sem):
        self.eng, self.sem, self.n, self.links = eng, sem, 0, 0

    def link(self, ins):
        ins.then_inc(self.sem, 1)
        self.n = self.n + 1
        self.links += 1
        self.eng.wait_ge(self.sem, self.n)


VROWS = [("gnn_norm_g", KT), ("gnn_norm_b", KT), ("gnn_b1", KT), ("gnn_bu", KT), ("mix_ln1_w", KT),
         ("mix_ln1_b", KT), ("mix_proj_b", KT), ("mix_fc2_b", KT), ("mix_ln2_w", KT), ("mix_ln2_b", KT),
         ("mix_qkv_b", 3 * KT), ("mix_fc1_b", 4 * KT)]
VROWS2 = [("ffn_b1", EXP * 2 * KT), ("ffn_b2", EXP * KT), ("ffn_router_w", EXP * KT)]
VC = {}
_c = 0
for _name, _k in VROWS + VROWS2 + [("gnn_b2", 2), ("one", KT), ("zero", KT)]:
    VC[_name] = _c
    _c += _k
NV = _c
NV1 = sum(k for _, k in VROWS)
NV2 = sum(k for _, k in VROWS2)

BY_SLOT = """act_tile block_out c_acc c_madd ct_out dve_half f_o gat_ct gat_e gat_lo gat_mad gat_mu gat_mx gat_p
gat_ph gat_pu mlp_dn mlp_lo mlp_up oh oh_used q_num t2_aa tf_ev tf_lo tf_tr tf_xh tile_out tt_ad tt_add
tt_ys tt_yt w_done w_hi w_in w_split x_y""".split()
SINGLE = """c_tc c_tr e0_mish e1_mish f_x2 gat_R gat_h gat_hs gat_o gat_s gat_tr gat_u kv_h kv_kT kv_ka kv_tr kv_vT
ln0_xn q_a q_ah q_att q_den q_hi q_lo q_mat q_mf q_mh q_mul q_rec q_s""".split()
LOOPED = SINGLE + [name + slot for name in BY_SLOT for slot in "01"]

WSTAGES = [("W1", KT), ("W2", 2), ("WuT", KT), ("WuB", KT), ("KV", 2 * KT), ("Q", KT), ("PROJ", KT),
           ("MLP", MLP_GROUPS * 2 * KT), ("EXP", TOPK * EXP_GROUPS * 2 * KT)]
WBASE = {}
_n = 0
for _name, _k in WSTAGES:
    WBASE[_name] = _n // 2
    _n += _k
WTOTAL = _n


def gps_layer(nc, A, out):
    ctx = ExitStack()
    with ctx:
        sems = {}

        shared = {}

        def share(kind, tags, counts):
            for name, per_tag in counts.items():
                before = 0
                for tag, k in zip(tags, per_tag):
                    shared[f"{tag}_{name}"] = (f"{kind}_{name}", before)
                    before += k

        share("tf", "gumlx", {f"{k}{s}": (NP,) * 5 for k in ("xh", "tr", "ev", "lo") for s in range(2)})
        share("tt", ("t1", "t2", "t3"), {f"{k}{s}": (NP,) * 3 for k in ("ys", "yt", "add") for s in range(2)}
              | {f"ad{s}": (16 * NP, 32 * NP, 0) for s in range(2)})
        share("mlp", ("ml", "e0", "e1"), {f"{k}{s}": (3 * MLP_GROUPS, 3 * EXP_GROUPS, 3 * EXP_GROUPS)
                                          for k in ("up", "dn", "lo") for s in range(2)})
        share("ln", ("lna", "lnb", "lnl", "lnx", "lnf"), {"st": (NT,) * 5, "ag": (NT,) * 5, "ve": (1, 2, 1, 1, 1),
                                                          "sd": (1,) * 5, "rs": (1, 2, 1, 1, 1)})
        share("gat", ("g1", "g2"), {"S": (2, 2), "S_tr": (2, 2), "srow": (2, 2), "r_out": (32, 32), "ssb": (16 * H1, 0),
                                    "h_out": (16, 16), "h": (3 * KT, 0), "tr": (3 * KT, 0), "ab": (32, 32), "s": (NT, NT),
                                    "R0": (1, 1), "ones": (1, 1), "hs": (H1, 1), "hh": (H1, 1), "u": (H1, H2), "o": (3 * H1, 0),
                                    "nb": (3 * H1, 0), "R": (H1, H2), "he0": (32, 0), "he1": (32, 0), "db0": (64, 0),
                                    "db1": (64, 0), "xh": (KT, H2), "x": (KT, H2)}
              | {f"{k}{s}": (NP, NP) for k in ("mx", "mu") for s in range(2)} | {f"mad{s}": (16 * NP, 0) for s in range(2)}
              | {f"ct{s}": (16 * NP * H1, 0) for s in range(2)}
              | {f"{k}{s}": (NP * H1, 0) for k in ("e", "p", "ph", "lo", "pu") for s in range(2)})

        def follow(kind, *parts):
            before = 0
            for name, k in parts:
                shared[name] = (kind, before)
                before += k

        follow("pe_once", ("v_tr", 1), ("e_tr", 1), ("e_bb", 1), ("e_row", 1), ("r_log", 1), ("r_gb", 1))
        follow("dve_once", ("e_f", 2), ("e_cmm", 2), ("e_ec", 1), ("e_bc", 1), ("bnd", 1), ("r_pool", 1), ("r_idx", 1),
               ("r_d", 1), ("r_gates", 1))
        follow("pool_once", ("g_pad", 1), ("u_pad", 1), ("kv_ones", 1))
        follow("load", ("x_in", 16 * NT), ("u_tok", 16 * NT), ("m_tok", 16 * NT), ("gnn_back", 16), ("gb_in", 48))
        follow("store", ("xn_out", 16), ("gnn_out", 16), ("t1_tok_out", 16), ("t2_tok_out", 16))
        for s in range(2):
            follow(f"block_out{s}", (f"w1_y{s}", 3), (f"w2_y{s}", 1), (f"wut_y{s}", 3), (f"wub_y{s}", 3), (f"pj_y{s}", 3))
            follow(f"act_tile{s}", (f"c_sb{s}", NP), (f"f_n{s}", NP))
            follow(f"tile_out{s}", (f"madd_out{s}", 16 * NP), (f"f_out{s}", 16 * NP))
            follow(f"dve_half{s}", (f"g_hi{s}", NP), (f"g1_a{s}", NP * H1), (f"g2_a{s}", NP * H2), (f"u_hi{s}", NP),
                   (f"m_hi{s}", NP), (f"l_hi{s}", NP), (f"ml_hi{s}", 3 * MLP_GROUPS), (f"x_hi{s}", NP),
                   (f"e0_hi{s}", 3 * EXP_GROUPS), (f"e1_hi{s}", 3 * EXP_GROUPS), (f"f_m{s}", NP))

        def sem(name):
            name = shared.get(name, (name, 0))[0]
            if name not in sems:
                sems[name] = ctx.enter_context(nc.semaphore(name))
            return sems[name]

        def at(name, value):
            name, before = shared.get(name, (name, 0))
            return sem(name), value + (before + 1 if name in LOOPED else before)

        def sb(name, shape, dt, stack=ctx):
            return stack.enter_context(nc.sbuf_tensor(name, shape, dt))

        def dram(name, shape, dt):
            return nc.dram_tensor(name, shape, dt, kind="Internal").ap()

        xn_d = dram("xn_d", (NT, TP, D), fp32)
        x1_d = dram("x1_d", (NT, TP, D), fp32)
        x2_d = dram("x2_d", (NT, TP, D), fp32)
        h1_d = dram("h1_d", (NT, TP, D), fp32)
        h2_d = dram("h2_d", (NT, TP, H2 * C2), fp32)
        gnn_d = dram("gnn_d", (P, KT, NF), fp32)
        ct_d = dram("ct_d", (NT, TP, N), u16)
        madd_d = dram("madd_d", (NT, TP, N), bf16)
        row_d = [dram(f"row_d{k}", (NT, 8, TP), fp32) for k in range(4)]

        x_t = A["x"].rearrange("(i t) d -> i t d", t=TP)
        out_t = out.rearrange("(i t) d -> i t d", t=TP)

        ident = sb("ident", [P, P], fp32)
        identb = sb("identb", [TP, TP], bf16)
        sel = sb("sel", [P, 3, P], fp32)
        ones_row = sb("ones_row", [1, P], fp32)
        tri = sb("tri", [NT, NT], fp32)
        V = sb("V", [P, NV], fp32)
        gb2 = sb("gb2", [P, KT], fp32)
        mv = sb("mv", [TP, NT, 2], fp32)
        st = sb("st", [TP, NT, 2, 6], fp32)
        ve = sb("ve", [TP, 4, NT], fp32)
        rs = sb("rs", [TP, 2, NT], fp32)
        nm = sb("nm", [TP, 2, NT], fp32)
        S = sb("S", [TP, NT, 8], fp32)
        S2 = sb("S2", [TP, NT, 8], fp32)
        Sd = sb("Sd", [TP, NT, 8], fp32)
        MU = sb("MU", [TP, NT, 4], fp32)
        Dc = sb("Dc", [TP, NT, 8], fp32)
        mus = sb("mus", [TP, 2, 4], fp32)
        rt = sb("rt", [1, 64], fp32)
        rti = sb("rti", [1, 16], u32)
        bnd = sb("bnd", [1, 3 * NT], i32)
        gate = sb("gate", [P, 4], fp32)
        KVf = sb("KVf", [P, KT, P + 1], fp32)
        bdiag = sb("bdiag", [P, P], fp32)
        pool_i = sb("pool_i", [P, NT, KT], fp32)
        pooled = sb("pooled", [P, KT], fp32)
        rb = sb("rb", [1, EXP], fp32)

        w_raw = [sb(f"w_raw{s}", [P, KT, P], fp32) for s in range(2)]
        w_hi = [sb(f"w_hi{s}", [P, KT, P], f32r) for s in range(2)]
        w_lo = [sb(f"w_lo{s}", [P, KT, P], f32r) for s in range(2)]
        t0 = [sb(f"t0_{s}", [P, NF], fp32) for s in range(2)]
        Y = sb("Y", [P, KT, NF], fp32)

        def area(*groups):
            made, size = {}, 0
            widest = []
            for g in groups:
                n = sum(_bytes(s, d) for _, s, d in g)
                if n > size:
                    size, widest = n, g
            order = [g for g in groups if g is not widest] + [widest]
            for g in order:
                tmp = ExitStack()
                for name, s, d in g:
                    made[name] = sb(name, s, d, ctx if g is widest else tmp)
                tmp.close()
            return made

        def _bytes(shape, dt):
            n = 1
            for x in shape[1:]:
                n *= x
            return -(-n * mybir.dt.size(dt) // 32) * 32

        XA = area([("X_hi", [P, KT, NF], f32r), ("X_lo", [P, KT, NF], f32r)],
                  [(f"he_{k}{s}", [TP, NT, 256], fp32 if k == "raw" else f32r)
                   for k in ("raw", "hi", "lo") for s in range(2)],
                  [("Z", [TP, 2 * NF], bf16), ("iota", [TP, NF], fp16)]
                  + [(f"S1h{s}", [TP, NF], bf16) for s in range(2)]
                  + [(f"D1h{s}", [TP, TP], bf16) for s in range(2)] + [("D1z", [TP, TP], bf16)]
                  + [("ei", [NEP, 2, EPAIR], i32), ("ef", [NEP, 2, EPAIR], fp32), ("ec", [TP, 5 * NEP], fp32),
                     ("cmm", [NEP, 2, NT], fp32), ("cm2", [NEP, 2], fp32), ("bb", [NT, 8, NEP], fp32),
                     ("bc", [NT, 8], fp32), ("ix", [NT, 2, NEP], fp32), ("madds0", [TP, NF], bf16), ("madds1", [TP, NF], bf16),
                     ("ctb0", [TP, NT, TP], u16), ("ctb1", [TP, NT, TP], u16)],
                  [("gb", [TP, 2, D], fp32), ("X2", [TP, NT, D], fp32)])
        XC = area([("H_hi", [P, KT, NF], f32r), ("H_lo", [P, KT, NF], f32r)],
                  [("TOK", [TP, NT, D], fp32)] + [(f"xh{s}", [TP, D], fp32) for s in range(2)]
                  + [(f"ft{s}", [P, KT, TP], fp32) for s in range(2)]
                  + [(f"ad{s}", [TP, 2, D], fp32) for s in range(2)],
                  [("Db0", [TP, 2, N], fp32), ("Db1", [TP, 2, N], fp32), ("U0", [P, NF], fp32),
                   ("U1", [P, NF], fp32), ("R", [P, NF], fp32), ("Ph0", [TP, NF], f32r), ("Ph1", [TP, NF], f32r),
                   ("Pl0", [TP, NF], f32r), ("Pl1", [TP, NF], f32r), ("CT0", [TP, N], u16), ("CT1", [TP, N], u16)],
                  [("HT", [TP, NT, D], fp32), ("ab", [TP, 2, D], fp32), 
                   ("pr", [TP, 8, C1], fp32), ("srow", [80, TP], fp32),
                   ("mad0", [TP, N], bf16), ("mad1", [TP, N], bf16), ("trash", [TP, 4, N], bf16)])
        XD = area([("q_hi", [P, NF], f32r), ("q_lo", [P, NF], f32r), ("rden", [P, NF], fp32)]
                  + [(f"m_{b}{s}", [P, 2, P], f32r) for b in ("h", "l") for s in range(2)]
                  + [("kvf", [P, 2, P], fp32)],
                  [("e2_0", [TP, N], fp32), ("e2_1", [TP, N], fp32), ("pp0", [TP, N], fp32), ("pp1", [TP, N], fp32)],
                  [("ssb", [TP, 4, N], fp32)],
                  [("O2h", [C2, H2, NF], f32r), ("O2l", [C2, H2, NF], f32r)],
                  [("k_tok", [TP, NT, P], fp32), ("v_tok", [TP, NT, P + 2], fp32), ("kT", [P, NF], fp32), ("vT", [P, NF], fp32)],
                  [("m1", [P, NF], fp32), ("m2", [P, NF], fp32), ("m3", [P, NF], fp32)])
        acc = [ctx.enter_context(nc.psum_tensor(f"acc{s}", [P, NCH, 512], fp32)) for s in range(2)]
        aux = ctx.enter_context(nc.psum_tensor("aux", [P, 2, 512], fp32))

        X_hi, X_lo, H_hi, H_lo = XA["X_hi"], XA["X_lo"], XC["H_hi"], XC["H_lo"]
        TOK = XC["TOK"]

        def accf(s, parts=P):
            return acc[s][0:parts, :, 0:CH]

        def f3(ap):
            return ap.rearrange("p (c n) -> p c n", c=NCH)

        def vcol(name, k, parts=P):
            if isinstance(k, int):
                return V[0:parts, VC[name] + k:VC[name] + k + 1]
            return V[0:parts, ds(k + VC[name], 1)]

        block = ctx.enter_context(nc.Block())

        @block.sync
        def _(sp):
            r = 0
            for name, k in VROWS:
                sp.dma_start(t0[0][r:r + k, 0:P], A[name].rearrange("(r p) -> r p", p=P)).then_inc(sem("v_in"), 16)
                r += k
            r = 0
            for name, k in VROWS2:
                sp.dma_start(t0[0][r:r + k, P:2 * P], A[name].rearrange("e (r p) -> (e r) p", p=P)).then_inc(sem("v_in"), 16)
                r += k
            sp.dma_start(t0[0][0:2, 2 * P:2 * P + C2], A["gnn_b2"].rearrange("(r p) -> r p", p=C2)).then_inc(sem("v_in"), 16)
            for v, name in enumerate(("src", "dst")):
                sp.dma_start(XA["ei"][:, v, :], A[name].rearrange("(r e) -> r e", e=EPAIR)).then_inc(sem("e_in"), 16)
            for i in range(NT):
                sp.dma_start(TOK[:, i, :], x_t[i]).then_inc(sem("x_in"), 16)
            sp.dma_start(rb[:], A["ffn_router_b"].rearrange("(a n) -> a n", a=1)).then_inc(sem("rb_in"), 16)
            sp.wait_ge(*at("ln0_xn", NT))
            sp.dma_start(xn_d.rearrange("i t d -> t i d"), TOK[:]).then_inc(sem("xn_out"), 16)

            with sp.Fori(0, NP) as i:
                for s in range(2):
                    sp.wait_ge(*at(f"c_madd{s}", i + 1))
                    sp.dma_start(madd_d[ds(2 * i + s, 1)].rearrange("a t n -> (a t) n"),
                                 XA[f"madds{s}"][:, 0:N]).then_inc(sem(f"madd_out{s}"), 16)
                for s in range(2):
                    sp.wait_ge(*at("c_tc", 6 * i + 3 * s + 3))
                    sp.dma_start(ct_d[:, :, ds((2 * i + s) * TP, TP)].rearrange("j t n -> t j n"),
                                 XA[f"ctb{s}"][:]).then_inc(sem(f"ct_out{s}"), 16)

            def wload(stage, k, s, src):
                if not (isinstance(k, int) and k == 0):
                    sp.wait_ge(*at(f"w_split{s}", k))
                kp, kt, n = src.shape
                sp.dma_start(w_raw[s][0:kp, 0:kt, 0:n], src).then_inc(sem(f"w_in{s}"), 16)

            def wcols(W, c, n=P, kp=P):
                return W.rearrange("(k p) n -> p k n", p=kp)[:, :, ds(c, n)]

            def gemm_weights(stage, W, n=P, kp=P, pairs=3):
                with sp.Fori(0, pairs) as i:
                    for s in range(2):
                        wload(stage, WBASE[stage] + i, s, wcols(W, (2 * i + s) * n, n, kp))

            gemm_weights("W1", A["gnn_W1"])

            def attention_loads(g, H, C, h_d, adst, asrc):
                W = H * C
                ab = XC["ab"]
                if g == 1:
                    for s in range(2):
                        sp.wait_ge(*at(f"g_lo{s}", NP))
                else:
                    sp.wait_ge(*at("g1_o", 3 * H1))
                for v, a in enumerate((asrc, adst)):
                    sp.dma_start(ab[:, v, 0:W], a.rearrange("h c -> (h c)").partition_broadcast(TP)).then_inc(sem(f"g{g}_ab"), 16)
                sp.wait_ge(*at(f"g{g}_h", (3 * KT if g == 1 else 3 * H2)))
                sp.dma_start(h_d.rearrange("i t d -> t i d"), XC["HT"][:, :, 0:W]).then_inc(sem(f"g{g}_h_out"), 16)
                rows = row_d[2 * (g - 1)]
                sp.wait_ge(*at(f"g{g}_srow", 1))
                sp.dma_start(rows.rearrange("i c t -> (i c) t"), XC["srow"][:]).then_inc(sem(f"g{g}_r_out"), 16)
                sp.wait_ge(*at(f"g{g}_r_out", 16))
                for h in range(H):
                    sp.dma_start(XD["ssb"][:, h, :].rearrange("t (i u) -> t i u", u=TP),
                                 rows[:, h, :].partition_broadcast(TP)).then_inc(sem(f"g{g}_ssb"), 16)
                if g == 1:
                    for s in range(2):
                        sp.wait_ge(*at(f"madd_out{s}", 16 * NP))
                with sp.Fori(0, NP) as i:
                    for s in range(2):
                        sp.wait_ge(*at(f"g{g}_mx{s}", i))
                        sp.dma_start(XC[f"mad{s}"][:], madd_d[ds(2 * i + s, 1)].rearrange("a t n -> (a t) n")).then_inc(sem(f"g{g}_mad{s}"), 16)
                rows = row_d[2 * (g - 1) + 1]
                sp.wait_ge(*at(f"g{g}_srow", 2))
                sp.dma_start(rows.rearrange("i c t -> (i c) t"), XC["srow"][:]).then_inc(sem(f"g{g}_r_out"), 16)
                sp.wait_ge(*at(f"g{g}_r_out", 32))
                sp.wait_ge(*at(f"g{g}_h_out", 16))
                if g == 1:
                    for s in range(2):
                        sp.wait_ge(*at(f"ct_out{s}", 16 * NP))

                def db_load(h, ps):
                    for v in range(2):
                        sp.dma_start(XC[f"Db{ps}"][:, v, :].rearrange("t (i u) -> t i u", u=TP),
                                     rows[:, 4 * v + h, :].partition_broadcast(TP)).then_inc(sem(f"g{g}_db{ps}"), 16)

                def ct_loads(units):
                    with sp.Fori(0, NP) as j:
                        for s in range(2):
                            sp.wait_ge(*at(f"g{g}_p{s}", j + units))
                            sp.dma_start(XC[f"CT{s}"][:], ct_d[ds(2 * j + s, 1)].rearrange("a t n -> (a t) n")).then_inc(sem(f"g{g}_ct{s}"), 16)

                hv = h_d.rearrange("i t d -> t i d")
                sp.wait_ge(*at(f"g{g}_ones", 1))

                def he_load(h):
                    if g == 1:
                        if h >= 2:
                            sp.wait_ge(*at("g1_hs", h - 1))
                        o = 64 * (h % 2)
                        sp.dma_start(XA[f"he_raw{h % 2}"][:, :, o:o + C], hv[:, :, h * C:(h + 1) * C]).then_inc(sem(f"g1_he{h % 2}"), 16)
                    else:
                        sp.dma_start(XA["he_raw0"][:, :, h * P:h * P + C], hv[:, :, h * C:(h + 1) * C]).then_inc(sem("g2_he0"), 16)

                for h in range(2):
                    he_load(h)
                    db_load(h, h)
                for h in range(H):
                    ct_loads(h * NP)
                    if h + 2 < H:
                        he_load(h + 2)
                        for s in range(2):
                            sp.wait_ge(*at(f"g{g}_a{s}", NP * (h + 1)))
                        db_load(h + 2, h % 2)

            attention_loads(1, H1, C1, h1_d, A["gnn_a_dst1"], A["gnn_a_src1"])
            for s in range(2):
                wload("W2", WBASE["W2"], s, wcols(A["gnn_W2"], s * C2, C2))
            attention_loads(2, H2, C2, h2_d, A["gnn_a_dst2"], A["gnn_a_src2"])

            def reload(tag, src, after):
                for s_, v_ in after:
                    sp.wait_ge(*at(s_, v_))
                for i in range(NT):
                    sp.dma_start(TOK[:, i, :], src[i]).then_inc(sem(f"{tag}_tok"), 16)

            reload("u", xn_d, [("g2_o", 3 * H2), ("xn_out", 16)])
            gemm_weights("WuT", A["gnn_Wu"][0:D, :])
            gemm_weights("WuB", A["gnn_Wu"][D:D + H2 * C2, :], kp=C2)
            reload("m", xn_d, [("u_lo0", NP), ("u_lo1", NP)])
            sp.wait_ge(*at("wub_y1", 3))
            sp.wait_ge(*at("wub_y0", 3))
            sp.dma_start(gnn_d, Y[:]).then_inc(sem("gnn_out"), 16)
            with sp.Fori(0, KT) as i:
                for s in range(2):
                    wload("KV", WBASE["KV"] + i, s, wcols(A["mix_qkv_w"], (i + (1 + s) * KT) * P))
            gemm_weights("Q", A["mix_qkv_w"][:, 0:D])
            gemm_weights("PROJ", A["mix_proj_w"])

            def addend_loads(tag, srcs, after):
                for s_, v_ in after:
                    sp.wait_ge(*at(s_, v_))
                with sp.Fori(0, NP) as i:
                    for s in range(2):
                        sp.wait_ge(*at(f"{tag}_add{s}", i))
                        for a, src in enumerate(srcs):
                            sp.dma_start(XC[f"ad{s}"][:, a, :], src[ds(2 * i + s, 1)].rearrange("a t d -> (a t) d")).then_inc(sem(f"{tag}_ad{s}"), 16)

            def xstore(tag, dst):
                for s in range(2):
                    sp.wait_ge(*at(f"{tag}_add{s}", NP))
                sp.dma_start(dst.rearrange("i t d -> t i d"), TOK[:]).then_inc(sem(f"{tag}_tok_out"), 16)

            addend_loads("t1", [xn_d], [("w_done0", WBASE["MLP"]), ("w_done1", WBASE["MLP"])])
            xstore("t1", x1_d)
            sp.wait_ge(*at("gnn_out", 16))
            sp.dma_start(Y[:], gnn_d).then_inc(sem("gnn_back"), 16)
            with sp.Fori(0, MLP_GROUPS) as g:
                with sp.Fori(0, 3) as i:
                    for s in range(2):
                        wload("MLP", WBASE["MLP"] + 6 * g + i, s, wcols(A["mix_fc1_w"], (6 * g + 2 * i + s) * P))
                with sp.Fori(0, 3) as i:
                    for s in range(2):
                        src = A["mix_fc2_w"].rearrange("(g k p) n -> p g k n", p=P, k=KT)[:, ds(g, 1), :, ds((2 * i + s) * P, P)]
                        wload("MLP", WBASE["MLP"] + 6 * g + 3 + i, s, src.rearrange("p g k n -> p (g k) n"))
            sp.wait_ge(*at("t1_tok_out", 16))
            addend_loads("t2", [x_t, x1_d], [("w_done0", WBASE["EXP"]), ("w_done1", WBASE["EXP"])])
            xstore("t2", x2_d)

            sp.wait_ge(*at("r_idx", 1))
            for e in range(TOPK):
                ei_ = sp.value_load(rti[0:1, e:e + 1], min_val=0, max_val=EXP - 1)
                WB = WBASE["EXP"] + 12 * e
                with sp.Fori(0, EXP_GROUPS) as g:
                    with sp.Fori(0, 3) as i:
                        for s in range(2):
                            src = A["ffn_w1"].rearrange("e (k p) n -> p e k n", p=P)[:, ds(ei_, 1), :, ds((6 * g + 2 * i + s) * P, P)]
                            wload("EXP", WB + 6 * g + i, s, src.rearrange("p e k n -> p (e k) n"))
                    with sp.Fori(0, 3) as i:
                        for s in range(2):
                            src = A["ffn_w2"].rearrange("e (g k p) n -> p (e g) k n", p=P, k=KT)[:, ds(ei_ * 2 + g, 1), :, ds((2 * i + s) * P, P)]
                            wload("EXP", WB + 6 * g + 3 + i, s, src.rearrange("p e k n -> p (e k) n"))
            sp.wait_ge(*at("w_done0", WBASE["EXP"] + 24))
            sp.wait_ge(*at("w_done1", WBASE["EXP"] + 24))
            sp.wait_ge(*at("t2_tok_out", 16))
            sp.dma_start(XA["gb"][:, 0, :], A["ffn_ln_g"].partition_broadcast(TP)).then_inc(sem("gb_in"), 16)
            sp.dma_start(XA["gb"][:, 1, :], A["ffn_ln_b"].partition_broadcast(TP)).then_inc(sem("gb_in"), 16)
            sp.dma_start(XA["X2"][:], x2_d.rearrange("i t d -> t i d")).then_inc(sem("gb_in"), 16)
            with sp.Fori(0, NP) as i:
                for s in range(2):
                    sp.wait_ge(*at(f"f_o{s}", i + 1))
                    sp.dma_start(out_t[ds(2 * i + s, 1)].rearrange("a t d -> (a t) d"), XC[f"xh{s}"][:]).then_inc(sem(f"f_out{s}"), 16)
            for s in range(2):
                sp.wait_ge(*at(f"f_out{s}", 16 * NP))
            sp.wait_ge(*at("gnn_out", 16))

        @block.tensor
        def _(pe):
            def transpose_tiles(src, parts, s, tag, first, bank0, w0, after_first=None):
                for q, (a, b) in enumerate(((0, 4), (4, 8), (8, 10))):
                    bank = (bank0 + q) % 2
                    pe.wait_ge(*at(f"{tag}_h", first + q - (1 if q + w0 else 0)))
                    for t in range(a, b):
                        last = nc.tensor.transpose(aux[0:TP, bank, (t - a) * P:(t - a) * P + parts],
                                                   src[0:parts, t * TP:(t + 1) * TP], ident[0:parts, 0:parts])
                    last.then_inc(sem(f"{tag}_tr"), 1)

            def gemm(s, k, rhs_hi, rhs_lo, a, kt=KT, kp=P, mp=P, ready=None):
                pe.wait_ge(*at(f"w_split{s}", k + 1))
                for kk in range(kt):
                    if ready is not None:
                        pe.wait_ge(*ready(kk))
                    for n, (w, r) in enumerate(((w_hi, rhs_hi), (w_hi, rhs_lo), (w_lo, rhs_hi))):
                        for c in range(NCH):
                            last = nc.tensor.matmul(acc[a][0:mp, c, 0:CH], w[s][0:kp, kk, 0:mp],
                                                    r[0:kp, kk, c * CH:(c + 1) * CH],
                                                    start=(kk == 0 and n == 0), stop=(kk == kt - 1 and n == 2))
                last.then_inc(sem(f"w_done{s}"), 1)

            for name in LOOPED[::2]:
                pe.sem_inc(sem(name), 1)
            pe.wait_ge(*at("cst", 3))
            pe.wait_ge(*at("v_in", 16 * (len(VROWS) + len(VROWS2) + 1)))
            nc.tensor.transpose(aux[:, 0, 0:NV1], t0[0][0:NV1, 0:P], ident[0:NV1, 0:NV1])
            nc.tensor.transpose(aux[:, 0, P:P + NV2], t0[0][0:NV2, P:2 * P], ident[0:NV2, 0:NV2])
            nc.tensor.transpose(aux[0:C2, 0, 2 * P:2 * P + 2], t0[0][0:2, 2 * P:2 * P + C2], ident[0:2, 0:2]).then_inc(sem("v_tr"), 1)
            pe.wait_ge(*at("e_f", 2))
            for v in range(2):
                for half in range(2):
                    o = (2 * v + half) * NEP
                    last = nc.tensor.transpose(aux[0:TP, 1, o:o + NEP], XA["ef"][:, v, half * TP:(half + 1) * TP],
                                               ident[0:NEP, 0:NEP])
            last.then_inc(sem("e_tr"), 1)
            pe.wait_ge(*at("e_cmm", 2))
            pe.wait_ge(*at("v_cp", 1))
            for k in range(2):
                last = nc.tensor.matmul(aux[0:NT, 0, k * P:k * P + NEP], XA["cmm"][:, k, :], ident[0:NEP, 0:NEP],
                                        start=True, stop=True)
            last.then_inc(sem("e_bb"), 1)
            pe.wait_ge(*at("e_bc", 1))
            pe.wait_ge(*at("e_ec", 1))
            nc.tensor.matmul(aux[0:1, 1, 0:NT], XA["bc"][:, 0:1], ident[0:NT, 0:NT], start=True, stop=True)
            nc.tensor.matmul(aux[0:1, 1, 16:16 + NT], XA["bc"][:, 2:3], ident[0:NT, 0:NT], start=True, stop=True)
            nc.tensor.matmul(aux[0:1, 1, 32:32 + NT], XA["bc"][:, 2:3], tri[:], start=True, stop=True).then_inc(sem("e_row"), 1)

            pe.wait_ge(*at("bnd", 1))
            pe.wait_ge(*at("c_const", 3))
            with pe.Fori(0, NP) as i:
                for s in range(2):
                    t = 2 * i + s
                    pairs = pe.value_load(bnd[0:1, ds(t + NT, 1)], min_val=1, max_val=NEP)
                    before = pe.value_load(bnd[0:1, ds(t + 2 * NT, 1)], min_val=0, max_val=NEP * NT)
                    pe.wait_ge(*at(f"c_sb{s}", i))
                    for c in range(NCH):
                        nc.tensor.matmul(acc[s][0:TP, c, 0:CH], identb[:], XA["Z"][:, ds(NF + c * CH - t * TP, CH)],
                                         start=True, stop=False)
                    with pe.Fori(0, pairs) as p:
                        for h in range(2):
                            pe.wait_ge(*at(f"oh{h}", p + before + 1))
                            for c in range(NCH):
                                last = nc.tensor.matmul(acc[s][0:TP, c, 0:CH], XA[f"D1h{h}"][:],
                                                        XA[f"S1h{h}"][:, c * CH:(c + 1) * CH], start=False, stop=False)
                            last.then_inc(sem(f"oh_used{h}"), 1)
                    for c in range(NCH):
                        last = nc.tensor.matmul(acc[s][0:TP, c, 0:CH], XA["D1z"][:], XA["Z"][:, 0:CH],
                                                start=False, stop=True)
                    last.then_inc(sem(f"c_acc{s}"), 1)
                for s in range(2):
                    pe.wait_ge(*at(f"c_sb{s}", i + 1))
                    for q, (a, b) in enumerate(((0, 4), (4, 8), (8, 10))):
                        bank = (3 * s + q) % 2
                        pe.wait_ge(*at("c_tc", 6 * i + 3 * s + q - (1 if 3 * s + q else 0)))
                        for j in range(a, b):
                            last = nc.tensor.transpose(aux[0:TP, bank, (j - a) * P:(j - a) * P + TP],
                                                       t0[s][0:TP, j * TP:(j + 1) * TP], ident[0:TP, 0:TP])
                        last.then_inc(sem("c_tr"), 1)

            def to_features(tag, frees):
                for f in frees:
                    pe.wait_ge(*f)
                with pe.Fori(0, NP) as i:
                    for s in range(2):
                        pe.wait_ge(*at(f"{tag}_xh{s}", i + 1))
                        pe.wait_ge(*at(f"{tag}_ev{s}", i))
                        for m in range(KT):
                            last = nc.tensor.transpose(acc[s][:, m // 4, (m % 4) * P:(m % 4) * P + TP],
                                                       XC[f"xh{s}"][:, m * P:(m + 1) * P], ident[0:TP, 0:TP])
                        last.then_inc(sem(f"{tag}_tr{s}"), 1)

            def to_tokens(tag, frees):
                for f in frees:
                    pe.wait_ge(*f)
                with pe.Fori(0, NP) as i:
                    for s in range(2):
                        pe.wait_ge(*at(f"{tag}_ys{s}", i + 1))
                        pe.wait_ge(*at(f"{tag}_add{s}", i))
                        for m in range(KT):
                            last = nc.tensor.transpose(acc[s][0:TP, m // 4, (m % 4) * P:(m % 4 + 1) * P],
                                                       XC[f"ft{s}"][:, m, :], ident[:])
                        last.then_inc(sem(f"{tag}_yt{s}"), 1)

            to_features("g", [at("c_sb0", NP), at("c_sb1", NP)])

            for s in range(2):
                pe.wait_ge(*at(f"g_ev{s}", NP))
                pe.wait_ge(*at(f"g_lo{s}", NP))
            pe.wait_ge(*at("c_tc", 3 * NT))
            with pe.Fori(0, 3) as i:
                for s in range(2):
                    pe.wait_ge(*at(f"w1_y{s}", i))
                    gemm(s, WBASE["W1"] + i, X_hi, X_lo, s)
                for s in range(2):
                    pe.wait_ge(*at(f"w1_y{s}", i + 1))
                    transpose_tiles(t0[s], P, s, "g1", 6 * i + 3 * s, s, s)

            def attention_rows(g, n):
                pe.wait_ge(*at(f"g{g}_S", n))
                nc.tensor.transpose(aux[0:80, 0, 0:TP], (S if n == 1 else Dc)[:].rearrange("t i c -> t (i c)"),
                                    ident[0:TP, 0:TP]).then_inc(sem(f"g{g}_S_tr"), 1)

            def attention_head(g, h, blocks, between=None):
                pe.wait_ge(*at(f"g{g}_hs", (h + 1) if g == 1 else 1))
                if h:
                    pe.wait_ge(*at(f"g{g}_u", h))
                for j in range(NT):
                    s = j % 2
                    pe.wait_ge(*at(f"g{g}_ph{s}", NP * h + j // 2 + 1))
                    for n, part in enumerate(("hi", "lo", "Pl")):
                        if part == "Pl":
                            pe.wait_ge(*at(f"g{g}_lo{s}", NP * h + j // 2 + 1))
                        for a, hi, lo in blocks:
                            w, r = (lo if part == "lo" else hi), XC[f"Pl{s}" if part == "Pl" else f"Ph{s}"]
                            for c in range(NCH):
                                last = nc.tensor.matmul(acc[a][:, c, 0:CH], w[:, j, :], r[:, c * CH:(c + 1) * CH],
                                                        start=(j == 0 and n == 0), stop=(j == NT - 1 and n == 2))
                    last.then_inc(sem(f"g{g}_pu{s}"), 1)
                    if j == 3 and between is not None:
                        between()

            def attention_norm(g, h, k):
                pe.wait_ge(*at(f"g{g}_R", h + 1))
                for c in range(NCH):
                    pe.wait_ge(*at(f"g{g}_o", 3 * h + c - (1 if c else 0)))
                    nc.tensor.matmul(aux[:, c % 2, 0:CH], sel[:, k, :], XC["R"][:, c * CH:(c + 1) * CH],
                                     start=True, stop=True).then_inc(sem(f"g{g}_nb"), 1)

            pe.wait_ge(*at("g1_h", 3 * KT))
            attention_rows(1, 1)
            attention_rows(1, 2)
            for h in range(H1):
                hi, lo = XA[f"he_hi{h % 2}"], XA[f"he_lo{h % 2}"]
                attention_head(1, h, [(a, hi[:, :, a * P:(a + 1) * P], lo[:, :, a * P:(a + 1) * P]) for a in range(2)],
                               (lambda: attention_norm(1, h - 1, (h - 1) % 2)) if h else None)
            attention_norm(1, H1 - 1, (H1 - 1) % 2)

            pe.wait_ge(*at("g1_x", KT))
            pe.wait_ge(*at("g1_u", H1))
            pe.wait_ge(*at("g1_o", 3 * H1))
            for s in range(2):
                gemm(s, WBASE["W2"], X_hi, X_lo, s, mp=C2)
            for s in range(2):
                pe.wait_ge(*at(f"w2_y{s}", 1))
                transpose_tiles(t0[s], C2, s, "g2", 3 * s, s, s)
            pe.wait_ge(*at("g2_h", 3 * H2))
            attention_rows(2, 1)
            attention_rows(2, 2)
            for h in range(H2):
                hi, lo = XA["he_hi0"], XA["he_lo0"]
                attention_head(2, h, [(h, hi[:, :, h * P:(h + 1) * P], lo[:, :, h * P:(h + 1) * P])],
                               (lambda: attention_norm(2, h - 1, 2)) if h else None)
            attention_norm(2, H2 - 1, 2)

            to_features("u", [at("g2_u", H2)])
            for s in range(2):
                pe.wait_ge(*at(f"u_ev{s}", NP))
                pe.wait_ge(*at(f"u_lo{s}", NP))
            with pe.Fori(0, 3) as i:
                for s in range(2):
                    pe.wait_ge(*at(f"wut_y{s}", i))
                    gemm(s, WBASE["WuT"] + i, X_hi, X_lo, s)
            pe.wait_ge(*at("g2_x", H2))
            with pe.Fori(0, 3) as i:
                for s in range(2):
                    pe.wait_ge(*at(f"wut_y{s}", 3))
                    pe.wait_ge(*at(f"wub_y{s}", i))
                    gemm(s, WBASE["WuB"] + i, XD["O2h"], XD["O2l"], s, kt=H2, kp=C2)

            to_features("m", [at("wub_y0", 3), at("wub_y1", 3)])
            for s in range(2):
                pe.wait_ge(*at(f"m_ev{s}", NP))
                pe.wait_ge(*at(f"m_lo{s}", NP))

            def tr_block(name, i, first, strict):
                pe.wait_ge(*at(f"kv_{name}", i + 1))
                for q, (a, b) in enumerate(((0, 4), (4, 8), (8, 10))):
                    pe.wait_ge(*at("kv_h", first + q - (0 if strict and q == 0 else 1)))
                    for t in range(a, b):
                        last = nc.tensor.transpose(aux[0:TP, q % 2, (t - a) * P:(t - a + 1) * P],
                                                   XD[name][:, t * TP:(t + 1) * TP], ident[:])
                    last.then_inc(sem("kv_tr"), 1)

            def kv_product(first):
                pe.wait_ge(*at("kv_h", first))
                for t in range(NT):
                    last = nc.tensor.matmul(aux[:, 1, 0:P + 2], XD["k_tok"][:, t, :], XD["v_tok"][:, t, :],
                                            start=(t == 0), stop=(t == NT - 1))
                last.then_inc(sem("kv_tr"), 1)

            gemm(0, WBASE["KV"], X_hi, X_lo, 0)
            gemm(1, WBASE["KV"], X_hi, X_lo, 1)
            tr_block("kT", 0, 0, True)
            with pe.Fori(1, KT) as i:
                g0 = 7 * i - 4
                pe.wait_ge(*at("kv_ka", i))
                gemm(0, WBASE["KV"] + i, X_hi, X_lo, 0)
                tr_block("vT", i - 1, g0, True)
                gemm(1, WBASE["KV"] + i, X_hi, X_lo, 1)
                kv_product(g0 + 3)
                tr_block("kT", i, g0 + 4, False)
            g0 = 7 * KT - 4
            tr_block("vT", KT - 1, g0, True)
            kv_product(g0 + 3)

            def q_gemm(m, s, k):
                pe.wait_ge(*at("q_a", m))
                gemm(s, k, X_hi, X_lo, 0)

            def blocks_product(mat, s):
                for n, (w, r) in enumerate(((f"m_h{s}", "q_hi"), (f"m_h{s}", "q_lo"), (f"m_l{s}", "q_hi"))):
                    for c in range(NCH):
                        last = nc.tensor.matmul(acc[1][:, c, 0:CH], XD[w][:, mat, :], XD[r][:, c * CH:(c + 1) * CH],
                                                start=(n == 0), stop=(n == 2))
                return last

            def q_apply(m, s):
                pe.wait_ge(*at("q_lo", m + 1))
                pe.wait_ge(*at("q_mat", m + 1))
                pe.wait_ge(*at("q_mul", m))
                blocks_product(1, s).then_inc(sem("q_den"), 1)
                pe.wait_ge(*at("q_rec", m + 1))
                blocks_product(0, s).then_inc(sem(f"q_num{s}"), 1)

            pe.wait_ge(*at("kv_ka", KT))
            pe.wait_ge(*at("kv_vT", KT))
            q_gemm(0, 0, WBASE["Q"])
            with pe.Fori(0, 2) as i:
                q_gemm(2 * i + 1, 1, WBASE["Q"] + i)
                q_apply(2 * i, 0)
                q_gemm(2 * i + 2, 0, WBASE["Q"] + i + 1)
                q_apply(2 * i + 1, 1)
            q_gemm(5, 1, WBASE["Q"] + 2)
            q_apply(4, 0)
            q_apply(5, 1)
            pe.wait_ge(*at("q_a", KT))
            with pe.Fori(0, 3) as i:
                for s in range(2):
                    if s:
                        pe.wait_ge(*at("q_mul", KT))
                    pe.wait_ge(*at(f"pj_y{s}", i))
                    gemm(s, WBASE["PROJ"] + i, H_hi, H_lo, s, ready=lambda kk: at("q_att", kk + 1))
            to_tokens("t1", [at("pj_y0", 3), at("pj_y1", 3)])
            to_features("l", [at("t1_add0", NP), at("t1_add1", NP)])

            def mlp(tag, wb, groups):
                with pe.Fori(0, groups) as g:
                    with pe.Fori(0, 3) as i:
                        for s in range(2):
                            pe.wait_ge(*at(f"{tag}_up{s}", 3 * g + i))
                            pe.wait_ge(*at(f"{tag}_dn{s}", 3 * g))
                            gemm(s, wb + 6 * g + i, X_hi, X_lo, s)
                    with pe.Fori(0, 3) as i:
                        for s in range(2):
                            pe.wait_ge(*at(f"{tag}_up{s}", 3 * g + 3))
                            pe.wait_ge(*at(f"{tag}_dn{s}", 3 * g + i))
                            gemm(s, wb + 6 * g + 3 + i, H_hi, H_lo, s,
                                 ready=lambda kk: at(f"{tag}_lo{kk % 2}", 3 * g + kk // 2 + 1))

            for s in range(2):
                pe.wait_ge(*at(f"l_ev{s}", NP))
                pe.wait_ge(*at(f"l_lo{s}", NP))
            mlp("ml", WBASE["MLP"], MLP_GROUPS)
            to_tokens("t2", [at(f"ml_dn{s}", 3 * MLP_GROUPS) for s in range(2)])
            to_features("x", [at("t2_add0", NP), at("t2_add1", NP)])
            pe.wait_ge(*at("r_pool", 1))
            for m in range(KT):
                o = VC["ffn_router_w"] + m
                last = nc.tensor.matmul(aux[0:1, 0, 0:EXP], pooled[:, m:m + 1], V[:, o:o + KT * (EXP - 1) + 1:KT],
                                        start=(m == 0), stop=(m == KT - 1))
            last.then_inc(sem("r_log"), 1)
            pe.wait_ge(*at("r_gates", 1))
            nc.tensor.matmul(aux[:, 0, 8:8 + TOPK], ones_row[:], rt[0:1, 20:20 + TOPK], start=True, stop=True).then_inc(sem("r_gb"), 1)
            for s in range(2):
                pe.wait_ge(*at(f"x_ev{s}", NP))
                pe.wait_ge(*at(f"x_lo{s}", NP))
            for e in range(TOPK):
                if e:
                    for s in range(2):
                        pe.wait_ge(*at(f"e{e - 1}_dn{s}", 3 * EXP_GROUPS))
                mlp(f"e{e}", WBASE["EXP"] + 6 * EXP_GROUPS * e, EXP_GROUPS)
            to_tokens("t3", [at(f"e{TOPK - 1}_dn{s}", 3 * EXP_GROUPS) for s in range(2)])

        @block.gpsimd
        def _(pool):
            ch = Chain(pool, sem("pool_chain"))
            for m in (ident, identb, tri, sel):
                nc.gpsimd.memset(m[:], 0.0).then_inc(sem("cz"), 1)
            nc.gpsimd.memset(bdiag[:], 1.0).then_inc(sem("cz"), 1)
            nc.gpsimd.memset(ones_row[:], 1.0)
            nc.gpsimd.memset(V[:, VC["one"]:VC["one"] + KT], 1.0)
            nc.gpsimd.memset(V[:, VC["zero"]:VC["zero"] + KT], 0.0)
            nc.gpsimd.memset(rt[:], -3e38)
            pool.wait_ge(*at("cz", 5))
            blocks = bdiag[:].rearrange("p (a n) -> p a n", n=HD)
            nc.gpsimd.affine_select(out=blocks, in_=blocks, compare_op=ALU.is_ge, fill=0.0, base=0,
                                    pattern=[[-HD, 2], [0, HD]], channel_multiplier=1).then_inc(sem("cz"), 1)
            pool.wait_ge(*at("cz", 6))
            nc.gpsimd.affine_select(out=blocks, in_=blocks, compare_op=ALU.is_ge, fill=0.0, base=HD - 1,
                                    pattern=[[HD, 2], [0, HD]], channel_multiplier=-1)
            for m, n in ((ident, P), (identb, TP)):
                nc.gpsimd.affine_select(out=m[:], in_=m[:], compare_op=ALU.not_equal, fill=1.0, base=0,
                                        pattern=[[-1, n]], channel_multiplier=1).then_inc(sem("cst"), 1)
            nc.gpsimd.affine_select(out=tri[:], in_=tri[:], compare_op=ALU.is_ge, fill=1.0, base=0,
                                    pattern=[[-1, NT]], channel_multiplier=1).then_inc(sem("cst"), 1)
            for k, row in enumerate((64, 0, 96)):
                nc.gpsimd.affine_select(out=sel[:, k, :], in_=sel[:, k, :], compare_op=ALU.not_equal, fill=1.0,
                                        base=-row, pattern=[[0, P]], channel_multiplier=1).then_inc(sem("sel"), 1)
            nc.gpsimd.iota(XA["iota"][:], pattern=[[1, NF]], base=0, channel_multiplier=0,
                           allow_small_or_imprecise_dtypes=True).then_inc(sem("c_const"), 1)
            nc.gpsimd.memset(XA["Z"][:], 0.0).then_inc(sem("cz"), 1)
            nc.gpsimd.memset(XA["D1z"][:], 0.0).then_inc(sem("c_const"), 1)
            pool.wait_ge(*at("cz", 7))
            nc.gpsimd.affine_select(out=XA["Z"][:, NF:NF + TP], in_=XA["Z"][:, NF:NF + TP], compare_op=ALU.not_equal,
                                    fill=1.0, base=0, pattern=[[-1, TP]], channel_multiplier=1).then_inc(sem("c_const"), 1)
            nc.gpsimd.iota(XA["ix"][:, 0, :], pattern=[[1, NEP]], base=1, channel_multiplier=0,
                           allow_small_or_imprecise_dtypes=True)
            nc.gpsimd.iota(XA["ix"][:, 1, :], pattern=[[-1, NEP]], base=NEP, channel_multiplier=0,
                           allow_small_or_imprecise_dtypes=True)
            nc.gpsimd.iota(XA["bc"][:, 6:7], pattern=[[0, 1]], base=0, channel_multiplier=TP,
                           allow_small_or_imprecise_dtypes=True)
            nc.gpsimd.iota(XA["bc"][:, 7:8], pattern=[[0, 1]], base=TP, channel_multiplier=TP,
                           allow_small_or_imprecise_dtypes=True).then_inc(sem("e_ix"), 1)

            with pool.Fori(0, NP) as i:
                for s in range(2):
                    pool.wait_ge(*at(f"c_sb{s}", i + 1))
                    pool.wait_ge(*at(f"madd_out{s}", 16 * i))
                    pool.sem_inc(sem("pool_go"), 1)
                    nc.gpsimd.tensor_scalar(XA[f"madds{s}"][:, 0:N], t0[s][0:TP, 0:N], 0.0, -BIG,
                                            ALU.is_equal, ALU.mult).then_inc(sem(f"c_madd{s}"), 1)

            def wsplit(s, k, kp=P, kt=KT, n=P):
                raw, hi, lo = (w[s][0:kp, 0:kt, 0:n] for w in (w_raw, w_hi, w_lo))
                pool.wait_ge(*at(f"w_in{s}", 16 * (k + 1)))
                pool.wait_ge(*at(f"w_done{s}", k))
                pool.sem_inc(sem("pool_go"), 1)
                nc.gpsimd.tensor_copy(hi, raw).then_inc(sem(f"w_hi{s}"), 1)
                pool.wait_ge(*at(f"w_hi{s}", k + 1))
                nc.gpsimd.tensor_tensor(lo, raw, hi.bitcast(fp32), ALU.subtract).then_inc(sem(f"w_split{s}"), 1)

            def wsplits(stage, pairs=3, extra=0, **kw):
                with pool.Fori(0, pairs) as i:
                    for s in range(2):
                        wsplit(s, WBASE[stage] + extra + i, **kw)

            def to_features(tag, k, frees, pads=False, keep=False):
                for s_, v_ in frees:
                    pool.wait_ge(*at(s_, v_))
                if pads:
                    nc.gpsimd.memset(X_hi[:, :, N:NF].bitcast(fp32), 0.0)
                    nc.gpsimd.memset(X_lo[:, :, N:NF].bitcast(fp32), 0.0).then_inc(sem(f"{tag}_pad"), 1)

                def xh(t):
                    s = t % 2
                    if t >= 2:
                        pool.wait_ge(*at(f"{tag}_tr{s}", t // 2))
                    if k is None:
                        nc.gpsimd.tensor_copy(XC[f"xh{s}"][:], TOK[:, t, :]).then_inc(sem(f"{tag}_xh{s}"), 1)
                    else:
                        nc.gpsimd.tensor_scalar(XC[f"xh{s}"][:], TOK[:, t, :], rs[:, k, t:t + 1], nm[:, k, t:t + 1],
                                                ALU.mult, ALU.add).then_inc(sem(f"{tag}_xh{s}"), 1)

                xh(0)
                xh(1)
                for t in range(NT):
                    s = t % 2
                    if keep:
                        pool.wait_ge(*at(f"{tag}_ev{s}", t // 2 + 1))
                        nc.gpsimd.tensor_copy(Y[:, :, t * TP:(t + 1) * TP], XC[f"ft{s}"][:]).then_inc(sem(f"{tag}_y{s}"), 1)
                    if t + 2 < NT:
                        xh(t + 2)

            to_features("g", 0, [("lnb_rs", 2), ("c_acc0", NP), ("c_acc1", NP), ("c_tc", 3 * NT), ("c_madd0", NP), ("c_madd1", NP),
                                 ("madd_out0", 16 * NP), ("madd_out1", 16 * NP), ("ct_out0", 16 * NP), ("ct_out1", 16 * NP)], pads=True)
            wsplits("W1")

            def attention(g, H, C):
                pool.wait_ge(*at(f"g{g}_r_out", 32))
                pool.wait_ge(*at(f"g{g}_h_out", 16))
                for s in range(2):
                    for k in ("Ph", "Pl"):
                        nc.gpsimd.memset(XC[f"{k}{s}"][:, N:NF].bitcast(fp32), 0.0)
                nc.gpsimd.memset(XC["R"][:], 0.0).then_inc(sem(f"g{g}_R0"), 1)
                if g == 1:
                    nc.gpsimd.memset(XA["he_raw0"][:, :, C:2 * P], 1.0)
                    last = nc.gpsimd.memset(XA["he_raw1"][:, :, 0:2 * P - C], 1.0)
                else:
                    nc.gpsimd.memset(XA["he_raw0"][:, :, C:P], 1.0)
                    last = nc.gpsimd.memset(XA["he_raw0"][:, :, P + C:2 * P], 1.0)
                last.then_inc(sem(f"g{g}_ones"), 1)

                def split(h):
                    ps = h % 2 if g == 1 else 0
                    pool.wait_ge(*at(f"g{g}_hh", h + 1))
                    nc.gpsimd.tensor_tensor(XA[f"he_lo{ps}"][:], XA[f"he_raw{ps}"][:], XA[f"he_hi{ps}"][:].bitcast(fp32),
                                            ALU.subtract).then_inc(sem(f"g{g}_hs"), 1)

                def lows(h, a, b):
                    with pool.Fori(a, b) as i:
                        for s in range(2):
                            pool.wait_ge(*at(f"g{g}_ph{s}", NP * h + i + 1))
                            nc.gpsimd.tensor_tensor(XC[f"Pl{s}"][:, 0:N], XD[f"pp{s}"][:], XC[f"Ph{s}"][:, 0:N].bitcast(fp32),
                                                    ALU.subtract).then_inc(sem(f"g{g}_lo{s}"), 1)

                split(0)
                for h in range(H):
                    lows(h, 0, 3)
                    if h + 1 < H and g == 1:
                        split(h + 1)
                    lows(h, 3, NP)

            def stage_y(tag, frees):
                for s_, v_ in frees:
                    pool.wait_ge(*at(s_, v_))
                with pool.Fori(0, NP) as i:
                    for s in range(2):
                        pool.wait_ge(*at(f"{tag}_yt{s}", i))
                        nc.gpsimd.tensor_copy(XC[f"ft{s}"][:], Y[:, :, ds((2 * i + s) * TP, TP)]).then_inc(sem(f"{tag}_ys{s}"), 1)

            attention(1, H1, C1)
            for s in range(2):
                wsplit(s, WBASE["W2"], n=C2)
            attention(2, H2, C2)
            to_features("u", None, [("u_tok", 16 * NT), ("g2_hs", 1)], pads=True)
            wsplits("WuT")
            wsplits("WuB", kp=C2, kt=H2)
            to_features("m", 1, [("m_tok", 16 * NT)])
            pool.wait_ge(*at("wub_y0", 3))
            pool.wait_ge(*at("wub_y1", 3))
            nc.gpsimd.memset(XD["v_tok"][:, :, P:P + 2], 1.0).then_inc(sem("kv_ones"), 1)
            wsplits("KV", KT)
            pool.wait_ge(*at("kv_h", 7 * KT))
            with pool.Fori(0, 3) as i:
                for s in range(2):
                    m = 2 * i + s
                    wsplit(s, WBASE["Q"] + i)
                    pool.wait_ge(*at(f"q_num{s}", i))
                    pool.wait_ge(*at("q_mat", m))
                    nc.gpsimd.tensor_tensor(XD["kvf"][:, 0, :], KVf[:, ds(m, 1), 0:P].rearrange("p a n -> p (a n)"), bdiag[:], ALU.mult)
                    nc.gpsimd.tensor_tensor(XD["kvf"][:, 1, :], KVf[:, ds(m, 1), P:P + 1].rearrange("p a n -> p (a n)").broadcast_to([P, P]),
                                            bdiag[:], ALU.mult).then_inc(sem("q_mf"), 1)
                    pool.wait_ge(*at("q_mf", m + 1))
                    pool.sem_inc(sem("pool_go"), 1)
                    nc.gpsimd.tensor_copy(XD[f"m_h{s}"][:], XD["kvf"][:]).then_inc(sem("q_mh"), 1)
                    pool.wait_ge(*at("q_mh", m + 1))
                    nc.gpsimd.tensor_tensor(XD[f"m_l{s}"][:], XD["kvf"][:], XD[f"m_h{s}"][:].bitcast(fp32), ALU.subtract).then_inc(sem("q_mat"), 1)
            wsplits("PROJ")
            stage_y("t1", [("pj_y0", 3), ("pj_y1", 3), ("w_done0", WBASE["MLP"]), ("w_done1", WBASE["MLP"])])
            to_features("l", 0, [("lnl_rs", 1)])
            wsplits("MLP", 6 * MLP_GROUPS)
            stage_y("t2", [("ml_dn0", 3 * MLP_GROUPS), ("ml_dn1", 3 * MLP_GROUPS)])
            to_features("x", 0, [("lnx_rs", 1)], keep=True)
            wsplits("EXP", 6 * EXP_GROUPS * TOPK)
            stage_y("t3", [(f"e{TOPK - 1}_dn{s}", 3 * EXP_GROUPS) for s in range(2)])
            pool.wait_ge(*at("gb_in", 48))
            with pool.Fori(0, NT) as i:
                nc.gpsimd.tensor_tensor(XA["X2"][:, ds(i, 1), :], XA["X2"][:, ds(i, 1), :], XA["gb"][:, 1:2, :], ALU.add).then_inc(sem("f_x2"), 1)

        @block.scalar
        def _(act):
            A_ = nc.scalar.activation

            def ln_root(tag, n):
                act.wait_ge(*at(f"{tag}_ve", n))
                A_(ve[:, 0:n, :], ve[:, 0:n, :], ACT.Sqrt).then_inc(sem(f"{tag}_sd"), 1)

            for name in LOOPED[1::2]:
                act.sem_inc(sem(name), 1)
            act.wait_ge(*at("v_tr", 1))
            A_(V[:, 0:NV1], aux[:, 0, 0:NV1], ACT.Copy)
            A_(V[:, NV1:NV1 + NV2], aux[:, 0, P:P + NV2], ACT.Copy)
            A_(V[0:C2, VC["gnn_b2"]:VC["gnn_b2"] + 2], aux[0:C2, 0, 2 * P:2 * P + 2], ACT.Copy).then_inc(sem("v_cp"), 1)
            ln_root("lna", 1)
            act.wait_ge(*at("lna_rs", 1))
            with act.Fori(0, NT) as i:
                A_(TOK[:, ds(i, 1), :], TOK[:, ds(i, 1), :], ACT.Identity, scale=rs[:, 0, ds(i, 1)],
                   bias=nm[:, 0, ds(i, 1)]).then_inc(sem("ln0_xn"), 1)
            ln_root("lnb", 2)

            with act.Fori(0, NP) as i:
                for s in range(2):
                    act.wait_ge(*at(f"c_acc{s}", i + 1))
                    act.wait_ge(*at(f"c_madd{s}", i))
                    A_(f3(t0[s][0:TP, :]), accf(s, TP), ACT.Copy).then_inc(sem(f"c_sb{s}"), 1)
                for s in range(2):
                    for q, (a, b) in enumerate(((0, 4), (4, 8), (8, 10))):
                        act.wait_ge(*at("c_tr", 6 * i + 3 * s + q + 1))
                        if q == 0:
                            act.wait_ge(*at(f"ct_out{s}", 16 * i))
                        A_(XA[f"ctb{s}"][:, a:b, :],
                           aux[0:TP, (3 * s + q) % 2, 0:(b - a) * P].rearrange("p (j n) -> p j n", n=P)[:, :, 0:TP],
                           ACT.Copy).then_inc(sem("c_tc"), 1)

            def to_features(tag, g, b, frees=(), keep=False):
                for s_, v_ in frees:
                    act.wait_ge(*at(s_, v_))
                with act.Fori(0, NP) as i:
                    for s in range(2):
                        act.wait_ge(*at(f"{tag}_tr{s}", i + 1))
                        act.wait_ge(*at(f"{tag}_lo{s}", i))
                        if keep:
                            act.wait_ge(*at(f"{tag}_y{s}", i))
                        for m in range(KT):
                            last = A_(XC[f"ft{s}"][:, m, :], acc[s][:, m // 4, (m % 4) * P:(m % 4) * P + TP],
                                      ACT.Identity, scale=vcol(g, m), bias=vcol(b, m))
                        last.then_inc(sem(f"{tag}_ev{s}"), 1)

            to_features("g", "gnn_norm_g", "gnn_norm_b")
            with act.Fori(0, 3) as i:
                for s in range(2):
                    act.wait_ge(*at(f"w_done{s}", WBASE["W1"] + i + 1))
                    act.wait_ge(*at("g1_h", 6 * i))
                    A_(f3(t0[s][:]), accf(s), ACT.Copy).then_inc(sem(f"w1_y{s}"), 1)

            def attention(g, H):
                for n in range(2):
                    act.wait_ge(*at(f"g{g}_S_tr", n + 1))
                    if n:
                        act.wait_ge(*at(f"g{g}_r_out", 16))
                    A_(XC["srow"][:], aux[0:80, 0, 0:TP], ACT.Copy).then_inc(sem(f"g{g}_srow"), 1)

                def high(h):
                    ps = h % 2 if g == 1 else 0
                    act.wait_ge(*at(f"g{g}_ones", 1))
                    act.wait_ge(*at(f"g{g}_he{ps}", 16 * (h // 2 + 1) if g == 1 else 32))
                    A_(XA[f"he_hi{ps}"][:], XA[f"he_raw{ps}"][:], ACT.Copy).then_inc(sem(f"g{g}_hh"), 1)

                def weights(h, i):
                    n = i + NP * h
                    for s in range(2):
                        act.wait_ge(*at(f"g{g}_a{s}", n + 1))
                        act.wait_ge(*at(f"g{g}_p{s}", n))
                        A_(t0[s][0:TP, 0:N], XD[f"e2_{s}"][:], ACT.Exp,
                           bias=S2[:, ds(2 * i + s, 1), h:h + 1].rearrange("p a b -> p (a b)")).then_inc(sem(f"g{g}_e{s}"), 1)
                    for s in range(2):
                        act.wait_ge(*at(f"g{g}_p{s}", n + 1))
                        act.wait_ge(*at(f"g{g}_pu{s}", n))
                        A_(XC[f"Ph{s}"][:, 0:N], XD[f"pp{s}"][:], ACT.Copy).then_inc(sem(f"g{g}_ph{s}"), 1)

                def sums(h):
                    for s in range(2):
                        act.wait_ge(*at(f"g{g}_pu{s}", NP * (h + 1)))
                    if h:
                        act.wait_ge(*at(f"g{g}_o", 3 * h))
                    if g == 1:
                        A_(f3(XC["U0"][:]), accf(0), ACT.Copy)
                        A_(f3(XC["U1"][:]), accf(1), ACT.Copy).then_inc(sem("g1_u"), 1)
                    else:
                        A_(f3(XC[f"U{h}"][:]), accf(h), ACT.Copy).then_inc(sem("g2_u"), 1)

                high(0)
                for h in range(H):
                    with act.Fori(0, 1) as i:
                        weights(h, i)
                    if h:
                        sums(h - 1)
                    if h + 1 < H and g == 1:
                        high(h + 1)
                    with act.Fori(1, NP) as i:
                        weights(h, i)
                sums(H - 1)

            attention(1, H1)
            act.wait_ge(*at("g1_o", 3 * H1))
            for m in range(KT):
                A_(X_hi[:, m, :], Y[:, m, :], ACT.Identity, bias=vcol("gnn_b1", m)).then_inc(sem("g1_xh"), 1)
            for s in range(2):
                act.wait_ge(*at(f"w_done{s}", WBASE["W2"] + 1))
                A_(f3(t0[s][0:C2, :]), accf(s, C2), ACT.Copy).then_inc(sem(f"w2_y{s}"), 1)
            attention(2, H2)
            act.wait_ge(*at("g2_o", 3 * H2))
            for h in range(H2):
                A_(XD["O2h"][:, h, :], Y[0:C2, h, :], ACT.Identity, bias=vcol("gnn_b2", h, C2)).then_inc(sem("g2_xh"), 1)

            def blocks_out(stage, ysem, bias, frees=()):
                for s_, v_ in frees:
                    act.wait_ge(*at(s_, v_))
                with act.Fori(0, 3) as i:
                    for s in range(2):
                        act.wait_ge(*at(f"w_done{s}", WBASE[stage] + i + 1))
                        A_(Y[:, ds(2 * i + s, 1), :].rearrange("p a (c n) -> p (a c) n", c=NCH), accf(s), ACT.Identity,
                           bias=vcol(bias, 2 * i + s)).then_inc(sem(f"{ysem}{s}"), 1)

            to_features("u", "one", "zero")
            blocks_out("WuT", "wut_y", "gnn_bu", [("g2_x", H2)])

            to_features("m", "mix_ln1_w", "mix_ln1_b")

            def elu_parts(m, s, done, k, ready, bias):
                act.wait_ge(*at(f"w_done{s}", k))
                act.wait_ge(*at(done, m))
                A_(f3(t0[0][:]), accf(0), ACT.Exp, bias=vcol("mix_qkv_b", bias))
                A_(f3(t0[1][:]), accf(0), ACT.Relu, bias=vcol("mix_qkv_b", bias)).then_inc(sem(ready), 1)

            with act.Fori(0, KT) as i:
                elu_parts(i, 0, "kv_kT", WBASE["KV"] + i + 1, "kv_ka", i + KT)
            with act.Fori(0, 3) as i:
                for s in range(2):
                    elu_parts(2 * i + s, s, "q_lo", WBASE["Q"] + i + 1, "q_a", 2 * i + s)
            blocks_out("PROJ", "pj_y", "mix_proj_b", [("gnn_out", 16)])
            ln_root("lnl", 1)
            to_features("l", "mix_ln2_w", "mix_ln2_b")

            def up(tag, wb, groups, func, bias):
                with act.Fori(0, groups) as g:
                    with act.Fori(0, 3) as i:
                        for s in range(2):
                            act.wait_ge(*at(f"w_done{s}", wb + 6 * g + i + 1))
                            act.wait_ge(*at(f"{tag}_lo{s}", 3 * g + i))
                            last = A_(f3(t0[s][:]), accf(s), ACT.Identity if func == "mish" else func, bias=bias(6 * g + 2 * i + s))
                            if func == "mish":
                                last = A_(f3(XD[f"m{1 + s}"][:]), accf(s), ACT.Exp, bias=bias(6 * g + 2 * i + s))
                            last.then_inc(sem(f"{tag}_up{s}"), 1)

            up("ml", WBASE["MLP"], MLP_GROUPS, ACT.Gelu, lambda m: vcol("mix_fc1_b", m))
            ln_root("lnx", 1)
            to_features("x", "one", "zero", keep=True)
            act.wait_ge(*at("r_d", 1))
            A_(rt[0:1, 17:18], rt[0:1, 16:17], ACT.Exp).then_inc(sem("r_e"), 1)
            act.wait_ge(*at("r_idx", 1))
            for e in range(TOPK):
                er = act.value_load(rti[0:1, e:e + 1], min_val=0, max_val=EXP - 1)
                args = (f"e{e}", WBASE["EXP"] + 6 * EXP_GROUPS * e, EXP_GROUPS)
                bias = lambda m: vcol("ffn_b1", er * (2 * KT) + m)
                with act.If(er == 2):
                    up(*args, "mish", bias)
                with act.Else():
                    with act.If(er == 1):
                        up(*args, ACT.Silu, bias)
                    with act.Else():
                        up(*args, ACT.Gelu, bias)
            ln_root("lnf", 1)
            act.wait_ge(*at("lnf_rs", 1))
            with act.Fori(0, NP) as i:
                for s in range(2):
                    act.wait_ge(*at(f"f_out{s}", 16 * i))
                    A_(XC[f"xh{s}"][:], TOK[:, ds(2 * i + s, 1), :].rearrange("p a n -> p (a n)"), ACT.Identity,
                       scale=rs[:, 0, ds(2 * i + s, 1)], bias=nm[:, 0, ds(2 * i + s, 1)]).then_inc(sem(f"f_n{s}"), 1)

        @block.vector
        def _(dve):
            v = nc.vector
            ch = Chain(dve, sem("dve_chain"))
            GROUPS = ((0, 4), (4, 8), (8, 10))

            ef, bb, bc, ix = XA["ef"], XA["bb"], XA["bc"], XA["ix"]
            dve.wait_ge(*at("e_in", 32))
            for k in range(2):
                v.tensor_copy(ef[:, k, :], XA["ei"][:, k, :]).then_inc(sem("e_f"), 1)
            dve.wait_ge(*at("e_f", 2))
            v.tensor_reduce(XA["cm2"][:, 0:1], ef[:, 1, :], AX.X, ALU.min)
            ch.link(v.tensor_reduce(XA["cm2"][:, 1:2], ef[:, 1, :], AX.X, ALU.max))
            for k in range(2):
                v.tensor_copy(XA["cmm"][:, k, :], XA["cm2"][:, k:k + 1].broadcast_to([NEP, NT])).then_inc(sem("e_cmm"), 1)
            dve.wait_ge(*at("e_tr", 1))
            v.tensor_copy(XA["ec"][:, 0:4 * NEP], aux[0:TP, 1, 0:4 * NEP]).then_inc(sem("e_ec"), 1)
            dve.wait_ge(*at("e_bb", 1))
            dve.wait_ge(*at("e_ix", 1))
            ch.link(v.tensor_scalar(bb[:, 0, :], aux[0:NT, 0, 0:NEP], bc[:, 7:8], None, ALU.is_lt))
            ch.link(v.scalar_tensor_tensor(out=bb[:, 1, :], in0=aux[0:NT, 0, P:P + NEP], scalar=bc[:, 6:7],
                                           in1=bb[:, 0, :], op0=ALU.is_ge, op1=ALU.mult))
            v.tensor_tensor(bb[:, 2, :], bb[:, 1, :], ix[:, 0, :], ALU.mult)
            ch.link(v.tensor_tensor(bb[:, 3, :], bb[:, 1, :], ix[:, 1, :], ALU.mult))
            v.tensor_reduce(bc[:, 4:5], bb[:, 2, :], AX.X, ALU.max)
            ch.link(v.tensor_reduce(bc[:, 3:4], bb[:, 3, :], AX.X, ALU.max))
            ch.link(v.tensor_scalar(bc[:, 5:6], bc[:, 3:4], -1.0, float(NEP), ALU.mult, ALU.add))
            ch.link(v.tensor_scalar(bc[:, 0:1], bc[:, 5:6], float(NEP - 1), None, ALU.min))
            ch.link(v.scalar_tensor_tensor(out=bc[:, 1:2], in0=bc[:, 0:1], scalar=1.0, in1=bc[:, 4:5],
                                           op0=ALU.add, op1=ALU.max))
            v.tensor_tensor(bc[:, 2:3], bc[:, 1:2], bc[:, 0:1], ALU.subtract).then_inc(sem("e_bc"), 1)
            dve.wait_ge(*at("e_row", 1))
            v.tensor_copy(bnd[:].rearrange("p (a b) -> p a b", b=NT),
                          aux[0:1, 1, 0:48].rearrange("p (a b) -> p a b", b=16)[:, :, 0:NT]).then_inc(sem("bnd"), 1)

            def tile_stats(tag, t):
                for k in range(2):
                    last = v.bn_stats(st[:, ds(t, 1), k, :].rearrange("p a b -> p (a b)"),
                                      TOK[:, ds(t, 1), k * (D // 2):(k + 1) * (D // 2)].rearrange("p a b -> p (a b)"))
                last.then_inc(sem(f"{tag}_st"), 1)

            def ln_terms(tag, eps):
                dve.wait_ge(*at(f"{tag}_st", NT))
                for i in range(NT):
                    v.bn_aggr(mv[:, i, :], st[:, i, :, :].rearrange("p k b -> p (k b)")).then_inc(sem(f"{tag}_ag"), 1)
                dve.wait_ge(*at(f"{tag}_ag", NT))
                for k, e in enumerate(eps):
                    v.tensor_scalar(ve[:, k, :], mv[:, :, 1], e, None, ALU.add).then_inc(sem(f"{tag}_ve"), 1)
                dve.wait_ge(*at(f"{tag}_sd", 1))
                ch.link(v.reciprocal(rs[:, 0:len(eps), :], ve[:, 0:len(eps), :]))
                for k in range(len(eps)):
                    v.scalar_tensor_tensor(out=nm[:, k, :], in0=mv[:, :, 0], scalar=-1.0, in1=rs[:, k, :],
                                           op0=ALU.mult, op1=ALU.mult).then_inc(sem(f"{tag}_rs"), 1)

            dve.wait_ge(*at("x_in", 16 * NT))
            with dve.Fori(0, NT) as i:
                tile_stats("lna", i)
            ln_terms("lna", (1e-5,))
            with dve.Fori(0, NT) as i:
                dve.wait_ge(*at("ln0_xn", i + 1))
                tile_stats("lnb", i)
            ln_terms("lnb", (1e-5, 1e-8))

            dve.wait_ge(*at("bnd", 1))
            dve.wait_ge(*at("e_ec", 1))
            dve.wait_ge(*at("c_const", 3))
            with dve.Fori(0, NT) as t:
                p0 = dve.value_load(bnd[0:1, ds(t, 1)], min_val=0, max_val=NEP - 1)
                pairs = dve.value_load(bnd[0:1, ds(t + NT, 1)], min_val=1, max_val=NEP)
                before = dve.value_load(bnd[0:1, ds(t + 2 * NT, 1)], min_val=0, max_val=NEP * NT)
                with dve.Fori(0, pairs) as p:
                    for h in range(2):
                        dve.wait_ge(*at(f"oh_used{h}", p + before))
                        v.tensor_scalar(XA[f"D1h{h}"][:], XA["iota"][:, ds(t * TP, TP)], XA["ec"][:, ds(p + p0 + (2 + h) * NEP, 1)],
                                        None, ALU.is_equal)
                        v.tensor_scalar(XA[f"S1h{h}"][:], XA["iota"][:], XA["ec"][:, ds(p + p0 + h * NEP, 1)],
                                        None, ALU.is_equal).then_inc(sem(f"oh{h}"), 1)

            def split_tiles(tag, frees=(), pool_sum=False):
                for s_, v_ in frees:
                    dve.wait_ge(*at(s_, v_))
                with dve.Fori(0, NP) as i:
                    for s in range(2):
                        t = 2 * i + s
                        dve.wait_ge(*at(f"{tag}_ev{s}", i + 1))
                        ft = XC[f"ft{s}"]
                        v.tensor_copy(X_hi[:, :, ds(t * TP, TP)], ft[:]).then_inc(sem(f"{tag}_hi{s}"), 1)
                        if pool_sum:
                            v.tensor_reduce(pool_i[:, ds(t, 1), :].rearrange("p a k -> p (a k)"), ft[:], AX.X, ALU.add)
                        dve.wait_ge(*at(f"{tag}_hi{s}", i + 1))
                        v.tensor_tensor(X_lo[:, :, ds(t * TP, TP)], ft[:], X_hi[:, :, ds(t * TP, TP)].bitcast(fp32),
                                        ALU.subtract).then_inc(sem(f"{tag}_lo{s}"), 1)

            split_tiles("g", [("g_pad", 1)])

            def head_terms(g, H, C, width, blocks):
                HT, ab = XC["HT"], XC["ab"]

                def group(m, col, first, bank0):
                    for q, (a, b) in enumerate(GROUPS):
                        dve.wait_ge(*at(f"g{g}_tr", first + q + 1))
                        v.tensor_copy(HT[:, a:b, ds(col, width)],
                                      aux[0:TP, (bank0 + q) % 2, 0:(b - a) * P].rearrange("p (t n) -> p t n", n=P)[:, :, 0:width]
                                      ).then_inc(sem(f"g{g}_h"), 1)
                with dve.Fori(0, blocks // 2) as i:
                    for s in range(2):
                        group(2 * i + s, (2 * i + s) * width, 6 * i + 3 * s, s)
                dve.wait_ge(*at(f"g{g}_h", 3 * blocks))
                dve.wait_ge(*at(f"g{g}_ab", 32))
                with dve.Fori(0, NT) as i:
                    dve.wait_ge(*at(f"g{g}_s", i))
                    for k in range(2):
                        for h in range(H):
                            last = v.scalar_tensor_tensor(
                                out=XC["pr"][:, 4 * k + h, 0:C], in0=HT[:, ds(i, 1), h * C:(h + 1) * C].rearrange("p a n -> p (a n)"),
                                scalar=1.0, in1=ab[:, k, h * C:(h + 1) * C], op0=ALU.mult, op1=ALU.mult,
                                accum_out=S[:, ds(i, 1), 4 * k + h:4 * k + h + 1].rearrange("p a n -> p (a n)"))
                    last.then_inc(sem(f"g{g}_s"), 1)
                dve.wait_ge(*at(f"g{g}_s", NT))
                v.tensor_scalar(S2[:], S[:], NEG, None, ALU.mult).then_inc(sem(f"g{g}_S"), 1)
                dve.wait_ge(*at(f"g{g}_ssb", 16 * H))
                with dve.Fori(0, NP) as i:
                    for s in range(2):
                        dve.wait_ge(*at(f"g{g}_mad{s}", 16 * (i + 1)))
                        dve.wait_ge(*at(f"g{g}_mu{s}", i))
                        dve.sem_inc(sem("dve_go"), 1)
                        for h in range(H):
                            last = v.tensor_tensor_reduce(out=XC["trash"][:, h, :], in0=XD["ssb"][:, h, :], in1=XC[f"mad{s}"][:],
                                                          scale=1.0, scalar=-3e38, op0=ALU.add, op1=ALU.max,
                                                          accum_out=mus[:, s, h:h + 1])
                        last.then_inc(sem(f"g{g}_mx{s}"), 1)
                        dve.wait_ge(*at(f"g{g}_mx{s}", i + 1))
                        v.tensor_copy(MU[:, ds(2 * i + s, 1), 0:H].rearrange("p a h -> p (a h)"),
                                      mus[:, s, 0:H]).then_inc(sem(f"g{g}_mu{s}"), 1)
                for s in range(2):
                    dve.wait_ge(*at(f"g{g}_mu{s}", NP))
                dst, dst2 = S[:, :, 4:4 + H], S2[:, :, 4:4 + H]
                dve.wait_ge(*at(f"g{g}_S", 1))
                v.tensor_tensor(Sd[:], S[:], S2[:], ALU.subtract)
                ch.link(v.tensor_tensor(Dc[:, :, 0:H], MU[:, :, 0:H], dst, ALU.add))
                ch.link(v.scalar_tensor_tensor(out=MU[:, :, 0:H], in0=Dc[:, :, 0:H], scalar=NEG, in1=Dc[:, :, 0:H],
                                               op0=ALU.mult, op1=ALU.max))
                v.tensor_tensor(Dc[:, :, 0:H], dst, MU[:, :, 0:H], ALU.subtract)
                v.tensor_tensor(Dc[:, :, 4:4 + H], dst2, MU[:, :, 0:H], ALU.subtract).then_inc(sem(f"g{g}_S"), 1)

            def head_weights(g, H):
                dve.wait_ge(*at(f"g{g}_R0", 1))
                dve.wait_ge(*at(f"g{g}_S", 2))
                R = XC["R"]

                def weights(h, a, b):
                    with dve.Fori(a, b) as i:
                        n = i + NP * h
                        for s in range(2):
                            dve.wait_ge(*at(f"g{g}_e{s}", n))
                            v.scalar_tensor_tensor(out=XD[f"e2_{s}"][:], in0=XC[f"Db{h % 2}"][:, 0, :],
                                                   scalar=Sd[:, ds(2 * i + s, 1), h:h + 1].rearrange("p a b -> p (a b)"),
                                                   in1=XC[f"Db{h % 2}"][:, 1, :], op0=ALU.add, op1=ALU.max).then_inc(sem(f"g{g}_a{s}"), 1)
                        for s in range(2):
                            dve.wait_ge(*at(f"g{g}_e{s}", n + 1))
                            dve.wait_ge(*at(f"g{g}_ct{s}", 16 * n + 16))
                            dve.wait_ge(*at(f"g{g}_lo{s}", n))
                            v.scalar_tensor_tensor(out=XD[f"pp{s}"][:], in0=t0[s][0:TP, 0:N], scalar=1.0, in1=XC[f"CT{s}"][:],
                                                   op0=ALU.min, op1=ALU.mult).then_inc(sem(f"g{g}_p{s}"), 1)

                def norm(h):
                    dve.wait_ge(*at(f"g{g}_u", h + 1))
                    if g == 1:
                        rows, U = (slice(64, 128), "U1") if h % 2 == 0 else (slice(0, 64), "U0")
                        b = 3 * (h // 2)
                        parts = [(slice(0, 128), "U0", b), (slice(0, 64), "U1", b + 1)] if h % 2 == 0 else \
                                [(slice(64, 128), "U0", b + 1), (slice(0, 128), "U1", b + 2)]
                    else:
                        rows, U = slice(96, 128), f"U{h}"
                        parts = [(slice(0, 96), f"U{h}", h)]
                    if h:
                        dve.wait_ge(*at(f"g{g}_nb", 3 * h))
                    v.reciprocal(R[rows, 0:N], XC[U][rows, 0:N]).then_inc(sem(f"g{g}_R"), 1)
                    for c in range(NCH):
                        cs = slice(c * CH, (c + 1) * CH)
                        dve.wait_ge(*at(f"g{g}_nb", 3 * h + c + 1))
                        for r, u, blk in parts:
                            last = v.tensor_tensor(Y[r, blk, cs], XC[u][r, cs], aux[r, c % 2, 0:CH], ALU.mult)
                        last.then_inc(sem(f"g{g}_o"), 1)

                for h in range(H):
                    dve.wait_ge(*at(f"g{g}_db{h % 2}", 32 * (h // 2 + 1)))
                    weights(h, 0, 2)
                    if h:
                        norm(h - 1)
                    weights(h, 2, NP)
                norm(H - 1)

            head_terms(1, H1, C1, P, KT)
            head_weights(1, H1)
            for m in range(KT):
                dve.wait_ge(*at("g1_xh", m + 1))
                v.scalar_tensor_tensor(out=X_lo[:, m, :], in0=Y[:, m, :], scalar=vcol("gnn_b1", m), in1=X_hi[:, m, :].bitcast(fp32),
                                       op0=ALU.add, op1=ALU.subtract).then_inc(sem("g1_x"), 1)
            head_terms(2, H2, C2, C2, 2)
            head_weights(2, H2)
            for h in range(H2):
                dve.wait_ge(*at("g2_xh", h + 1))
                v.scalar_tensor_tensor(out=XD["O2l"][:, h, :], in0=Y[0:C2, h, :], scalar=vcol("gnn_b2", h, C2),
                                       in1=XD["O2h"][:, h, :].bitcast(fp32), op0=ALU.add, op1=ALU.subtract).then_inc(sem("g2_x"), 1)
            split_tiles("u", [("u_pad", 1)])

            def yblock(m):
                return Y[:, ds(m, 1), :].rearrange("p a (c n) -> p (a c) n", c=NCH)

            with dve.Fori(0, 3) as i:
                for s in range(2):
                    dve.wait_ge(*at(f"w_done{s}", WBASE["WuB"] + i + 1))
                    dve.wait_ge(*at(f"wut_y{s}", 3))
                    v.scalar_tensor_tensor(out=yblock(2 * i + s), in0=accf(s), scalar=vcol("mix_fc2_b", 2 * i + s), in1=yblock(2 * i + s),
                                           op0=ALU.add, op1=ALU.add).then_inc(sem(f"wub_y{s}"), 1)
            split_tiles("m")

            def kT_part(m, tr):
                dve.wait_ge(*at("kv_ka", m + 1))
                if tr is not None:
                    dve.wait_ge(*at("kv_tr", tr))
                v.scalar_tensor_tensor(out=XD["kT"][:], in0=t0[0][:], scalar=1.0, in1=t0[1][:],
                                       op0=ALU.min, op1=ALU.add).then_inc(sem("kv_kT"), 1)

            def vT_part(m, tr):
                dve.wait_ge(*at("w_done1", WBASE["KV"] + 1 + m))
                if tr is not None:
                    dve.wait_ge(*at("kv_tr", tr))
                v.tensor_scalar(f3(XD["vT"][:]), accf(1), vcol("mix_qkv_b", m + 2 * KT), None, ALU.add).then_inc(sem("kv_vT"), 1)

            def tok_part(name, first):
                for q, (a, b) in enumerate(GROUPS):
                    dve.wait_ge(*at("kv_tr", first + q + 1))
                    v.tensor_copy(XD[name][:, a:b, 0:P],
                                  aux[0:TP, q % 2, 0:(b - a) * P].rearrange("p (t n) -> p t n", n=P)).then_inc(sem("kv_h"), 1)

            def kv_part(m, first):
                dve.wait_ge(*at("kv_tr", first + 1))
                last = v.tensor_copy(KVf[:, ds(m, 1), :].rearrange("p a n -> p (a n)"), aux[:, 1, 0:P + 1])
                last.then_inc(sem("kv_h"), 1)

            dve.wait_ge(*at("kv_ones", 1))
            kT_part(0, None)
            tok_part("k_tok", 0)
            vT_part(0, None)
            with dve.Fori(1, KT) as i:
                g0 = 7 * i - 4
                kT_part(i, g0)
                tok_part("v_tok", g0)
                kv_part(i - 1, g0 + 3)
                tok_part("k_tok", g0 + 4)
                vT_part(i, g0 + 3)
            g0 = 7 * KT - 4
            tok_part("v_tok", g0)
            kv_part(KT - 1, g0 + 3)

            with dve.Fori(0, 3) as i:
                for s in range(2):
                    m = 2 * i + s
                    dve.wait_ge(*at("q_a", m + 1))
                    v.scalar_tensor_tensor(out=t0[0][:], in0=t0[0][:], scalar=1.0, in1=t0[1][:],
                                           op0=ALU.min, op1=ALU.add).then_inc(sem("q_s"), 1)
                    dve.wait_ge(*at("q_s", m + 1))
                    dve.wait_ge(*at(f"q_num{1 - s}", i + s))
                    v.tensor_copy(XD["q_hi"][:], t0[0][:]).then_inc(sem("q_hi"), 1)
                    dve.wait_ge(*at("q_hi", m + 1))
                    v.tensor_tensor(XD["q_lo"][:], t0[0][:], XD["q_hi"][:].bitcast(fp32), ALU.subtract).then_inc(sem("q_lo"), 1)
                    dve.wait_ge(*at("q_den", m + 1))
                    dve.wait_ge(*at("q_att", m))
                    v.reciprocal(f3(XD["rden"][:]), accf(1)).then_inc(sem("q_rec"), 1)
                    dve.wait_ge(*at("q_rec", m + 1))
                    dve.wait_ge(*at(f"q_num{s}", i + 1))
                    v.tensor_tensor(f3(XD["rden"][:]), accf(1), f3(XD["rden"][:]), ALU.mult).then_inc(sem("q_mul"), 1)
                    dve.wait_ge(*at("q_mul", m + 1))
                    Hh, Hl = (x[:, ds(m, 1), :].rearrange("p a n -> p (a n)") for x in (H_hi, H_lo))
                    v.tensor_copy(Hh, XD["rden"][:]).then_inc(sem("q_ah"), 1)
                    dve.wait_ge(*at("q_ah", m + 1))
                    v.tensor_tensor(Hl, XD["rden"][:], Hh.bitcast(fp32), ALU.subtract).then_inc(sem("q_att"), 1)

            def from_tokens(tag, adds, ln, frees=()):
                for s_, v_ in frees:
                    dve.wait_ge(*at(s_, v_))
                with dve.Fori(0, NP) as i:
                    for s in range(2):
                        tok = TOK[:, ds(2 * i + s, 1), :].rearrange("p a n -> p (a n)")
                        ps = acc[s][0:TP].rearrange("p c n -> p (c n)")[:, 0:D]
                        dve.wait_ge(*at(f"{tag}_yt{s}", i + 1))
                        if adds:
                            dve.wait_ge(*at(f"{tag}_ad{s}", 16 * adds * (i + 1)))
                        if adds == 2:
                            v.tensor_tensor(XC[f"ad{s}"][:, 0, :], XC[f"ad{s}"][:, 0, :], XC[f"ad{s}"][:, 1, :], ALU.add).then_inc(sem(f"{tag}_aa{s}"), 1)
                            dve.wait_ge(*at(f"{tag}_aa{s}", i + 1))
                        if adds:
                            v.tensor_tensor(tok, ps, XC[f"ad{s}"][:, 0, :], ALU.add).then_inc(sem(f"{tag}_add{s}"), 1)
                        else:
                            v.tensor_copy(tok, ps).then_inc(sem(f"{tag}_add{s}"), 1)
                        dve.wait_ge(*at(f"{tag}_add{s}", i + 1))
                        tile_stats(ln, 2 * i + s)
                ln_terms(ln, (1e-8,) if tag == "t1" else (1e-5,))

            from_tokens("t1", 1, "lnl")
            split_tiles("l")

            def mlp(tag, wb, groups, scale, mish=False):
                with dve.Fori(0, groups) as g:
                    with dve.Fori(0, 3) as i:
                        for s in range(2):
                            n = 3 * g + i
                            Hh, Hl = (x[:, ds(2 * i + s, 1), :].rearrange("p a n -> p (a n)") for x in (H_hi, H_lo))
                            dve.wait_ge(*at(f"{tag}_up{s}", n + 1))
                            if mish:
                                ex, n2 = XD[f"m{1 + s}"][:], XD["m3"][:]
                                k = [6 * (2 * n + s)]

                                def step(ins):
                                    k[0] = k[0] + 1
                                    ins.then_inc(sem(f"{tag}_mish"), 1)
                                    dve.wait_ge(*at(f"{tag}_mish", k[0]))
                                step(v.tensor_scalar(ex, ex, 1e9, None, ALU.min))
                                step(v.scalar_tensor_tensor(out=n2, in0=ex, scalar=2.0, in1=ex, op0=ALU.add, op1=ALU.mult))
                                step(v.tensor_scalar(ex, n2, 2.0, None, ALU.add))
                                step(v.reciprocal(ex, ex))
                                step(v.tensor_tensor(n2, n2, ex, ALU.mult))
                                step(v.tensor_tensor(t0[s][:], t0[s][:], n2, ALU.mult))
                            dve.wait_ge(*at("w_done1", 6 * g + wb))
                            v.tensor_copy(Hh, t0[s][:]).then_inc(sem(f"{tag}_hi{s}"), 1)
                            dve.wait_ge(*at(f"{tag}_hi{s}", n + 1))
                            v.tensor_tensor(Hl, t0[s][:], Hh.bitcast(fp32), ALU.subtract).then_inc(sem(f"{tag}_lo{s}"), 1)
                    with dve.Fori(0, 3) as i:
                        for s in range(2):
                            dve.wait_ge(*at(f"w_done{s}", 6 * g + i + wb + 4))
                            dve.wait_ge(*at(f"{tag}_dn{s}", 3 * g + i))
                            v.scalar_tensor_tensor(out=yblock(2 * i + s), in0=accf(s), scalar=scale, in1=yblock(2 * i + s),
                                                   op0=ALU.mult, op1=ALU.add).then_inc(sem(f"{tag}_dn{s}"), 1)

            dve.wait_ge(*at("gnn_back", 16))
            mlp("ml", WBASE["MLP"], MLP_GROUPS, 1.0)
            from_tokens("t2", 2, "lnx")
            split_tiles("x", pool_sum=True)

            dve.wait_ge(*at("x_lo1", NP))
            ch.link(v.tensor_reduce(pooled[:], pool_i[:].rearrange("p i k -> p k i"), AX.X, ALU.add))
            v.tensor_scalar(pooled[:], pooled[:], 1.0 / N, None, ALU.mult).then_inc(sem("r_pool"), 1)
            dve.wait_ge(*at("r_log", 1))
            dve.wait_ge(*at("rb_in", 16))
            ch.link(v.tensor_tensor(rt[0:1, 0:EXP], aux[0:1, 0, 0:EXP], rb[:], ALU.add))
            ch.link(v.max(rt[0:1, 8:16], rt[0:1, 0:8]))
            v.max_index(rti[0:1, 0:8], rt[0:1, 8:16], rt[0:1, 0:8]).then_inc(sem("r_idx"), 1)
            v.tensor_tensor(rt[0:1, 16:17], rt[0:1, 9:10], rt[0:1, 8:9], ALU.subtract).then_inc(sem("r_d"), 1)
            dve.wait_ge(*at("r_e", 1))
            ch.link(v.tensor_scalar(rt[0:1, 18:19], rt[0:1, 17:18], 1.0, None, ALU.add))
            ch.link(v.reciprocal(rt[0:1, 20:21], rt[0:1, 18:19]))
            v.tensor_tensor(rt[0:1, 21:22], rt[0:1, 20:21], rt[0:1, 17:18], ALU.mult).then_inc(sem("r_gates"), 1)
            dve.wait_ge(*at("r_gb", 1))
            ch.link(v.tensor_copy(gate[:, 0:TOPK], aux[:, 0, 8:8 + TOPK]))
            dve.wait_ge(*at("r_idx", 1))
            ers = [dve.value_load(rti[0:1, e:e + 1], min_val=0, max_val=EXP - 1) for e in range(TOPK)]
            ch.link(v.tensor_scalar(gb2[:], V[:, ds(ers[0] * KT + VC["ffn_b2"], KT)], gate[:, 0:1], None, ALU.mult))
            ch.link(v.scalar_tensor_tensor(out=gb2[:], in0=V[:, ds(ers[1] * KT + VC["ffn_b2"], KT)], scalar=gate[:, 1:2],
                                           in1=gb2[:], op0=ALU.mult, op1=ALU.add))
            for s in range(2):
                dve.wait_ge(*at(f"x_y{s}", NP))
            for m in range(KT):
                last = v.tensor_scalar(Y[:, m, :], Y[:, m, :], gb2[:, m:m + 1], None, ALU.add)
            ch.link(last)
            for e in range(TOPK):
                args = (f"e{e}", WBASE["EXP"] + 6 * EXP_GROUPS * e, EXP_GROUPS, gate[:, e:e + 1])
                with dve.If(ers[e] == 2):
                    mlp(*args, mish=True)
                with dve.Else():
                    mlp(*args)
            from_tokens("t3", 0, "lnf")
            dve.wait_ge(*at("gb_in", 48))
            with dve.Fori(0, NP) as i:
                for s in range(2):
                    xh = XC[f"xh{s}"][:]
                    dve.wait_ge(*at(f"f_n{s}", i + 1))
                    v.tensor_tensor(xh, xh, XA["gb"][:, 0, :], ALU.mult).then_inc(sem(f"f_m{s}"), 1)
                    dve.wait_ge(*at(f"f_m{s}", i + 1))
                    dve.wait_ge(*at("f_x2", 2 * i + s + 1))
                    v.tensor_tensor(xh, xh, XA["X2"][:, ds(2 * i + s, 1), :].rearrange("p a n -> p (a n)"), ALU.add).then_inc(sem(f"f_o{s}"), 1)


_INS = ["x", "src", "dst"] + ["L0_" + n for n in (
    "gnn_norm_g gnn_norm_b gnn_W1 gnn_a_src1 gnn_a_dst1 gnn_b1 gnn_W2 gnn_a_src2 gnn_a_dst2 gnn_b2 gnn_Wu gnn_bu "
    "mix_qkv_w mix_qkv_b mix_proj_w mix_proj_b mix_fc1_w mix_fc1_b mix_fc2_w mix_fc2_b mix_ln1_w mix_ln1_b "
    "mix_ln2_w mix_ln2_b ffn_router_w ffn_router_b ffn_w1 ffn_b1 ffn_w2 ffn_b2 ffn_ln_g ffn_ln_b").split()]


def kernel(**inputs):
    import numpy as _np
    import concourse.bacc as _bacc
    from concourse import mybir as _mybir
    from concourse.bass_utils import run_bass_kernel_spmd as _run

    nc = _bacc.Bacc("TRN2", target_bir_lowering=False, num_devices=1)
    arrays, args = {}, {}
    for name in _INS:
        a = _np.ascontiguousarray(inputs[name])
        arrays[f"in_{name}"] = a
        args[name.removeprefix("L0_")] = nc.dram_tensor(f"in_{name}", a.shape, _mybir.dt.from_np(a.dtype), kind="ExternalInput").ap()
    out = nc.dram_tensor("out", (N, D), _mybir.dt.from_np(_np.dtype("float32")), kind="ExternalOutput").ap()
    gps_layer(nc, args, out)
    r = _run(nc, [arrays], core_ids=[0])
    return r.results[0]["out"]
```

```python
from contextlib import ExitStack

import concourse.bass as bass
from concourse import mybir

N = 1250
D = 768
TP = 125
NT = N // TP
NP = NT // 2
CH = 418
NCH = 3
NF = CH * NCH
P = 128
KT = D // P
E = 21250
EPAIR = 2 * TP
NEP = E // EPAIR
H1, C1 = 4, 192
H2, C2 = 2, 96
NEG = 0.2
NHEAD, HD = 12, 64
MLP_GROUPS = 4
EXP, TOPK, EXP_GROUPS = 4, 2, 2
EH = 2 * D
BIG = 1e30

fp32 = mybir.dt.float32
f32r = mybir.dt.float32r
bf16 = mybir.dt.bfloat16
fp16 = mybir.dt.float16
i32 = mybir.dt.int32
u32 = mybir.dt.uint32
u16 = mybir.dt.uint16
ALU = mybir.AluOpType
ACT = mybir.ActivationFunctionType
AX = mybir.AxisListType
ds = bass.ds


class Chain:

    def __init__(self, eng, sem):
        self.eng, self.sem, self.n, self.links = eng, sem, 0, 0

    def link(self, ins):
        ins.then_inc(self.sem, 1)
        self.n = self.n + 1
        self.links += 1
        self.eng.wait_ge(self.sem, self.n)


VROWS = [("gnn_norm_g", KT), ("gnn_norm_b", KT), ("gnn_b1", KT), ("gnn_bu", KT), ("mix_ln1_w", KT),
         ("mix_ln1_b", KT), ("mix_proj_b", KT), ("mix_fc2_b", KT), ("mix_ln2_w", KT), ("mix_ln2_b", KT),
         ("mix_qkv_b", 3 * KT), ("mix_fc1_b", 4 * KT)]
VROWS2 = [("ffn_b1", EXP * 2 * KT), ("ffn_b2", EXP * KT), ("ffn_router_w", EXP * KT)]
VC = {}
_c = 0
for _name, _k in VROWS + VROWS2 + [("gnn_b2", 2), ("one", 1)]:
    VC[_name] = _c
    _c += _k
NV = _c
NV1 = sum(k for _, k in VROWS)
NV2 = sum(k for _, k in VROWS2)

BY_SLOT = """act_tile block_out c_acc c_madd ct_out dve_half f_o gat_ct gat_e gat_lo gat_mad gat_mu gat_mx gat_p
gat_ph gat_pu mlp_dn mlp_lo mlp_up oh oh_used q_num t2_aa tf_ev tf_lo tf_tr tf_xh tile_out tt_ad tt_add
tt_yt w_done w_hi w_in w_split""".split()
SINGLE = """c_tc c_tr e0_mish e1_mish f_x2 gat_R gat_h gat_hs gat_o gat_s gat_tr gat_u kv_h kv_kT kv_ka kv_tr kv_vT
ln0_xn q_a q_ah q_att q_dc q_den q_hi q_lo q_mat q_mf q_mh q_mul q_rec q_s""".split()
LOOPED = SINGLE + [name + slot for name in BY_SLOT for slot in "01"]

WSTAGES = [("W1", KT), ("W2", 2), ("WuT", KT), ("WuB", KT), ("KV", 2 * KT), ("Q", KT), ("PROJ", KT),
           ("MLP", MLP_GROUPS * 2 * KT), ("EXP", TOPK * EXP_GROUPS * 2 * KT)]
WBASE = {}
_n = 0
for _name, _k in WSTAGES:
    WBASE[_name] = _n // 2
    _n += _k
WTOTAL = _n


def gps_layer(nc, A, out):
    ctx = ExitStack()
    with ctx:
        sems = {}

        shared = {}

        def share(kind, tags, counts):
            for name, per_tag in counts.items():
                before = 0
                for tag, k in zip(tags, per_tag):
                    shared[f"{tag}_{name}"] = (f"{kind}_{name}", before)
                    before += k

        share("tf", "gumlx", {f"{k}{s}": (NP,) * 5 for k in ("tr", "ev", "lo") for s in range(2)}
              | {f"xh{s}": (NP, 0, NP, NP, NP) for s in range(2)})
        share("tt", ("t1", "t2", "t3"), {f"{k}{s}": (NP,) * 3 for k in ("yt", "add") for s in range(2)}
              | {f"ad{s}": (16 * NP, 96, 0) for s in range(2)})
        share("mlp", ("ml", "e0", "e1"), {f"{k}{s}": (3 * MLP_GROUPS, 3 * EXP_GROUPS, 3 * EXP_GROUPS)
                                          for k in ("up", "dn", "lo") for s in range(2)})
        share("ln", ("lna", "lnb", "lnl", "lnx", "lnf"), {"st": (NT,) * 5, "ag": (NT,) * 5, "ve": (1, 2, 1, 1, 1),
                                                          "sd": (1,) * 5, "rs": (1, 2, 1, 1, 1)})
        share("gat", ("g1", "g2"), {"S": (2, 2), "S_tr": (2, 2), "srow": (2, 2), "r_out": (32, 32), "ssb": (16 * H1, 0),
                                    "h_out": (16, 16), "h": (3 * KT, 0), "tr": (3 * KT, 0), "ab": (32, 32), "s": (2 * NT, NT),
                                    "R0": (1, 1), "ones": (1, 1), "hs": (H1, 1), "hh": (H1, 1), "u": (H1, H2), "o": (3 * H1, 0),
                                    "nb": (3 * H1, 0), "R": (H1, H2), "he0": (32, 0), "he1": (32, 0), "db0": (64, 0),
                                    "db1": (64, 0), "xh": (KT, H2), "x": (KT, H2)}
              | {f"{k}{s}": (NP, NP) for k in ("mx", "mu") for s in range(2)} | {f"mad{s}": (16 * NP, 0) for s in range(2)}
              | {f"ct{s}": (16 * NP * H1, 0) for s in range(2)}
              | {f"{k}{s}": (NP * H1, 0) for k in ("e", "p", "ph", "lo", "pu") for s in range(2)})

        def follow(kind, *parts):
            before = 0
            for name, k in parts:
                shared[name] = (kind, before)
                before += k

        follow("pe_once", ("v_tr", 1), ("e_tr", 1), ("e_bb", 1), ("e_row", 1), ("r_sum", 1), ("r_log", 1), ("r_gb", 1))
        follow("dve_once", ("e_f", 2), ("e_cmm", 2), ("e_ec", 1), ("e_bc", 1), ("bnd", 1), ("r_pool", 1), ("r_idx", 1),
               ("r_d", 1), ("r_gates", 1))
        follow("pool_once", ("g_pad", 1), ("u_pad", 1), ("m_pad", 1), ("kv_ones", 1))
        follow("load", ("x_in", 16 * NT), ("m_tok", 16 * NT), ("gnn_back", 16), ("gb_in", 48))
        follow("store", ("xn_out", 16), ("gnn_out", 16), ("t1_tok_out", 16), ("t2_tok_out", 16))
        for s in range(2):
            follow(f"block_out{s}", (f"w1_y{s}", 3), (f"w2_y{s}", 1), (f"wut_y{s}", 3), (f"wub_y{s}", 3), (f"pj_y{s}", 3))
            follow(f"act_tile{s}", (f"c_sb{s}", NP), (f"f_n{s}", NP))
            follow(f"tile_out{s}", (f"madd_out{s}", 16 * NP), (f"f_out{s}", 16 * NP))
            follow(f"dve_half{s}", (f"g_hi{s}", NP), (f"g1_a{s}", NP * H1), (f"u_hi{s}", NP), (f"g2_a{s}", NP * H2),
                   (f"m_hi{s}", NP), (f"l_hi{s}", NP), (f"ml_hi{s}", 3 * MLP_GROUPS), (f"x_hi{s}", NP),
                   (f"e0_hi{s}", 3 * EXP_GROUPS), (f"e1_hi{s}", 3 * EXP_GROUPS), (f"f_m{s}", NP))

        def sem(name):
            name = shared.get(name, (name, 0))[0]
            if name not in sems:
                sems[name] = ctx.enter_context(nc.semaphore(name))
            return sems[name]

        def at(name, value):
            name, before = shared.get(name, (name, 0))
            return sem(name), value + (before + 1 if name in LOOPED else before)

        def sb(name, shape, dt, stack=ctx):
            return stack.enter_context(nc.sbuf_tensor(name, shape, dt))

        def dram(name, shape, dt):
            return nc.dram_tensor(name, shape, dt, kind="Internal").ap()

        xn_d = dram("xn_d", (NT, TP, D), fp32)
        x1_d = dram("x1_d", (NT, TP, D), fp32)
        x2_d = dram("x2_d", (NT, TP, D), fp32)
        h1_d = dram("h1_d", (NT, TP, D), fp32)
        h2_d = dram("h2_d", (NT, TP, H2 * C2), fp32)
        gnn_d = dram("gnn_d", (P, KT, NF), fp32)
        ct_d = dram("ct_d", (NT, TP, N), u16)
        madd_d = dram("madd_d", (NT, TP, N), bf16)
        row_d = [dram(f"row_d{k}", (NT, 8, TP), fp32) for k in range(4)]

        x_t = A["x"].rearrange("(i t) d -> i t d", t=TP)
        out_t = out.rearrange("(i t) d -> i t d", t=TP)

        ident = sb("ident", [P, P], fp32)
        identb = sb("identb", [TP, TP], bf16)
        sel = sb("sel", [P, 3, P], fp32)
        ones_row = sb("ones_row", [1, P], fp32)
        tri = sb("tri", [NT, NT], fp32)
        V = sb("V", [P, NV], fp32)
        gb2 = sb("gb2", [P, KT], fp32)
        mv = sb("mv", [TP, NT, 2], fp32)
        st = sb("st", [TP, NT, 2, 6], fp32)
        ve = sb("ve", [TP, 4, NT], fp32)
        rs = sb("rs", [TP, 2, NT], fp32)
        nm = sb("nm", [TP, 2, NT], fp32)
        S = sb("S", [TP, NT, 8], fp32)
        S2 = sb("S2", [TP, NT, 8], fp32)
        Sd = sb("Sd", [TP, NT, 8], fp32)
        MU = sb("MU", [TP, NT, 4], fp32)
        Dc = sb("Dc", [TP, NT, 8], fp32)
        mus = sb("mus", [TP, 2, 4], fp32)
        rt = sb("rt", [1, 64], fp32)
        rti = sb("rti", [1, 16], u32)
        bnd = sb("bnd", [1, 3 * NT], i32)
        gate = sb("gate", [P, 4], fp32)
        KVf = sb("KVf", [P, KT, P + 1], fp32)
        bdiag = sb("bdiag", [P, P], fp32)
        pooled = sb("pooled", [P, KT], fp32)
        rb = sb("rb", [1, EXP], fp32)

        w_raw = [sb(f"w_raw{s}", [P, KT, P], fp32) for s in range(2)]
        w_hi = [sb(f"w_hi{s}", [P, KT, P], f32r) for s in range(2)]
        w_lo = [sb(f"w_lo{s}", [P, KT, P], f32r) for s in range(2)]
        t0 = [sb(f"t0_{s}", [P, NF], fp32) for s in range(2)]
        Y = sb("Y", [P, KT, NF], fp32)

        def area(*groups):
            made, size = {}, 0
            widest = []
            for g in groups:
                n = sum(_bytes(s, d) for _, s, d in g)
                if n > size:
                    size, widest = n, g
            order = [g for g in groups if g is not widest] + [widest]
            for g in order:
                tmp = ExitStack()
                for name, s, d in g:
                    made[name] = sb(name, s, d, ctx if g is widest else tmp)
                tmp.close()
            return made

        def _bytes(shape, dt):
            n = 1
            for x in shape[1:]:
                n *= x
            return -(-n * mybir.dt.size(dt) // 32) * 32

        XA = area([("X_hi", [P, KT, NF], f32r), ("X_lo", [P, KT, NF], f32r)],
                  [(f"he_{k}{s}", [TP, NT, 256], fp32 if k == "raw" else f32r)
                   for k in ("raw", "hi", "lo") for s in range(2)],
                  [("Z", [TP, 2 * NF], bf16), ("iota", [TP, NF], fp16)]
                  + [(f"S1h{s}", [TP, 2, NF], bf16) for s in range(2)]
                  + [(f"D1h{s}", [TP, 2, TP], bf16) for s in range(2)] + [("D1z", [TP, TP], bf16)]
                  + [("ei", [NEP, 2, EPAIR], i32), ("ef", [NEP, 2, EPAIR], fp32), ("ec", [TP, 5 * NEP], fp32),
                     ("cmm", [NEP, 2, NT], fp32), ("cm2", [NEP, 2], fp32), ("bb", [NT, 8, NEP], fp32),
                     ("bc", [NT, 8], fp32), ("ix", [NT, 2, NEP], fp32), ("madds0", [TP, NF], bf16), ("madds1", [TP, NF], bf16),
                     ("ctb0", [TP, NT, TP], u16), ("ctb1", [TP, NT, TP], u16)],
                  [("gb", [TP, 2, D], fp32), ("X2", [TP, NT, D], fp32)])
        XC = area([("H_hi", [P, KT, NF], f32r), ("H_lo", [P, KT, NF], f32r)],
                  [("TOK", [TP, NT, D], fp32)] + [(f"xh{s}", [TP, D], fp32) for s in range(2)]
                  + [(f"ft{s}", [P, KT, TP], fp32) for s in range(2)]
                  + [(f"ad{s}", [TP, 2, D], fp32) for s in range(2)],
                  [("TOK_", [TP, NT, D], fp32)] + [(f"aa{q}", [TP, 2, D], fp32) for q in range(4)],
                  [("Db0", [TP, 2, N], fp32), ("Db1", [TP, 2, N], fp32), ("U0", [P, NF], fp32),
                   ("U1", [P, NF], fp32), ("R", [P, NF], fp32), ("Ph0", [TP, NF], f32r), ("Ph1", [TP, NF], f32r),
                   ("Pl0", [TP, NF], f32r), ("Pl1", [TP, NF], f32r), ("CT0", [TP, N], u16), ("CT1", [TP, N], u16)],
                  [("HT", [TP, NT, D], fp32), ("ab", [TP, 2, D], fp32), 
                   ("pr", [TP, 8, C1], fp32), ("srow", [80, TP], fp32),
                   ("mad0", [TP, N], bf16), ("mad1", [TP, N], bf16), ("trash", [TP, 4, N], bf16)],
                  [("HT2", [TP, NT, H2 * C2], fp32), ("ab2", [TP, 2, H2 * C2], fp32), ("pr2", [TP, 2 * H2, C2], fp32),
                   ("srow2", [80, TP], fp32), ("trash2", [TP, H2, N], bf16), ("mads2", [TP, NT, N], bf16)]
                  + [(f"uxh{q}", [TP, D], fp32) for q in range(4)] + [(f"uft{s}", [P, KT, TP], fp32) for s in range(2)])
        XD = area([("q_hi", [P, NF], f32r), ("q_lo", [P, NF], f32r), ("rden", [P, NF], fp32)]
                  + [(f"m_{b}{s}", [P, 2, P], f32r) for b in ("h", "l") for s in range(2)]
                  + [("kvf", [P, 2, P], fp32)],
                  [("e2_0", [TP, N], fp32), ("e2_1", [TP, N], fp32), ("pp0", [TP, N], fp32), ("pp1", [TP, N], fp32)],
                  [("ssb", [TP, 4, N], fp32)],
                  [("O2h", [C2, H2, NF], f32r), ("O2l", [C2, H2, NF], f32r)],
                  [("k_tok", [TP, NT, P], fp32), ("v_tok", [TP, NT, P + 2], fp32), ("kT", [P, NF], fp32), ("vT", [P, NF], fp32)],
                  [("m1", [P, NF], fp32), ("m2", [P, NF], fp32), ("m3", [P, NF], fp32)])
        acc = [ctx.enter_context(nc.psum_tensor(f"acc{s}", [P, NCH, 512], fp32)) for s in range(2)]
        aux = ctx.enter_context(nc.psum_tensor("aux", [P, 2, 512], fp32))

        X_hi, X_lo, H_hi, H_lo = XA["X_hi"], XA["X_lo"], XC["H_hi"], XC["H_lo"]
        TOK = XC["TOK"]

        def accf(s, parts=P):
            return acc[s][0:parts, :, 0:CH]

        def f3(ap):
            return ap.rearrange("p (c n) -> p c n", c=NCH)

        def vcol(name, k, parts=P):
            if isinstance(k, int):
                return V[0:parts, VC[name] + k:VC[name] + k + 1]
            return V[0:parts, ds(k + VC[name], 1)]

        block = ctx.enter_context(nc.Block())

        @block.sync
        def _(sp):
            r = 0
            for name, k in VROWS:
                sp.dma_start(t0[0][r:r + k, 0:P], A[name].rearrange("(r p) -> r p", p=P)).then_inc(sem("v_in"), 16)
                r += k
            r = 0
            for name, k in VROWS2:
                sp.dma_start(t0[0][r:r + k, P:2 * P], A[name].rearrange("e (r p) -> (e r) p", p=P)).then_inc(sem("v_in"), 16)
                r += k
            sp.dma_start(t0[0][0:2, 2 * P:2 * P + C2], A["gnn_b2"].rearrange("(r p) -> r p", p=C2)).then_inc(sem("v_in"), 16)
            for v, name in enumerate(("src", "dst")):
                sp.dma_start(XA["ei"][:, v, :], A[name].rearrange("(r e) -> r e", e=EPAIR)).then_inc(sem("e_in"), 16)
            for i in range(NT):
                sp.dma_start(TOK[:, i, :], x_t[i]).then_inc(sem("x_in"), 16)
            sp.dma_start(rb[:], A["ffn_router_b"].rearrange("(a n) -> a n", a=1)).then_inc(sem("rb_in"), 16)

            def wload(stage, k, s, src):
                if not (isinstance(k, int) and k == 0):
                    sp.wait_ge(*at(f"w_split{s}", k))
                kp, kt, n = src.shape
                sp.dma_start(w_raw[s][0:kp, 0:kt, 0:n], src).then_inc(sem(f"w_in{s}"), 16)

            def wcols(W, c, n=P, kp=P):
                return W.rearrange("(k p) n -> p k n", p=kp)[:, :, ds(c, n)]

            def gemm_weights(stage, W, n=P, kp=P, pairs=(0, 3)):
                with sp.Fori(*pairs) as i:
                    for s in range(2):
                        wload(stage, WBASE[stage] + i, s, wcols(W, (2 * i + s) * n, n, kp))

            gemm_weights("W1", A["gnn_W1"], pairs=(0, 1))

            with sp.Fori(0, NP) as i:
                for s in range(2):
                    sp.wait_ge(*at(f"c_madd{s}", i + 1))
                    sp.dma_start(madd_d[ds(2 * i + s, 1)].rearrange("a t n -> (a t) n"),
                                 XA[f"madds{s}"][:, 0:N]).then_inc(sem(f"madd_out{s}"), 16)
                for s in range(2):
                    sp.wait_ge(*at("c_tc", 6 * i + 3 * s + 3))
                    sp.dma_start(ct_d[:, :, ds((2 * i + s) * TP, TP)].rearrange("j t n -> t j n"),
                                 XA[f"ctb{s}"][:]).then_inc(sem(f"ct_out{s}"), 16)

            sp.wait_ge(*at("ln0_xn", NT))
            sp.dma_start(xn_d.rearrange("i t d -> t i d"), TOK[:]).then_inc(sem("xn_out"), 16)

            gemm_weights("W1", A["gnn_W1"], pairs=(1, 3))

            def attention_loads(g, H, C, h_d, adst, asrc):
                W = H * C
                HT, ab, srow = ((XC[k + ("2" if g == 2 else "")]) for k in ("HT", "ab", "srow"))
                if g == 1:
                    for s in range(2):
                        sp.wait_ge(*at(f"g_lo{s}", NP))
                else:
                    sp.wait_ge(*at("g1_o", 3 * H1))
                for v, a in enumerate((asrc, adst)):
                    sp.dma_start(ab[:, v, 0:W], a.rearrange("h c -> (h c)").partition_broadcast(TP)).then_inc(sem(f"g{g}_ab"), 16)
                if g == 2:
                    sp.dma_start(XC["mads2"][:], madd_d.rearrange("j t n -> t j n")).then_inc(sem("g2_mad0"), 16)
                    sp.wait_ge(*at("xn_out", 16))
                    for q in range(4):
                        sp.dma_start(XC[f"uxh{q}"][:], xn_d[q]).then_inc(sem(f"u_in{q}"), 16)
                    gemm_weights("WuT", A["gnn_Wu"][0:D, :], pairs=(0, 1))
                hv = h_d.rearrange("i t d -> t i d")

                def he_load(h):
                    if g == 1:
                        if h >= 2:
                            sp.wait_ge(*at("g1_hs", h - 1))
                        o = 64 * (h % 2)
                        sp.dma_start(XA[f"he_raw{h % 2}"][:, :, o:o + C], hv[:, :, h * C:(h + 1) * C]).then_inc(sem(f"g1_he{h % 2}"), 16)
                    else:
                        sp.dma_start(XA["he_raw0"][:, :, h * P:h * P + C], hv[:, :, h * C:(h + 1) * C]).then_inc(sem("g2_he0"), 16)

                sp.wait_ge(*at(f"g{g}_h", (3 * KT if g == 1 else 3 * H2)))
                sp.dma_start(h_d.rearrange("i t d -> t i d"), HT[:, :, 0:W]).then_inc(sem(f"g{g}_h_out"), 16)
                rows = row_d[2 * (g - 1)]
                sp.wait_ge(*at(f"g{g}_srow", 1))
                sp.dma_start(rows.rearrange("i c t -> (i c) t"), srow[:]).then_inc(sem(f"g{g}_r_out"), 16)
                sp.wait_ge(*at(f"g{g}_r_out", 16))
                for h in range(H):
                    sp.dma_start(XD["ssb"][:, h, :].rearrange("t (i u) -> t i u", u=TP),
                                 rows[:, h, :].partition_broadcast(TP)).then_inc(sem(f"g{g}_ssb"), 16)
                if g == 1:
                    for s in range(2):
                        sp.wait_ge(*at(f"madd_out{s}", 16 * NP))
                    for s in range(2):
                        sp.dma_start(XC[f"mad{s}"][:], madd_d[s]).then_inc(sem(f"g{g}_mad{s}"), 16)
                    sp.wait_ge(*at("g1_h_out", 16))
                    sp.wait_ge(*at("g1_ones", 1))
                    for h in range(2):
                        he_load(h)
                    with sp.Fori(1, NP) as i:
                        for s in range(2):
                            sp.wait_ge(*at(f"g{g}_mx{s}", i))
                            sp.dma_start(XC[f"mad{s}"][:], madd_d[ds(2 * i + s, 1)].rearrange("a t n -> (a t) n")).then_inc(sem(f"g{g}_mad{s}"), 16)
                else:
                    for t in range(4, NT):
                        sp.wait_ge(*at(f"u_tr{t % 2}", (t - 4) // 2 + 1))
                        sp.dma_start(XC[f"uxh{t % 4}"][:], xn_d[t]).then_inc(sem(f"u_in{t % 4}"), 16)
                    gemm_weights("WuT", A["gnn_Wu"][0:D, :], pairs=(1, 3))
                rows = row_d[2 * (g - 1) + 1]
                sp.wait_ge(*at(f"g{g}_srow", 2))
                sp.dma_start(rows.rearrange("i c t -> (i c) t"), srow[:]).then_inc(sem(f"g{g}_r_out"), 16)
                sp.wait_ge(*at(f"g{g}_r_out", 32))
                sp.wait_ge(*at(f"g{g}_h_out", 16))
                if g == 1:
                    for s in range(2):
                        sp.wait_ge(*at(f"ct_out{s}", 16 * NP))

                def db_load(h, ps):
                    for v in range(2):
                        sp.dma_start(XC[f"Db{ps}"][:, v, :].rearrange("t (i u) -> t i u", u=TP),
                                     rows[:, 4 * v + h, :].partition_broadcast(TP)).then_inc(sem(f"g{g}_db{ps}"), 16)

                def ct_loads(units):
                    with sp.Fori(0, NP) as j:
                        for s in range(2):
                            sp.wait_ge(*at(f"g{g}_p{s}", j + units))
                            sp.dma_start(XC[f"CT{s}"][:], ct_d[ds(2 * j + s, 1)].rearrange("a t n -> (a t) n")).then_inc(sem(f"g{g}_ct{s}"), 16)

                for h in range(2):
                    db_load(h, h)

                if g == 2:
                    sp.wait_ge(*at("g2_ones", 1))
                    for h in range(2):
                        he_load(h)
                for h in range(H):
                    ct_loads(h * NP)
                    if h + 2 < H:
                        he_load(h + 2)
                        for s in range(2):
                            sp.wait_ge(*at(f"g{g}_a{s}", NP * (h + 1)))
                        db_load(h + 2, h % 2)

            attention_loads(1, H1, C1, h1_d, A["gnn_a_dst1"], A["gnn_a_src1"])
            for s in range(2):
                wload("W2", WBASE["W2"], s, wcols(A["gnn_W2"], s * C2, C2))
            attention_loads(2, H2, C2, h2_d, A["gnn_a_dst2"], A["gnn_a_src2"])

            def reload(tag, src, after):
                for s_, v_ in after:
                    sp.wait_ge(*at(s_, v_))
                for i in range(NT):
                    sp.dma_start(TOK[:, i, :], src[i]).then_inc(sem(f"{tag}_tok"), 16)

            gemm_weights("WuB", A["gnn_Wu"][D:D + H2 * C2, :], kp=C2)

            def kv_weights(a, b):
                with sp.Fori(a, b) as i:
                    for s in range(2):
                        wload("KV", WBASE["KV"] + i, s, wcols(A["mix_qkv_w"], (i + (1 + s) * KT) * P))

            kv_weights(0, 1)
            reload("m", xn_d, [("g2_x", H2)])
            sp.wait_ge(*at("wub_y1", 3))
            sp.wait_ge(*at("wub_y0", 3))
            sp.dma_start(gnn_d, Y[:]).then_inc(sem("gnn_out"), 16)
            kv_weights(1, KT)
            gemm_weights("Q", A["mix_qkv_w"][:, 0:D])
            gemm_weights("PROJ", A["mix_proj_w"])

            def addend_loads(tag, srcs, after):
                for s_, v_ in after:
                    sp.wait_ge(*at(s_, v_))
                with sp.Fori(0, NP) as i:
                    for s in range(2):
                        sp.wait_ge(*at(f"{tag}_add{s}", i))
                        for a, src in enumerate(srcs):
                            sp.dma_start(XC[f"ad{s}"][:, a, :], src[ds(2 * i + s, 1)].rearrange("a t d -> (a t) d")).then_inc(sem(f"{tag}_ad{s}"), 16)

            def xstore(tag, dst):
                for s in range(2):
                    sp.wait_ge(*at(f"{tag}_add{s}", NP))
                sp.dma_start(dst.rearrange("i t d -> t i d"), TOK[:]).then_inc(sem(f"{tag}_tok_out"), 16)

            def fc1_weights(g, a, b):
                with sp.Fori(a, b) as i:
                    for s in range(2):
                        wload("MLP", WBASE["MLP"] + 6 * g + i, s, wcols(A["mix_fc1_w"], (6 * g + 2 * i + s) * P))

            def fc2_weights(g):
                with sp.Fori(0, 3) as i:
                    for s in range(2):
                        src = A["mix_fc2_w"].rearrange("(g k p) n -> p g k n", p=P, k=KT)[:, ds(g, 1), :, ds((2 * i + s) * P, P)]
                        wload("MLP", WBASE["MLP"] + 6 * g + 3 + i, s, src.rearrange("p g k n -> p (g k) n"))

            fc1_weights(0, 0, 1)
            addend_loads("t1", [xn_d], [("w_done0", WBASE["MLP"]), ("w_done1", WBASE["MLP"])])
            xstore("t1", x1_d)
            sp.wait_ge(*at("gnn_out", 16))
            sp.dma_start(Y[:], gnn_d).then_inc(sem("gnn_back"), 16)
            fc1_weights(0, 1, 3)
            fc2_weights(0)
            with sp.Fori(1, MLP_GROUPS) as g:
                fc1_weights(g, 0, 3)
                fc2_weights(g)
            sp.wait_ge(*at("t1_tok_out", 16))
            for s in range(2):
                sp.wait_ge(*at(f"w_done{s}", WBASE["EXP"]))
            for t in range(NT):
                if t >= 4:
                    sp.wait_ge(*at(f"t2_add{t % 2}", (t - 4) // 2 + 1))
                for a, src in enumerate((x_t, x1_d)):
                    sp.dma_start(XC[f"aa{t % 4}"][:, a, :], src[t]).then_inc(sem(f"t2_ad{t % 4}"), 16)
            xstore("t2", x2_d)

            sp.wait_ge(*at("r_idx", 1))
            for e in range(TOPK):
                ei_ = sp.value_load(rti[0:1, e:e + 1], min_val=0, max_val=EXP - 1)
                WB = WBASE["EXP"] + 12 * e
                with sp.Fori(0, EXP_GROUPS) as g:
                    with sp.Fori(0, 3) as i:
                        for s in range(2):
                            src = A["ffn_w1"].rearrange("e (k p) n -> p e k n", p=P)[:, ds(ei_, 1), :, ds((6 * g + 2 * i + s) * P, P)]
                            wload("EXP", WB + 6 * g + i, s, src.rearrange("p e k n -> p (e k) n"))
                    with sp.Fori(0, 3) as i:
                        for s in range(2):
                            src = A["ffn_w2"].rearrange("e (g k p) n -> p (e g) k n", p=P, k=KT)[:, ds(ei_ * 2 + g, 1), :, ds((2 * i + s) * P, P)]
                            wload("EXP", WB + 6 * g + 3 + i, s, src.rearrange("p e k n -> p (e k) n"))
            sp.wait_ge(*at("w_done0", WBASE["EXP"] + 24))
            sp.wait_ge(*at("w_done1", WBASE["EXP"] + 24))
            sp.wait_ge(*at("t2_tok_out", 16))
            sp.dma_start(XA["gb"][:, 0, :], A["ffn_ln_g"].partition_broadcast(TP)).then_inc(sem("gb_in"), 16)
            sp.dma_start(XA["gb"][:, 1, :], A["ffn_ln_b"].partition_broadcast(TP)).then_inc(sem("gb_in"), 16)
            sp.dma_start(XA["X2"][:], x2_d.rearrange("i t d -> t i d")).then_inc(sem("gb_in"), 16)
            with sp.Fori(0, NP) as i:
                for s in range(2):
                    sp.wait_ge(*at(f"f_o{s}", i + 1))
                    sp.dma_start(out_t[ds(2 * i + s, 1)].rearrange("a t d -> (a t) d"),
                                 TOK[:, ds(2 * i + s, 1), :].rearrange("p a n -> p (a n)")).then_inc(sem(f"f_out{s}"), 16)
            for s in range(2):
                sp.wait_ge(*at(f"f_out{s}", 16 * NP))
            sp.wait_ge(*at("gnn_out", 16))

        @block.tensor
        def _(pe):
            def transpose_tiles(src, parts, s, tag, first, bank0, w0, after_first=None):
                for q, (a, b) in enumerate(((0, 4), (4, 8), (8, 10))):
                    bank = (bank0 + q) % 2
                    pe.wait_ge(*at(f"{tag}_h", first + q - (1 if q + w0 else 0)))
                    for t in range(a, b):
                        last = nc.tensor.transpose(aux[0:TP, bank, (t - a) * P:(t - a) * P + parts],
                                                   src[0:parts, t * TP:(t + 1) * TP], ident[0:parts, 0:parts])
                    last.then_inc(sem(f"{tag}_tr"), 1)

            def gemm(s, k, rhs_hi, rhs_lo, a, kt=KT, kp=P, mp=P, ready=None):
                pe.wait_ge(*at(f"w_split{s}", k + 1))
                for kk in range(kt):
                    if ready is not None:
                        pe.wait_ge(*ready(kk))
                    for n, (w, r) in enumerate(((w_hi, rhs_hi), (w_hi, rhs_lo), (w_lo, rhs_hi))):
                        for c in range(NCH):
                            last = nc.tensor.matmul(acc[a][0:mp, c, 0:CH], w[s][0:kp, kk, 0:mp],
                                                    r[0:kp, kk, c * CH:(c + 1) * CH],
                                                    start=(kk == 0 and n == 0), stop=(kk == kt - 1 and n == 2))
                last.then_inc(sem(f"w_done{s}"), 1)

            for name in LOOPED[::2]:
                pe.sem_inc(sem(name), 1)
            for h in range(2):
                pe.sem_inc(sem(f"oh_used{h}"), 1)
            pe.wait_ge(*at("cst", 3))
            pe.wait_ge(*at("v_in", 16 * (len(VROWS) + len(VROWS2) + 1)))
            nc.tensor.transpose(aux[:, 0, 0:NV1], t0[0][0:NV1, 0:P], ident[0:NV1, 0:NV1])
            nc.tensor.transpose(aux[:, 0, P:P + NV2], t0[0][0:NV2, P:2 * P], ident[0:NV2, 0:NV2])
            nc.tensor.transpose(aux[0:C2, 0, 2 * P:2 * P + 2], t0[0][0:2, 2 * P:2 * P + C2], ident[0:2, 0:2]).then_inc(sem("v_tr"), 1)
            pe.wait_ge(*at("e_f", 2))
            for v in range(2):
                for half in range(2):
                    o = (2 * v + half) * NEP
                    last = nc.tensor.transpose(aux[0:TP, 1, o:o + NEP], XA["ef"][:, v, half * TP:(half + 1) * TP],
                                               ident[0:NEP, 0:NEP])
            last.then_inc(sem("e_tr"), 1)
            pe.wait_ge(*at("e_cmm", 2))
            pe.wait_ge(*at("v_cp", 1))
            for k in range(2):
                last = nc.tensor.matmul(aux[0:NT, 0, k * P:k * P + NEP], XA["cmm"][:, k, :], ident[0:NEP, 0:NEP],
                                        start=True, stop=True)
            last.then_inc(sem("e_bb"), 1)
            pe.wait_ge(*at("e_bc", 1))
            pe.wait_ge(*at("e_ec", 1))
            nc.tensor.matmul(aux[0:1, 1, 0:NT], XA["bc"][:, 0:1], ident[0:NT, 0:NT], start=True, stop=True)
            nc.tensor.matmul(aux[0:1, 1, 16:16 + NT], XA["bc"][:, 2:3], ident[0:NT, 0:NT], start=True, stop=True)
            nc.tensor.matmul(aux[0:1, 1, 32:32 + NT], XA["bc"][:, 2:3], tri[:], start=True, stop=True).then_inc(sem("e_row"), 1)

            pe.wait_ge(*at("bnd", 1))
            pe.wait_ge(*at("c_const", 3))
            with pe.Fori(0, NP) as i:
                for s in range(2):
                    t = 2 * i + s
                    pairs = pe.value_load(bnd[0:1, ds(t + NT, 1)], min_val=1, max_val=NEP)
                    before = pe.value_load(bnd[0:1, ds(t + 2 * NT, 1)], min_val=0, max_val=NEP * NT)
                    pe.wait_ge(*at(f"c_sb{s}", i))
                    for c in range(NCH):
                        nc.tensor.matmul(acc[s][0:TP, c, 0:CH], identb[:], XA["Z"][:, ds(NF + c * CH - t * TP, CH)],
                                         start=True, stop=False)
                    with pe.Fori(0, pairs) as p:
                        q = (p + before) & 1
                        for h in range(2):
                            D1, S1 = (XA[f"{k}{h}"][:, ds(q, 1), :].rearrange("p a n -> p (a n)") for k in ("D1h", "S1h"))
                            pe.wait_ge(*at(f"oh{h}", p + before + 1))
                            for c in range(NCH):
                                last = nc.tensor.matmul(acc[s][0:TP, c, 0:CH], D1,
                                                        S1[:, c * CH:(c + 1) * CH], start=False, stop=False)
                            last.then_inc(sem(f"oh_used{h}"), 1)
                    for c in range(NCH):
                        last = nc.tensor.matmul(acc[s][0:TP, c, 0:CH], XA["D1z"][:], XA["Z"][:, 0:CH],
                                                start=False, stop=True)
                    last.then_inc(sem(f"c_acc{s}"), 1)
                for s in range(2):
                    pe.wait_ge(*at(f"c_sb{s}", i + 1))
                    for q, (a, b) in enumerate(((0, 4), (4, 8), (8, 10))):
                        bank = (3 * s + q) % 2
                        pe.wait_ge(*at("c_tc", 6 * i + 3 * s + q - (1 if 3 * s + q else 0)))
                        for j in range(a, b):
                            last = nc.tensor.transpose(aux[0:TP, bank, (j - a) * P:(j - a) * P + TP],
                                                       t0[s][0:TP, j * TP:(j + 1) * TP], ident[0:TP, 0:TP])
                        last.then_inc(sem("c_tr"), 1)

            def to_features(tag, frees):
                for f in frees:
                    pe.wait_ge(*f)
                with pe.Fori(0, NP) as i:
                    for s in range(2):
                        pe.wait_ge(*at(f"{tag}_xh{s}", i + 1))
                        pe.wait_ge(*at(f"{tag}_ev{s}", i))
                        for m in range(KT):
                            last = nc.tensor.transpose(acc[s][:, m // 4, (m % 4) * P:(m % 4) * P + TP],
                                                       XC[f"xh{s}"][:, m * P:(m + 1) * P], ident[0:TP, 0:TP])
                        last.then_inc(sem(f"{tag}_tr{s}"), 1)

            def to_tokens(tag, frees):
                for f in frees:
                    pe.wait_ge(*f)
                for t in range(NT):
                    s = t % 2
                    if t >= 2:
                        pe.wait_ge(*at(f"{tag}_add{s}", t // 2))
                    for m in range(KT):
                        last = nc.tensor.transpose(acc[s][0:TP, m // 4, (m % 4) * P:(m % 4 + 1) * P],
                                                   Y[:, m, t * TP:(t + 1) * TP], ident[:])
                    last.then_inc(sem(f"{tag}_yt{s}"), 1)

            to_features("g", [at("c_sb0", NP), at("c_sb1", NP)])

            for s in range(2):
                pe.wait_ge(*at(f"g_ev{s}", NP))
                pe.wait_ge(*at(f"g_lo{s}", NP))
            pe.wait_ge(*at("c_tc", 3 * NT))
            with pe.Fori(0, 3) as i:
                for s in range(2):
                    pe.wait_ge(*at(f"w1_y{s}", i))
                    gemm(s, WBASE["W1"] + i, X_hi, X_lo, s)
                for s in range(2):
                    pe.wait_ge(*at(f"w1_y{s}", i + 1))
                    transpose_tiles(t0[s], P, s, "g1", 6 * i + 3 * s, s, s)

            def attention_rows(g, n):
                pe.wait_ge(*at(f"g{g}_S", n))
                nc.tensor.transpose(aux[0:80, 0, 0:TP], (S if n == 1 else Dc)[:].rearrange("t i c -> t (i c)"),
                                    ident[0:TP, 0:TP]).then_inc(sem(f"g{g}_S_tr"), 1)

            def attention_head(g, h, blocks, between=None):
                pe.wait_ge(*at(f"g{g}_hs", (h + 1) if g == 1 else 1))
                if h:
                    pe.wait_ge(*at(f"g{g}_u", h))
                for j in range(NT):
                    s = j % 2
                    pe.wait_ge(*at(f"g{g}_ph{s}", NP * h + j // 2 + 1))
                    for n, part in enumerate(("hi", "lo", "Pl")):
                        if part == "Pl":
                            pe.wait_ge(*at(f"g{g}_lo{s}", NP * h + j // 2 + 1))
                        for a, hi, lo in blocks:
                            w, r = (lo if part == "lo" else hi), XC[f"Pl{s}" if part == "Pl" else f"Ph{s}"]
                            for c in range(NCH):
                                last = nc.tensor.matmul(acc[a][:, c, 0:CH], w[:, j, :], r[:, c * CH:(c + 1) * CH],
                                                        start=(j == 0 and n == 0), stop=(j == NT - 1 and n == 2))
                    last.then_inc(sem(f"g{g}_pu{s}"), 1)
                    if j == 3 and between is not None:
                        between()

            def attention_norm(g, h, k):
                pe.wait_ge(*at(f"g{g}_R", h + 1))
                for c in range(NCH):
                    pe.wait_ge(*at(f"g{g}_o", 3 * h + c - (1 if c else 0)))
                    nc.tensor.matmul(aux[:, c % 2, 0:CH], sel[:, k, :], XC["R"][:, c * CH:(c + 1) * CH],
                                     start=True, stop=True).then_inc(sem(f"g{g}_nb"), 1)

            pe.wait_ge(*at("g1_h", 3 * KT))
            attention_rows(1, 1)
            attention_rows(1, 2)
            for h in range(H1):
                hi, lo = XA[f"he_hi{h % 2}"], XA[f"he_lo{h % 2}"]
                attention_head(1, h, [(a, hi[:, :, a * P:(a + 1) * P], lo[:, :, a * P:(a + 1) * P]) for a in range(2)],
                               (lambda: attention_norm(1, h - 1, (h - 1) % 2)) if h else None)
            attention_norm(1, H1 - 1, (H1 - 1) % 2)

            pe.wait_ge(*at("g1_x", KT))
            pe.wait_ge(*at("g1_u", H1))
            pe.wait_ge(*at("g1_o", 3 * H1))
            for s in range(2):
                gemm(s, WBASE["W2"], X_hi, X_lo, s, mp=C2)
            for s in range(2):
                pe.wait_ge(*at(f"w2_y{s}", 1))
                transpose_tiles(t0[s], C2, s, "g2", 3 * s, s, s)
            pe.wait_ge(*at("g2_h", 3 * H2))
            attention_rows(2, 1)

            for t in range(NT):
                s = t % 2
                pe.wait_ge(*at(f"u_in{t % 4}", 16 * (t // 4 + 1)))
                if t >= 2:
                    pe.wait_ge(*at(f"u_ev{s}", t // 2))
                for m in range(KT):
                    last = nc.tensor.transpose(acc[s][:, m // 4, (m % 4) * P:(m % 4) * P + TP],
                                               XC[f"uxh{t % 4}"][:, m * P:(m + 1) * P], ident[0:TP, 0:TP])
                last.then_inc(sem(f"u_tr{s}"), 1)
            for s in range(2):
                pe.wait_ge(*at(f"u_ev{s}", NP))
                pe.wait_ge(*at(f"u_lo{s}", NP))

            def wut(a, b):
                with pe.Fori(a, b) as i:
                    for s in range(2):
                        pe.wait_ge(*at(f"wut_y{s}", i))
                        gemm(s, WBASE["WuT"] + i, X_hi, X_lo, s)

            wut(0, 2)
            attention_rows(2, 2)
            wut(2, 3)
            for h in range(H2):
                pe.wait_ge(*at(f"wut_y{h}", 3))
                hi, lo = XA["he_hi0"], XA["he_lo0"]
                attention_head(2, h, [(h, hi[:, :, h * P:(h + 1) * P], lo[:, :, h * P:(h + 1) * P])],
                               (lambda: attention_norm(2, h - 1, 2)) if h else None)
            attention_norm(2, H2 - 1, 2)

            pe.wait_ge(*at("g2_x", H2))
            with pe.Fori(0, 3) as i:
                for s in range(2):
                    pe.wait_ge(*at(f"wut_y{s}", 3))
                    pe.wait_ge(*at(f"wub_y{s}", i))
                    gemm(s, WBASE["WuB"] + i, XD["O2h"], XD["O2l"], s, kt=H2, kp=C2)

            to_features("m", [at("wub_y0", 3), at("wub_y1", 3)])
            for s in range(2):
                pe.wait_ge(*at(f"m_ev{s}", NP))
                pe.wait_ge(*at(f"m_lo{s}", NP))

            def tr_block(name, i, first, strict):
                pe.wait_ge(*at(f"kv_{name}", i + 1))
                for q, (a, b) in enumerate(((0, 4), (4, 8), (8, 10))):
                    pe.wait_ge(*at("kv_h", first + q - (0 if strict and q == 0 else 1)))
                    for t in range(a, b):
                        last = nc.tensor.transpose(aux[0:TP, q % 2, (t - a) * P:(t - a + 1) * P],
                                                   XD[name][:, t * TP:(t + 1) * TP], ident[:])
                    last.then_inc(sem("kv_tr"), 1)

            def kv_product(first):
                pe.wait_ge(*at("kv_h", first))
                for t in range(NT):
                    last = nc.tensor.matmul(aux[:, 1, 0:P + 2], XD["k_tok"][:, t, :], XD["v_tok"][:, t, :],
                                            start=(t == 0), stop=(t == NT - 1))
                last.then_inc(sem("kv_tr"), 1)

            gemm(0, WBASE["KV"], X_hi, X_lo, 0)
            gemm(1, WBASE["KV"], X_hi, X_lo, 1)
            tr_block("kT", 0, 0, True)
            with pe.Fori(1, KT) as i:
                g0 = 7 * i - 4
                pe.wait_ge(*at("kv_ka", i))
                gemm(0, WBASE["KV"] + i, X_hi, X_lo, 0)
                tr_block("vT", i - 1, g0, True)
                gemm(1, WBASE["KV"] + i, X_hi, X_lo, 1)
                kv_product(g0 + 3)
                tr_block("kT", i, g0 + 4, False)
            g0 = 7 * KT - 4
            tr_block("vT", KT - 1, g0, True)
            kv_product(g0 + 3)

            def q_gemm(m, s, k):
                pe.wait_ge(*at("q_a", m))
                gemm(s, k, X_hi, X_lo, 0)

            def blocks_product(mat, s):
                for n, (w, r) in enumerate(((f"m_h{s}", "q_hi"), (f"m_h{s}", "q_lo"), (f"m_l{s}", "q_hi"))):
                    for c in range(NCH):
                        last = nc.tensor.matmul(acc[1][:, c, 0:CH], XD[w][:, mat, :], XD[r][:, c * CH:(c + 1) * CH],
                                                start=(n == 0), stop=(n == 2))
                return last

            def q_apply(m, s):
                pe.wait_ge(*at("q_lo", m + 1))
                pe.wait_ge(*at("q_mat", m + 1))
                pe.wait_ge(*at("q_mul", m))
                blocks_product(1, s).then_inc(sem("q_den"), 1)
                pe.wait_ge(*at("q_dc", m + 1))
                blocks_product(0, s).then_inc(sem(f"q_num{s}"), 1)

            pe.wait_ge(*at("kv_ka", KT))
            pe.wait_ge(*at("kv_vT", KT))
            q_gemm(0, 0, WBASE["Q"])
            with pe.Fori(0, 2) as i:
                q_gemm(2 * i + 1, 1, WBASE["Q"] + i)
                q_apply(2 * i, 0)
                q_gemm(2 * i + 2, 0, WBASE["Q"] + i + 1)
                q_apply(2 * i + 1, 1)
            q_gemm(5, 1, WBASE["Q"] + 2)
            q_apply(4, 0)
            q_apply(5, 1)
            pe.wait_ge(*at("q_a", KT))
            with pe.Fori(0, 3) as i:
                for s in range(2):
                    if s:
                        pe.wait_ge(*at("q_mul", KT))
                    pe.wait_ge(*at(f"pj_y{s}", i))
                    gemm(s, WBASE["PROJ"] + i, H_hi, H_lo, s, ready=lambda kk: at("q_att", kk + 1))
            to_tokens("t1", [at("pj_y0", 3), at("pj_y1", 3)])
            to_features("l", [at("t1_add0", NP), at("t1_add1", NP)])

            def mlp(tag, wb, groups):
                with pe.Fori(0, groups) as g:
                    with pe.Fori(0, 3) as i:
                        for s in range(2):
                            pe.wait_ge(*at(f"{tag}_up{s}", 3 * g + i))
                            pe.wait_ge(*at(f"{tag}_dn{s}", 3 * g))
                            gemm(s, wb + 6 * g + i, X_hi, X_lo, s)
                    with pe.Fori(0, 3) as i:
                        for s in range(2):
                            pe.wait_ge(*at(f"{tag}_up{s}", 3 * g + 3))
                            pe.wait_ge(*at(f"{tag}_dn{s}", 3 * g + i))
                            gemm(s, wb + 6 * g + 3 + i, H_hi, H_lo, s,
                                 ready=lambda kk: at(f"{tag}_lo{kk % 2}", 3 * g + kk // 2 + 1))

            for s in range(2):
                pe.wait_ge(*at(f"l_ev{s}", NP))
                pe.wait_ge(*at(f"l_lo{s}", NP))
            mlp("ml", WBASE["MLP"], MLP_GROUPS)
            to_tokens("t2", [at(f"ml_dn{s}", 3 * MLP_GROUPS) for s in range(2)])
            for s in range(2):
                pe.wait_ge(*at(f"t2_add{s}", NP))
            for t in range(NT):
                s = t % 2
                pe.wait_ge(*at(f"x_xh{s}", t // 2 + 1))
                if t >= 2:
                    pe.wait_ge(*at(f"x_ev{s}", t // 2))
                for m in range(KT):
                    last = nc.tensor.matmul(aux[:, 1, t * KT + m:t * KT + m + 1], XC[f"xh{s}"][:, m * P:(m + 1) * P],
                                            V[0:TP, VC["one"]:VC["one"] + 1], start=True, stop=True)
                if t == NT - 1:
                    last.then_inc(sem("r_sum"), 1)
                for m in range(KT):
                    last = nc.tensor.transpose(acc[s][:, m // 4, (m % 4) * P:(m % 4) * P + TP],
                                               XC[f"xh{s}"][:, m * P:(m + 1) * P], ident[0:TP, 0:TP])
                last.then_inc(sem(f"x_tr{s}"), 1)
            pe.wait_ge(*at("r_pool", 1))
            for m in range(KT):
                o = VC["ffn_router_w"] + m
                last = nc.tensor.matmul(aux[0:1, 0, 0:EXP], pooled[:, m:m + 1], V[:, o:o + KT * (EXP - 1) + 1:KT],
                                        start=(m == 0), stop=(m == KT - 1))
            last.then_inc(sem("r_log"), 1)
            pe.wait_ge(*at("r_gates", 1))
            nc.tensor.matmul(aux[:, 0, 8:8 + TOPK], ones_row[:], rt[0:1, 20:20 + TOPK], start=True, stop=True).then_inc(sem("r_gb"), 1)
            for s in range(2):
                pe.wait_ge(*at(f"x_ev{s}", NP))
                pe.wait_ge(*at(f"x_lo{s}", NP))
            for e in range(TOPK):
                if e:
                    for s in range(2):
                        pe.wait_ge(*at(f"e{e - 1}_dn{s}", 3 * EXP_GROUPS))
                mlp(f"e{e}", WBASE["EXP"] + 6 * EXP_GROUPS * e, EXP_GROUPS)
            to_tokens("t3", [at(f"e{TOPK - 1}_dn{s}", 3 * EXP_GROUPS) for s in range(2)])

        @block.gpsimd
        def _(pool):
            ch = Chain(pool, sem("pool_chain"))
            for m in (ident, identb, tri, sel):
                nc.gpsimd.memset(m[:], 0.0).then_inc(sem("cz"), 1)
            nc.gpsimd.memset(bdiag[:], 1.0).then_inc(sem("cz"), 1)
            nc.gpsimd.memset(ones_row[:], 1.0)
            nc.gpsimd.memset(V[:, VC["one"]:VC["one"] + 1], 1.0)
            nc.gpsimd.memset(rt[:], -3e38)
            pool.wait_ge(*at("cz", 5))
            blocks = bdiag[:].rearrange("p (a n) -> p a n", n=HD)
            nc.gpsimd.affine_select(out=blocks, in_=blocks, compare_op=ALU.is_ge, fill=0.0, base=0,
                                    pattern=[[-HD, 2], [0, HD]], channel_multiplier=1).then_inc(sem("cz"), 1)
            pool.wait_ge(*at("cz", 6))
            nc.gpsimd.affine_select(out=blocks, in_=blocks, compare_op=ALU.is_ge, fill=0.0, base=HD - 1,
                                    pattern=[[HD, 2], [0, HD]], channel_multiplier=-1)
            for m, n in ((ident, P), (identb, TP)):
                nc.gpsimd.affine_select(out=m[:], in_=m[:], compare_op=ALU.not_equal, fill=1.0, base=0,
                                        pattern=[[-1, n]], channel_multiplier=1).then_inc(sem("cst"), 1)
            nc.gpsimd.affine_select(out=tri[:], in_=tri[:], compare_op=ALU.is_ge, fill=1.0, base=0,
                                    pattern=[[-1, NT]], channel_multiplier=1).then_inc(sem("cst"), 1)
            for k, row in enumerate((64, 0, 96)):
                nc.gpsimd.affine_select(out=sel[:, k, :], in_=sel[:, k, :], compare_op=ALU.not_equal, fill=1.0,
                                        base=-row, pattern=[[0, P]], channel_multiplier=1).then_inc(sem("sel"), 1)
            nc.gpsimd.iota(XA["iota"][:], pattern=[[1, NF]], base=0, channel_multiplier=0,
                           allow_small_or_imprecise_dtypes=True).then_inc(sem("c_const"), 1)
            nc.gpsimd.memset(XA["Z"][:], 0.0).then_inc(sem("cz"), 1)
            nc.gpsimd.memset(XA["D1z"][:], 0.0).then_inc(sem("c_const"), 1)
            pool.wait_ge(*at("cz", 7))
            nc.gpsimd.affine_select(out=XA["Z"][:, NF:NF + TP], in_=XA["Z"][:, NF:NF + TP], compare_op=ALU.not_equal,
                                    fill=1.0, base=0, pattern=[[-1, TP]], channel_multiplier=1).then_inc(sem("c_const"), 1)
            nc.gpsimd.iota(XA["ix"][:, 0, :], pattern=[[1, NEP]], base=1, channel_multiplier=0,
                           allow_small_or_imprecise_dtypes=True)
            nc.gpsimd.iota(XA["ix"][:, 1, :], pattern=[[-1, NEP]], base=NEP, channel_multiplier=0,
                           allow_small_or_imprecise_dtypes=True)
            nc.gpsimd.iota(XA["bc"][:, 6:7], pattern=[[0, 1]], base=0, channel_multiplier=TP,
                           allow_small_or_imprecise_dtypes=True)
            nc.gpsimd.iota(XA["bc"][:, 7:8], pattern=[[0, 1]], base=TP, channel_multiplier=TP,
                           allow_small_or_imprecise_dtypes=True).then_inc(sem("e_ix"), 1)

            with pool.Fori(0, NP) as i:
                for s in range(2):
                    pool.wait_ge(*at(f"c_sb{s}", i + 1))
                    pool.wait_ge(*at(f"madd_out{s}", 16 * i))
                    pool.sem_inc(sem("pool_go"), 1)
                    nc.gpsimd.tensor_scalar(XA[f"madds{s}"][:, 0:N], t0[s][0:TP, 0:N], 0.0, -BIG,
                                            ALU.is_equal, ALU.mult).then_inc(sem(f"c_madd{s}"), 1)

            def wsplit(s, k, kp=P, kt=KT, n=P):
                raw, hi, lo = (w[s][0:kp, 0:kt, 0:n] for w in (w_raw, w_hi, w_lo))
                pool.wait_ge(*at(f"w_in{s}", 16 * (k + 1)))
                pool.wait_ge(*at(f"w_done{s}", k))
                pool.sem_inc(sem("pool_go"), 1)
                nc.gpsimd.tensor_copy(hi, raw).then_inc(sem(f"w_hi{s}"), 1)
                pool.wait_ge(*at(f"w_hi{s}", k + 1))
                nc.gpsimd.tensor_tensor(lo, raw, hi.bitcast(fp32), ALU.subtract).then_inc(sem(f"w_split{s}"), 1)

            def wsplits(stage, pairs=(0, 3), **kw):
                with pool.Fori(*pairs) as i:
                    for s in range(2):
                        wsplit(s, WBASE[stage] + i, **kw)

            def x_pads(tag):
                nc.gpsimd.memset(X_hi[:, :, N:NF].bitcast(fp32), 0.0)
                nc.gpsimd.memset(X_lo[:, :, N:NF].bitcast(fp32), 0.0).then_inc(sem(f"{tag}_pad"), 1)

            def to_features(tag, k, frees, pads=False):
                for s_, v_ in frees:
                    pool.wait_ge(*at(s_, v_))
                if pads:
                    x_pads(tag)

                def xh(t):
                    s = t % 2
                    if t >= 2:
                        pool.wait_ge(*at(f"{tag}_tr{s}", t // 2))
                    nc.gpsimd.tensor_scalar(XC[f"xh{s}"][:], TOK[:, t, :], rs[:, k, t:t + 1], nm[:, k, t:t + 1],
                                            ALU.mult, ALU.add).then_inc(sem(f"{tag}_xh{s}"), 1)

                for t in range(NT):
                    xh(t)

            wsplits("W1", (0, 1))
            to_features("g", 0, [("lnb_rs", 2), ("c_acc0", NP), ("c_acc1", NP), ("c_tc", 3 * NT), ("c_madd0", NP), ("c_madd1", NP),
                                 ("madd_out0", 16 * NP), ("madd_out1", 16 * NP), ("ct_out0", 16 * NP), ("ct_out1", 16 * NP)], pads=True)
            wsplits("W1", (1, 3))

            def attention(g, H, C):
                stage = "W1" if g == 1 else "WuT"
                for s in range(2):
                    pool.wait_ge(*at(f"w_done{s}", WBASE[stage] + 3))
                if g == 1:
                    nc.gpsimd.memset(XA["he_raw0"][:, :, C:2 * P], 1.0)
                    last = nc.gpsimd.memset(XA["he_raw1"][:, :, 0:2 * P - C], 1.0)
                else:
                    nc.gpsimd.memset(XA["he_raw0"][:, :, C:P], 1.0)
                    last = nc.gpsimd.memset(XA["he_raw0"][:, :, P + C:2 * P], 1.0)
                last.then_inc(sem(f"g{g}_ones"), 1)
                pool.wait_ge(*at(f"g{g}_ones", 1))

                def split(h):
                    ps = h % 2 if g == 1 else 0
                    pool.wait_ge(*at(f"g{g}_hh", h + 1))
                    nc.gpsimd.tensor_tensor(XA[f"he_lo{ps}"][:], XA[f"he_raw{ps}"][:], XA[f"he_hi{ps}"][:].bitcast(fp32),
                                            ALU.subtract).then_inc(sem(f"g{g}_hs"), 1)

                def lows(h, a, b):
                    with pool.Fori(a, b) as i:
                        for s in range(2):
                            pool.wait_ge(*at(f"g{g}_ph{s}", NP * h + i + 1))
                            nc.gpsimd.tensor_tensor(XC[f"Pl{s}"][:, 0:N], XD[f"pp{s}"][:], XC[f"Ph{s}"][:, 0:N].bitcast(fp32),
                                                    ALU.subtract).then_inc(sem(f"g{g}_lo{s}"), 1)

                split(0)
                pool.wait_ge(*at(f"g{g}_r_out", 32))
                pool.wait_ge(*at(f"g{g}_h_out", 16))
                for s in range(2):
                    for k in ("Ph", "Pl"):
                        nc.gpsimd.memset(XC[f"{k}{s}"][:, N:NF].bitcast(fp32), 0.0)
                nc.gpsimd.memset(XC["R"][:], 0.0).then_inc(sem(f"g{g}_R0"), 1)
                for h in range(H):
                    lows(h, 0, 3)
                    if h + 1 < H and g == 1:
                        split(h + 1)
                    lows(h, 3, NP)

            attention(1, H1, C1)
            for s in range(2):
                wsplit(s, WBASE["W2"], n=C2)
            for s in range(2):
                pool.wait_ge(*at(f"w_done{s}", WBASE["W2"] + 1))
            x_pads("u")
            wsplits("WuT")
            attention(2, H2, C2)
            wsplits("WuB", kp=C2, kt=H2)
            wsplits("KV", (0, 1))
            to_features("m", 1, [("m_tok", 16 * NT)], pads=True)
            pool.wait_ge(*at("wub_y0", 3))
            pool.wait_ge(*at("wub_y1", 3))
            nc.gpsimd.memset(XD["v_tok"][:, :, P:P + 2], 1.0).then_inc(sem("kv_ones"), 1)
            wsplits("KV", (1, KT))
            pool.wait_ge(*at("kv_h", 7 * KT))
            with pool.Fori(0, 3) as i:
                for s in range(2):
                    m = 2 * i + s
                    wsplit(s, WBASE["Q"] + i)
                    pool.wait_ge(*at(f"q_num{s}", i))
                    pool.wait_ge(*at("q_mat", m))
                    nc.gpsimd.tensor_tensor(XD["kvf"][:, 0, :], KVf[:, ds(m, 1), 0:P].rearrange("p a n -> p (a n)"), bdiag[:], ALU.mult)
                    nc.gpsimd.tensor_tensor(XD["kvf"][:, 1, :], KVf[:, ds(m, 1), P:P + 1].rearrange("p a n -> p (a n)").broadcast_to([P, P]),
                                            bdiag[:], ALU.mult).then_inc(sem("q_mf"), 1)
                    pool.wait_ge(*at("q_mf", m + 1))
                    pool.sem_inc(sem("pool_go"), 1)
                    nc.gpsimd.tensor_copy(XD[f"m_h{s}"][:], XD["kvf"][:]).then_inc(sem("q_mh"), 1)
                    pool.wait_ge(*at("q_mh", m + 1))
                    nc.gpsimd.tensor_tensor(XD[f"m_l{s}"][:], XD["kvf"][:], XD[f"m_h{s}"][:].bitcast(fp32), ALU.subtract).then_inc(sem("q_mat"), 1)
            wsplits("PROJ")
            wsplits("MLP", (0, 1))
            to_features("l", 0, [("lnl_rs", 1)])
            wsplits("MLP", (1, 6 * MLP_GROUPS))
            for t in range(NT):
                pool.wait_ge(*at(f"t2_ad{t % 4}", 32 * (t // 4 + 1)))
                aa = XC[f"aa{t % 4}"]
                nc.gpsimd.tensor_tensor(aa[:, 0, :], aa[:, 0, :], aa[:, 1, :], ALU.add).then_inc(sem(f"t2_aa{t % 2}"), 1)
            to_features("x", 0, [("lnx_rs", 1)])
            wsplits("EXP", (0, 6 * EXP_GROUPS * TOPK))
            pool.wait_ge(*at("gb_in", 48))
            with pool.Fori(0, NT) as i:
                nc.gpsimd.tensor_tensor(XA["X2"][:, ds(i, 1), :], XA["X2"][:, ds(i, 1), :], XA["gb"][:, 1:2, :], ALU.add).then_inc(sem("f_x2"), 1)

        @block.scalar
        def _(act):
            A_ = nc.scalar.activation

            def ln_root(tag, n):
                act.wait_ge(*at(f"{tag}_ve", n))
                A_(ve[:, 0:n, :], ve[:, 0:n, :], ACT.Sqrt).then_inc(sem(f"{tag}_sd"), 1)

            for name in LOOPED[1::2]:
                act.sem_inc(sem(name), 1)
            act.wait_ge(*at("v_tr", 1))
            A_(V[:, 0:NV1], aux[:, 0, 0:NV1], ACT.Copy)
            A_(V[:, NV1:NV1 + NV2], aux[:, 0, P:P + NV2], ACT.Copy)
            A_(V[0:C2, VC["gnn_b2"]:VC["gnn_b2"] + 2], aux[0:C2, 0, 2 * P:2 * P + 2], ACT.Copy).then_inc(sem("v_cp"), 1)

            with act.Fori(0, NP) as i:
                for s in range(2):
                    act.wait_ge(*at(f"c_acc{s}", i + 1))
                    act.wait_ge(*at(f"c_madd{s}", i))
                    A_(f3(t0[s][0:TP, :]), accf(s, TP), ACT.Copy).then_inc(sem(f"c_sb{s}"), 1)
                for s in range(2):
                    for q, (a, b) in enumerate(((0, 4), (4, 8), (8, 10))):
                        act.wait_ge(*at("c_tr", 6 * i + 3 * s + q + 1))
                        if q == 0:
                            act.wait_ge(*at(f"ct_out{s}", 16 * i))
                        A_(XA[f"ctb{s}"][:, a:b, :],
                           aux[0:TP, (3 * s + q) % 2, 0:(b - a) * P].rearrange("p (j n) -> p j n", n=P)[:, :, 0:TP],
                           ACT.Copy).then_inc(sem("c_tc"), 1)

            ln_root("lna", 1)
            act.wait_ge(*at("lna_rs", 1))
            with act.Fori(0, NT) as i:
                A_(TOK[:, ds(i, 1), :], TOK[:, ds(i, 1), :], ACT.Identity, scale=rs[:, 0, ds(i, 1)],
                   bias=nm[:, 0, ds(i, 1)]).then_inc(sem("ln0_xn"), 1)
            ln_root("lnb", 2)

            def to_features(tag, g, b):
                with act.Fori(0, NP) as i:
                    for s in range(2):
                        act.wait_ge(*at(f"{tag}_tr{s}", i + 1))
                        act.wait_ge(*at(f"{tag}_lo{s}", i))
                        for m in range(KT):
                            last = A_(XC[f"ft{s}"][:, m, :], acc[s][:, m // 4, (m % 4) * P:(m % 4) * P + TP],
                                      ACT.Identity, scale=vcol(g, m), bias=vcol(b, m))
                        last.then_inc(sem(f"{tag}_ev{s}"), 1)

            def to_features_plain(tag, dest):
                with act.Fori(0, NP) as i:
                    for s in range(2):
                        act.wait_ge(*at(f"{tag}_tr{s}", i + 1))
                        if tag == "u":
                            act.wait_ge(*at("u_lo%d" % s, i))
                        for bank, (a, b) in enumerate(((0, 4), (4, 6))):
                            last = A_(dest(s, 2 * i + s, slice(a, b)),
                                      acc[s][:, bank, 0:(b - a) * P].rearrange("p (m n) -> p m n", n=P)[:, :, 0:TP], ACT.Copy)
                        last.then_inc(sem(f"{tag}_ev{s}"), 1)

            to_features("g", "gnn_norm_g", "gnn_norm_b")
            with act.Fori(0, 3) as i:
                for s in range(2):
                    act.wait_ge(*at(f"w_done{s}", WBASE["W1"] + i + 1))
                    act.wait_ge(*at("g1_h", 6 * i))
                    A_(f3(t0[s][:]), accf(s), ACT.Copy).then_inc(sem(f"w1_y{s}"), 1)

            def attention_row(g, n):
                act.wait_ge(*at(f"g{g}_S_tr", n))
                if n == 2:
                    act.wait_ge(*at(f"g{g}_r_out", 16))
                A_(XC["srow" if g == 1 else "srow2"][:], aux[0:80, 0, 0:TP], ACT.Copy).then_inc(sem(f"g{g}_srow"), 1)

            def blocks_out(stage, ysem, bias, frees=(), pairs=(0, 3)):
                for s_, v_ in frees:
                    act.wait_ge(*at(s_, v_))
                with act.Fori(*pairs) as i:
                    for s in range(2):
                        act.wait_ge(*at(f"w_done{s}", WBASE[stage] + i + 1))
                        A_(Y[:, ds(2 * i + s, 1), :].rearrange("p a (c n) -> p (a c) n", c=NCH), accf(s), ACT.Identity,
                           bias=vcol(bias, 2 * i + s)).then_inc(sem(f"{ysem}{s}"), 1)

            def attention(g, H):
                def high(h):
                    ps = h % 2 if g == 1 else 0
                    act.wait_ge(*at(f"g{g}_ones", 1))
                    act.wait_ge(*at(f"g{g}_he{ps}", 16 * (h // 2 + 1) if g == 1 else 32))
                    A_(XA[f"he_hi{ps}"][:], XA[f"he_raw{ps}"][:], ACT.Copy).then_inc(sem(f"g{g}_hh"), 1)

                def weights(h, i):
                    n = i + NP * h
                    for s in range(2):
                        act.wait_ge(*at(f"g{g}_a{s}", n + 1))
                        act.wait_ge(*at(f"g{g}_p{s}", n))
                        A_(t0[s][0:TP, 0:N], XD[f"e2_{s}"][:], ACT.Exp,
                           bias=S2[:, ds(2 * i + s, 1), h:h + 1].rearrange("p a b -> p (a b)")).then_inc(sem(f"g{g}_e{s}"), 1)
                    for s in range(2):
                        act.wait_ge(*at(f"g{g}_p{s}", n + 1))
                        act.wait_ge(*at(f"g{g}_pu{s}", n))
                        A_(XC[f"Ph{s}"][:, 0:N], XD[f"pp{s}"][:], ACT.Copy).then_inc(sem(f"g{g}_ph{s}"), 1)

                def sums(h):
                    for s in range(2):
                        act.wait_ge(*at(f"g{g}_pu{s}", NP * (h + 1)))
                    if h:
                        act.wait_ge(*at(f"g{g}_o", 3 * h))
                    if g == 1:
                        A_(f3(XC["U0"][:]), accf(0), ACT.Copy)
                        A_(f3(XC["U1"][:]), accf(1), ACT.Copy).then_inc(sem("g1_u"), 1)
                    else:
                        A_(f3(XC[f"U{h}"][:]), accf(h), ACT.Copy).then_inc(sem("g2_u"), 1)

                high(0)
                if g == 1:
                    attention_row(1, 2)
                for h in range(H):
                    with act.Fori(0, 1) as i:
                        weights(h, i)
                    if h:
                        sums(h - 1)
                    if h + 1 < H and g == 1:
                        high(h + 1)
                    with act.Fori(1, NP) as i:
                        weights(h, i)
                sums(H - 1)

            attention_row(1, 1)
            attention(1, H1)
            act.wait_ge(*at("g1_o", 3 * H1))
            for m in range(KT):
                A_(X_hi[:, m, :], Y[:, m, :], ACT.Identity, bias=vcol("gnn_b1", m)).then_inc(sem("g1_xh"), 1)
            for s in range(2):
                act.wait_ge(*at(f"w_done{s}", WBASE["W2"] + 1))
                A_(f3(t0[s][0:C2, :]), accf(s, C2), ACT.Copy).then_inc(sem(f"w2_y{s}"), 1)
            attention_row(2, 1)
            to_features_plain("u", lambda s, t, m: XC[f"uft{s}"][:, m, :])
            blocks_out("WuT", "wut_y", "gnn_bu", [("g1_x", KT)], (0, 2))
            attention_row(2, 2)
            blocks_out("WuT", "wut_y", "gnn_bu", (), (2, 3))
            attention(2, H2)
            act.wait_ge(*at("g2_o", 3 * H2))
            for h in range(H2):
                A_(XD["O2h"][:, h, :], XC[f"U{h}"][0:C2, :], ACT.Identity, bias=vcol("gnn_b2", h, C2)).then_inc(sem("g2_xh"), 1)

            to_features("m", "mix_ln1_w", "mix_ln1_b")

            def elu_parts(m, s, done, k, ready, bias):
                act.wait_ge(*at(f"w_done{s}", k))
                act.wait_ge(*at(done, m))
                A_(f3(t0[0][:]), accf(0), ACT.Exp, bias=vcol("mix_qkv_b", bias))
                A_(f3(t0[1][:]), accf(0), ACT.Relu, bias=vcol("mix_qkv_b", bias)).then_inc(sem(ready), 1)

            with act.Fori(0, KT) as i:
                elu_parts(i, 0, "kv_kT", WBASE["KV"] + i + 1, "kv_ka", i + KT)

            def q_part(m, s, k):
                elu_parts(m, s, "q_lo", k, "q_a", m)

            def denominator(m):
                act.wait_ge(*at("q_den", m + 1))
                act.wait_ge(*at("q_att", m))
                A_(f3(XD["rden"][:]), accf(1), ACT.Copy).then_inc(sem("q_dc"), 1)

            q_part(0, 0, WBASE["Q"] + 1)
            with act.Fori(0, 2) as i:
                q_part(2 * i + 1, 1, WBASE["Q"] + i + 1)
                denominator(2 * i)
                q_part(2 * i + 2, 0, WBASE["Q"] + i + 2)
                denominator(2 * i + 1)
            q_part(5, 1, WBASE["Q"] + 3)
            denominator(4)
            denominator(5)
            blocks_out("PROJ", "pj_y", "mix_proj_b", [("gnn_out", 16)])
            ln_root("lnl", 1)
            to_features("l", "mix_ln2_w", "mix_ln2_b")

            def up(tag, wb, groups, func, bias):
                with act.Fori(0, groups) as g:
                    with act.Fori(0, 3) as i:
                        for s in range(2):
                            act.wait_ge(*at(f"w_done{s}", wb + 6 * g + i + 1))
                            act.wait_ge(*at(f"{tag}_lo{s}", 3 * g + i))
                            last = A_(f3(t0[s][:]), accf(s), ACT.Identity if func == "mish" else func, bias=bias(6 * g + 2 * i + s))
                            if func == "mish":
                                last = A_(f3(XD[f"m{1 + s}"][:]), accf(s), ACT.Exp, bias=bias(6 * g + 2 * i + s))
                            last.then_inc(sem(f"{tag}_up{s}"), 1)

            up("ml", WBASE["MLP"], MLP_GROUPS, ACT.Gelu, lambda m: vcol("mix_fc1_b", m))
            ln_root("lnx", 1)
            to_features_plain("x", lambda s, t, m: Y[:, m, ds(t * TP, TP)])
            act.wait_ge(*at("r_d", 1))
            A_(rt[0:1, 17:18], rt[0:1, 16:17], ACT.Exp).then_inc(sem("r_e"), 1)
            act.wait_ge(*at("r_idx", 1))
            for e in range(TOPK):
                er = act.value_load(rti[0:1, e:e + 1], min_val=0, max_val=EXP - 1)
                args = (f"e{e}", WBASE["EXP"] + 6 * EXP_GROUPS * e, EXP_GROUPS)
                bias = lambda m: vcol("ffn_b1", er * (2 * KT) + m)
                with act.If(er == 2):
                    up(*args, "mish", bias)
                with act.Else():
                    with act.If(er == 1):
                        up(*args, ACT.Silu, bias)
                    with act.Else():
                        up(*args, ACT.Gelu, bias)
            ln_root("lnf", 1)
            act.wait_ge(*at("lnf_rs", 1))
            with act.Fori(0, NP) as i:
                for s in range(2):
                    tok = TOK[:, ds(2 * i + s, 1), :].rearrange("p a n -> p (a n)")
                    A_(tok, tok, ACT.Identity,
                       scale=rs[:, 0, ds(2 * i + s, 1)], bias=nm[:, 0, ds(2 * i + s, 1)]).then_inc(sem(f"f_n{s}"), 1)

        @block.vector
        def _(dve):
            v = nc.vector
            ch = Chain(dve, sem("dve_chain"))
            GROUPS = ((0, 4), (4, 8), (8, 10))

            ef, bb, bc, ix = XA["ef"], XA["bb"], XA["bc"], XA["ix"]
            dve.wait_ge(*at("e_in", 32))
            for k in range(2):
                v.tensor_copy(ef[:, k, :], XA["ei"][:, k, :]).then_inc(sem("e_f"), 1)
            dve.wait_ge(*at("e_f", 2))
            v.tensor_reduce(XA["cm2"][:, 0:1], ef[:, 1, :], AX.X, ALU.min)
            ch.link(v.tensor_reduce(XA["cm2"][:, 1:2], ef[:, 1, :], AX.X, ALU.max))
            for k in range(2):
                v.tensor_copy(XA["cmm"][:, k, :], XA["cm2"][:, k:k + 1].broadcast_to([NEP, NT])).then_inc(sem("e_cmm"), 1)
            dve.wait_ge(*at("e_tr", 1))
            v.tensor_copy(XA["ec"][:, 0:4 * NEP], aux[0:TP, 1, 0:4 * NEP]).then_inc(sem("e_ec"), 1)
            dve.wait_ge(*at("e_bb", 1))
            dve.wait_ge(*at("e_ix", 1))
            ch.link(v.tensor_scalar(bb[:, 0, :], aux[0:NT, 0, 0:NEP], bc[:, 7:8], None, ALU.is_lt))
            ch.link(v.scalar_tensor_tensor(out=bb[:, 1, :], in0=aux[0:NT, 0, P:P + NEP], scalar=bc[:, 6:7],
                                           in1=bb[:, 0, :], op0=ALU.is_ge, op1=ALU.mult))
            v.tensor_tensor(bb[:, 2, :], bb[:, 1, :], ix[:, 0, :], ALU.mult)
            ch.link(v.tensor_tensor(bb[:, 3, :], bb[:, 1, :], ix[:, 1, :], ALU.mult))
            v.tensor_reduce(bc[:, 4:5], bb[:, 2, :], AX.X, ALU.max)
            ch.link(v.tensor_reduce(bc[:, 3:4], bb[:, 3, :], AX.X, ALU.max))
            ch.link(v.tensor_scalar(bc[:, 5:6], bc[:, 3:4], -1.0, float(NEP), ALU.mult, ALU.add))
            ch.link(v.tensor_scalar(bc[:, 0:1], bc[:, 5:6], float(NEP - 1), None, ALU.min))
            ch.link(v.scalar_tensor_tensor(out=bc[:, 1:2], in0=bc[:, 0:1], scalar=1.0, in1=bc[:, 4:5],
                                           op0=ALU.add, op1=ALU.max))
            v.tensor_tensor(bc[:, 2:3], bc[:, 1:2], bc[:, 0:1], ALU.subtract).then_inc(sem("e_bc"), 1)
            dve.wait_ge(*at("e_row", 1))
            v.tensor_copy(bnd[:].rearrange("p (a b) -> p a b", b=NT),
                          aux[0:1, 1, 0:48].rearrange("p (a b) -> p a b", b=16)[:, :, 0:NT]).then_inc(sem("bnd"), 1)

            def tile_stats(tag, t):
                for k in range(2):
                    last = v.bn_stats(st[:, ds(t, 1), k, :].rearrange("p a b -> p (a b)"),
                                      TOK[:, ds(t, 1), k * (D // 2):(k + 1) * (D // 2)].rearrange("p a b -> p (a b)"))
                last.then_inc(sem(f"{tag}_st"), 1)

            def ln_terms(tag, eps):
                dve.wait_ge(*at(f"{tag}_st", NT))
                for i in range(NT):
                    v.bn_aggr(mv[:, i, :], st[:, i, :, :].rearrange("p k b -> p (k b)")).then_inc(sem(f"{tag}_ag"), 1)
                dve.wait_ge(*at(f"{tag}_ag", NT))
                for k, e in enumerate(eps):
                    v.tensor_scalar(ve[:, k, :], mv[:, :, 1], e, None, ALU.add).then_inc(sem(f"{tag}_ve"), 1)
                dve.wait_ge(*at(f"{tag}_sd", 1))
                ch.link(v.reciprocal(rs[:, 0:len(eps), :], ve[:, 0:len(eps), :]))
                for k in range(len(eps)):
                    v.scalar_tensor_tensor(out=nm[:, k, :], in0=mv[:, :, 0], scalar=-1.0, in1=rs[:, k, :],
                                           op0=ALU.mult, op1=ALU.mult).then_inc(sem(f"{tag}_rs"), 1)

            dve.wait_ge(*at("bnd", 1))
            dve.wait_ge(*at("e_ec", 1))
            dve.wait_ge(*at("c_const", 3))
            with dve.Fori(0, NT) as t:
                p0 = dve.value_load(bnd[0:1, ds(t, 1)], min_val=0, max_val=NEP - 1)
                pairs = dve.value_load(bnd[0:1, ds(t + NT, 1)], min_val=1, max_val=NEP)
                before = dve.value_load(bnd[0:1, ds(t + 2 * NT, 1)], min_val=0, max_val=NEP * NT)
                with dve.Fori(0, pairs) as p:
                    q = (p + before) & 1
                    for h in range(2):
                        D1, S1 = (XA[f"{k}{h}"][:, ds(q, 1), :].rearrange("p a n -> p (a n)") for k in ("D1h", "S1h"))
                        dve.wait_ge(*at(f"oh_used{h}", p + before))
                        v.tensor_scalar(D1, XA["iota"][:, ds(t * TP, TP)], XA["ec"][:, ds(p + p0 + (2 + h) * NEP, 1)],
                                        None, ALU.is_equal)
                        v.tensor_scalar(S1, XA["iota"][:], XA["ec"][:, ds(p + p0 + h * NEP, 1)],
                                        None, ALU.is_equal).then_inc(sem(f"oh{h}"), 1)

            dve.wait_ge(*at("x_in", 16 * NT))
            with dve.Fori(0, NT) as i:
                tile_stats("lna", i)
            ln_terms("lna", (1e-5,))
            with dve.Fori(0, NT) as i:
                dve.wait_ge(*at("ln0_xn", i + 1))
                tile_stats("lnb", i)
            ln_terms("lnb", (1e-5, 1e-8))

            def split_tiles(tag, frees=()):
                for s_, v_ in frees:
                    dve.wait_ge(*at(s_, v_))
                with dve.Fori(0, NP) as i:
                    for s in range(2):
                        t = 2 * i + s
                        dve.wait_ge(*at(f"{tag}_ev{s}", i + 1))
                        if tag == "x":
                            ft = Y[:, :, ds(t * TP, TP)]
                        else:
                            ft = XC[("uft" if tag == "u" else "ft") + str(s)][:]
                        v.tensor_copy(X_hi[:, :, ds(t * TP, TP)], ft).then_inc(sem(f"{tag}_hi{s}"), 1)
                        dve.wait_ge(*at(f"{tag}_hi{s}", i + 1))
                        v.tensor_tensor(X_lo[:, :, ds(t * TP, TP)], ft, X_hi[:, :, ds(t * TP, TP)].bitcast(fp32),
                                        ALU.subtract).then_inc(sem(f"{tag}_lo{s}"), 1)

            split_tiles("g", [("g_pad", 1)])

            def head_terms(g, H, C, width, blocks):
                HT, ab, pr = (XC[k + ("2" if g == 2 else "")] for k in ("HT", "ab", "pr"))

                def group(m, col, first, bank0):
                    for q, (a, b) in enumerate(GROUPS):
                        dve.wait_ge(*at(f"g{g}_tr", first + q + 1))
                        v.tensor_copy(HT[:, a:b, ds(col, width)],
                                      aux[0:TP, (bank0 + q) % 2, 0:(b - a) * P].rearrange("p (t n) -> p t n", n=P)[:, :, 0:width]
                                      ).then_inc(sem(f"g{g}_h"), 1)

                def groups(a, b):
                    with dve.Fori(a, b) as i:
                        for s in range(2):
                            group(2 * i + s, (2 * i + s) * width, 6 * i + 3 * s, s)
                    dve.wait_ge(*at(f"g{g}_h", 6 * b))

                def terms(heads, before):
                    with dve.Fori(0, NT) as i:
                        dve.wait_ge(*at(f"g{g}_s", i + before))
                        for k in range(2):
                            for h in heads:
                                last = v.scalar_tensor_tensor(
                                    out=pr[:, H * k + h, 0:C], in0=HT[:, ds(i, 1), h * C:(h + 1) * C].rearrange("p a n -> p (a n)"),
                                    scalar=1.0, in1=ab[:, k, h * C:(h + 1) * C], op0=ALU.mult, op1=ALU.mult,
                                    accum_out=S[:, ds(i, 1), 4 * k + h:4 * k + h + 1].rearrange("p a n -> p (a n)"))
                        last.then_inc(sem(f"g{g}_s"), 1)

                if g == 1:
                    dve.wait_ge(*at("xn_out", 16))
                    groups(0, 2)
                    dve.wait_ge(*at("g1_ab", 32))
                    terms((0, 1), 0)
                    groups(2, 3)
                    terms((2, 3), NT)
                    dve.wait_ge(*at("g1_s", 2 * NT))
                else:
                    groups(0, 1)
                    dve.wait_ge(*at("g2_ab", 32))
                    terms((0, 1), 0)
                    dve.wait_ge(*at("g2_s", NT))
                v.tensor_scalar(S2[:], S[:], NEG, None, ALU.mult).then_inc(sem(f"g{g}_S"), 1)

            def maxima(g, H):
                if g == 2:
                    dve.wait_ge(*at("g2_mad0", 16))
                dve.wait_ge(*at(f"g{g}_ssb", 16 * H))

                def tile_maxima(i, s, mask, trash):
                    dve.wait_ge(*at(f"g{g}_mu{s}", i))
                    dve.sem_inc(sem("dve_go"), 1)
                    for h in range(H):
                        last = v.tensor_tensor_reduce(out=trash[:, h, :], in0=XD["ssb"][:, h, :], in1=mask,
                                                      scale=1.0, scalar=-3e38, op0=ALU.add, op1=ALU.max,
                                                      accum_out=mus[:, s, h:h + 1])
                    last.then_inc(sem(f"g{g}_mx{s}"), 1)
                    dve.wait_ge(*at(f"g{g}_mx{s}", i + 1))
                    v.tensor_copy(MU[:, ds(2 * i + s, 1), 0:H].rearrange("p a h -> p (a h)"),
                                  mus[:, s, 0:H]).then_inc(sem(f"g{g}_mu{s}"), 1)

                if g == 1:
                    with dve.Fori(0, NP) as i:
                        for s in range(2):
                            dve.wait_ge(*at(f"g{g}_mad{s}", 16 * (i + 1)))
                            tile_maxima(i, s, XC[f"mad{s}"][:], XC["trash"])
                else:
                    for t in range(NT):
                        tile_maxima(t // 2, t % 2, XC["mads2"][:, t, :], XC["trash2"])
                for s in range(2):
                    dve.wait_ge(*at(f"g{g}_mu{s}", NP))
                dst, dst2 = S[:, :, 4:4 + H], S2[:, :, 4:4 + H]
                dve.wait_ge(*at(f"g{g}_S", 1))
                v.tensor_tensor(Sd[:], S[:], S2[:], ALU.subtract)
                ch.link(v.tensor_tensor(Dc[:, :, 0:H], MU[:, :, 0:H], dst, ALU.add))
                ch.link(v.scalar_tensor_tensor(out=MU[:, :, 0:H], in0=Dc[:, :, 0:H], scalar=NEG, in1=Dc[:, :, 0:H],
                                               op0=ALU.mult, op1=ALU.max))
                v.tensor_tensor(Dc[:, :, 0:H], dst, MU[:, :, 0:H], ALU.subtract)
                v.tensor_tensor(Dc[:, :, 4:4 + H], dst2, MU[:, :, 0:H], ALU.subtract).then_inc(sem(f"g{g}_S"), 1)

            def head_weights(g, H):
                dve.wait_ge(*at(f"g{g}_R0", 1))
                dve.wait_ge(*at(f"g{g}_S", 2))
                R = XC["R"]

                def weights(h, a, b):
                    with dve.Fori(a, b) as i:
                        n = i + NP * h
                        for s in range(2):
                            dve.wait_ge(*at(f"g{g}_e{s}", n))
                            v.scalar_tensor_tensor(out=XD[f"e2_{s}"][:], in0=XC[f"Db{h % 2}"][:, 0, :],
                                                   scalar=Sd[:, ds(2 * i + s, 1), h:h + 1].rearrange("p a b -> p (a b)"),
                                                   in1=XC[f"Db{h % 2}"][:, 1, :], op0=ALU.add, op1=ALU.max).then_inc(sem(f"g{g}_a{s}"), 1)
                        for s in range(2):
                            dve.wait_ge(*at(f"g{g}_e{s}", n + 1))
                            dve.wait_ge(*at(f"g{g}_ct{s}", 16 * n + 16))
                            dve.wait_ge(*at(f"g{g}_lo{s}", n))
                            v.scalar_tensor_tensor(out=XD[f"pp{s}"][:], in0=t0[s][0:TP, 0:N], scalar=1.0, in1=XC[f"CT{s}"][:],
                                                   op0=ALU.min, op1=ALU.mult).then_inc(sem(f"g{g}_p{s}"), 1)

                def norm(h):
                    dve.wait_ge(*at(f"g{g}_u", h + 1))
                    if g == 1:
                        rows, U = (slice(64, 128), "U1") if h % 2 == 0 else (slice(0, 64), "U0")
                        b = 3 * (h // 2)
                        parts = [(slice(0, 128), "U0", b), (slice(0, 64), "U1", b + 1)] if h % 2 == 0 else \
                                [(slice(64, 128), "U0", b + 1), (slice(0, 128), "U1", b + 2)]
                    else:
                        rows, U = slice(96, 128), f"U{h}"
                        parts = [(slice(0, 96), f"U{h}", h)]
                    if h:
                        dve.wait_ge(*at(f"g{g}_nb", 3 * h))
                    v.reciprocal(R[rows, 0:N], XC[U][rows, 0:N]).then_inc(sem(f"g{g}_R"), 1)
                    for c in range(NCH):
                        cs = slice(c * CH, (c + 1) * CH)
                        dve.wait_ge(*at(f"g{g}_nb", 3 * h + c + 1))
                        for r, u, blk in parts:
                            out_ = Y[r, blk, cs] if g == 1 else XC[u][r, cs]
                            last = v.tensor_tensor(out_, XC[u][r, cs], aux[r, c % 2, 0:CH], ALU.mult)
                        last.then_inc(sem(f"g{g}_o"), 1)

                for h in range(H):
                    dve.wait_ge(*at(f"g{g}_db{h % 2}", 32 * (h // 2 + 1)))
                    weights(h, 0, 2)
                    if h:
                        norm(h - 1)
                    weights(h, 2, NP)
                norm(H - 1)

            head_terms(1, H1, C1, P, KT)
            maxima(1, H1)
            head_weights(1, H1)
            for m in range(KT):
                dve.wait_ge(*at("g1_xh", m + 1))
                v.scalar_tensor_tensor(out=X_lo[:, m, :], in0=Y[:, m, :], scalar=vcol("gnn_b1", m), in1=X_hi[:, m, :].bitcast(fp32),
                                       op0=ALU.add, op1=ALU.subtract).then_inc(sem("g1_x"), 1)
            head_terms(2, H2, C2, C2, 2)
            split_tiles("u", [("u_pad", 1)])
            maxima(2, H2)
            head_weights(2, H2)
            for h in range(H2):
                dve.wait_ge(*at("g2_xh", h + 1))
                v.scalar_tensor_tensor(out=XD["O2l"][:, h, :], in0=XC[f"U{h}"][0:C2, :], scalar=vcol("gnn_b2", h, C2),
                                       in1=XD["O2h"][:, h, :].bitcast(fp32), op0=ALU.add, op1=ALU.subtract).then_inc(sem("g2_x"), 1)

            def yblock(m):
                return Y[:, ds(m, 1), :].rearrange("p a (c n) -> p (a c) n", c=NCH)

            with dve.Fori(0, 3) as i:
                for s in range(2):
                    dve.wait_ge(*at(f"w_done{s}", WBASE["WuB"] + i + 1))
                    dve.wait_ge(*at(f"wut_y{s}", 3))
                    v.scalar_tensor_tensor(out=yblock(2 * i + s), in0=accf(s), scalar=vcol("mix_fc2_b", 2 * i + s), in1=yblock(2 * i + s),
                                           op0=ALU.add, op1=ALU.add).then_inc(sem(f"wub_y{s}"), 1)
            split_tiles("m", [("m_pad", 1)])

            def kT_part(m, tr):
                dve.wait_ge(*at("kv_ka", m + 1))
                if tr is not None:
                    dve.wait_ge(*at("kv_tr", tr))
                v.scalar_tensor_tensor(out=XD["kT"][:], in0=t0[0][:], scalar=1.0, in1=t0[1][:],
                                       op0=ALU.min, op1=ALU.add).then_inc(sem("kv_kT"), 1)

            def vT_part(m, tr):
                dve.wait_ge(*at("w_done1", WBASE["KV"] + 1 + m))
                if tr is not None:
                    dve.wait_ge(*at("kv_tr", tr))
                v.tensor_scalar(f3(XD["vT"][:]), accf(1), vcol("mix_qkv_b", m + 2 * KT), None, ALU.add).then_inc(sem("kv_vT"), 1)

            def tok_part(name, first):
                for q, (a, b) in enumerate(GROUPS):
                    dve.wait_ge(*at("kv_tr", first + q + 1))
                    v.tensor_copy(XD[name][:, a:b, 0:P],
                                  aux[0:TP, q % 2, 0:(b - a) * P].rearrange("p (t n) -> p t n", n=P)).then_inc(sem("kv_h"), 1)

            def kv_part(m, first):
                dve.wait_ge(*at("kv_tr", first + 1))
                last = v.tensor_copy(KVf[:, ds(m, 1), :].rearrange("p a n -> p (a n)"), aux[:, 1, 0:P + 1])
                last.then_inc(sem("kv_h"), 1)

            dve.wait_ge(*at("kv_ones", 1))
            kT_part(0, None)
            tok_part("k_tok", 0)
            vT_part(0, None)
            with dve.Fori(1, KT) as i:
                g0 = 7 * i - 4
                tok_part("v_tok", g0)
                kT_part(i, g0)
                kv_part(i - 1, g0 + 3)
                tok_part("k_tok", g0 + 4)
                vT_part(i, g0 + 3)
            g0 = 7 * KT - 4
            tok_part("v_tok", g0)
            kv_part(KT - 1, g0 + 3)

            with dve.Fori(0, 3) as i:
                for s in range(2):
                    m = 2 * i + s
                    dve.wait_ge(*at("q_a", m + 1))
                    v.scalar_tensor_tensor(out=t0[0][:], in0=t0[0][:], scalar=1.0, in1=t0[1][:],
                                           op0=ALU.min, op1=ALU.add).then_inc(sem("q_s"), 1)
                    dve.wait_ge(*at("q_s", m + 1))
                    dve.wait_ge(*at(f"q_num{1 - s}", i + s))
                    v.tensor_copy(XD["q_hi"][:], t0[0][:]).then_inc(sem("q_hi"), 1)
                    dve.wait_ge(*at("q_hi", m + 1))
                    v.tensor_tensor(XD["q_lo"][:], t0[0][:], XD["q_hi"][:].bitcast(fp32), ALU.subtract).then_inc(sem("q_lo"), 1)
                    dve.wait_ge(*at("q_dc", m + 1))
                    v.reciprocal(XD["rden"][:], XD["rden"][:]).then_inc(sem("q_rec"), 1)
                    dve.wait_ge(*at("q_rec", m + 1))
                    dve.wait_ge(*at(f"q_num{s}", i + 1))
                    v.tensor_tensor(f3(XD["rden"][:]), accf(1), f3(XD["rden"][:]), ALU.mult).then_inc(sem("q_mul"), 1)
                    dve.wait_ge(*at("q_mul", m + 1))
                    Hh, Hl = (x[:, ds(m, 1), :].rearrange("p a n -> p (a n)") for x in (H_hi, H_lo))
                    v.tensor_copy(Hh, XD["rden"][:]).then_inc(sem("q_ah"), 1)
                    dve.wait_ge(*at("q_ah", m + 1))
                    v.tensor_tensor(Hl, XD["rden"][:], Hh.bitcast(fp32), ALU.subtract).then_inc(sem("q_att"), 1)

            def from_tokens(tag, adds, ln, frees=()):
                for s_, v_ in frees:
                    dve.wait_ge(*at(s_, v_))
                def tile(i, s, addend):
                    tok = TOK[:, ds(2 * i + s, 1), :].rearrange("p a n -> p (a n)")
                    ps = acc[s][0:TP].rearrange("p c n -> p (c n)")[:, 0:D]
                    dve.wait_ge(*at(f"{tag}_yt{s}", i + 1))
                    if adds == 1:
                        dve.wait_ge(*at(f"{tag}_ad{s}", 16 * (i + 1)))
                    if adds == 2:
                        dve.wait_ge(*at(f"{tag}_aa{s}", i + 1))
                    if adds:
                        v.tensor_tensor(tok, ps, addend, ALU.add).then_inc(sem(f"{tag}_add{s}"), 1)
                    else:
                        v.tensor_copy(tok, ps).then_inc(sem(f"{tag}_add{s}"), 1)
                    dve.wait_ge(*at(f"{tag}_add{s}", i + 1))
                    tile_stats(ln, 2 * i + s)

                if adds == 2:
                    for t in range(NT):
                        tile(t // 2, t % 2, XC[f"aa{t % 4}"][:, 0, :])
                else:
                    with dve.Fori(0, NP) as i:
                        for s in range(2):
                            tile(i, s, XC[f"ad{s}"][:, 0, :])
                ln_terms(ln, (1e-8,) if tag == "t1" else (1e-5,))

            from_tokens("t1", 1, "lnl")
            split_tiles("l")

            def mlp(tag, wb, groups, scale, mish=False):
                with dve.Fori(0, groups) as g:
                    with dve.Fori(0, 3) as i:
                        for s in range(2):
                            n = 3 * g + i
                            Hh, Hl = (x[:, ds(2 * i + s, 1), :].rearrange("p a n -> p (a n)") for x in (H_hi, H_lo))
                            dve.wait_ge(*at(f"{tag}_up{s}", n + 1))
                            if mish:
                                ex, n2 = XD[f"m{1 + s}"][:], XD["m3"][:]
                                k = [6 * (2 * n + s)]

                                def step(ins):
                                    k[0] = k[0] + 1
                                    ins.then_inc(sem(f"{tag}_mish"), 1)
                                    dve.wait_ge(*at(f"{tag}_mish", k[0]))
                                step(v.tensor_scalar(ex, ex, 1e9, None, ALU.min))
                                step(v.scalar_tensor_tensor(out=n2, in0=ex, scalar=2.0, in1=ex, op0=ALU.add, op1=ALU.mult))
                                step(v.tensor_scalar(ex, n2, 2.0, None, ALU.add))
                                step(v.reciprocal(ex, ex))
                                step(v.tensor_tensor(n2, n2, ex, ALU.mult))
                                step(v.tensor_tensor(t0[s][:], t0[s][:], n2, ALU.mult))
                            dve.wait_ge(*at("w_done1", 6 * g + wb))
                            v.tensor_copy(Hh, t0[s][:]).then_inc(sem(f"{tag}_hi{s}"), 1)
                            dve.wait_ge(*at(f"{tag}_hi{s}", n + 1))
                            v.tensor_tensor(Hl, t0[s][:], Hh.bitcast(fp32), ALU.subtract).then_inc(sem(f"{tag}_lo{s}"), 1)
                    with dve.Fori(0, 3) as i:
                        for s in range(2):
                            dve.wait_ge(*at(f"w_done{s}", 6 * g + i + wb + 4))
                            dve.wait_ge(*at(f"{tag}_dn{s}", 3 * g + i))
                            v.scalar_tensor_tensor(out=yblock(2 * i + s), in0=accf(s), scalar=scale, in1=yblock(2 * i + s),
                                                   op0=ALU.mult, op1=ALU.add).then_inc(sem(f"{tag}_dn{s}"), 1)

            dve.wait_ge(*at("gnn_back", 16))
            mlp("ml", WBASE["MLP"], MLP_GROUPS, 1.0)
            from_tokens("t2", 2, "lnx")
            split_tiles("x")

            dve.wait_ge(*at("r_sum", 1))
            ch.link(v.tensor_reduce(pooled[:], aux[:, 1, 0:NT * KT].rearrange("p (i k) -> p k i", k=KT), AX.X, ALU.add))
            v.tensor_scalar(pooled[:], pooled[:], 1.0 / N, None, ALU.mult).then_inc(sem("r_pool"), 1)
            dve.wait_ge(*at("r_log", 1))
            dve.wait_ge(*at("rb_in", 16))
            ch.link(v.tensor_tensor(rt[0:1, 0:EXP], aux[0:1, 0, 0:EXP], rb[:], ALU.add))
            ch.link(v.max(rt[0:1, 8:16], rt[0:1, 0:8]))
            v.max_index(rti[0:1, 0:8], rt[0:1, 8:16], rt[0:1, 0:8]).then_inc(sem("r_idx"), 1)
            v.tensor_tensor(rt[0:1, 16:17], rt[0:1, 9:10], rt[0:1, 8:9], ALU.subtract).then_inc(sem("r_d"), 1)
            dve.wait_ge(*at("r_e", 1))
            ch.link(v.tensor_scalar(rt[0:1, 18:19], rt[0:1, 17:18], 1.0, None, ALU.add))
            ch.link(v.reciprocal(rt[0:1, 20:21], rt[0:1, 18:19]))
            v.tensor_tensor(rt[0:1, 21:22], rt[0:1, 20:21], rt[0:1, 17:18], ALU.mult).then_inc(sem("r_gates"), 1)
            dve.wait_ge(*at("r_gb", 1))
            ch.link(v.tensor_copy(gate[:, 0:TOPK], aux[:, 0, 8:8 + TOPK]))
            dve.wait_ge(*at("r_idx", 1))
            ers = [dve.value_load(rti[0:1, e:e + 1], min_val=0, max_val=EXP - 1) for e in range(TOPK)]
            ch.link(v.tensor_scalar(gb2[:], V[:, ds(ers[0] * KT + VC["ffn_b2"], KT)], gate[:, 0:1], None, ALU.mult))
            ch.link(v.scalar_tensor_tensor(out=gb2[:], in0=V[:, ds(ers[1] * KT + VC["ffn_b2"], KT)], scalar=gate[:, 1:2],
                                           in1=gb2[:], op0=ALU.mult, op1=ALU.add))
            dve.wait_ge(*at("x_lo0", NP))
            dve.wait_ge(*at("x_lo1", NP))
            for m in range(KT):
                last = v.tensor_scalar(Y[:, m, :], Y[:, m, :], gb2[:, m:m + 1], None, ALU.add)
            ch.link(last)
            for e in range(TOPK):
                args = (f"e{e}", WBASE["EXP"] + 6 * EXP_GROUPS * e, EXP_GROUPS, gate[:, e:e + 1])
                with dve.If(ers[e] == 2):
                    mlp(*args, mish=True)
                with dve.Else():
                    mlp(*args)
            from_tokens("t3", 0, "lnf")
            dve.wait_ge(*at("gb_in", 48))
            with dve.Fori(0, NP) as i:
                for s in range(2):
                    xh = TOK[:, ds(2 * i + s, 1), :].rearrange("p a n -> p (a n)")
                    dve.wait_ge(*at(f"f_n{s}", i + 1))
                    v.tensor_tensor(xh, xh, XA["gb"][:, 0, :], ALU.mult).then_inc(sem(f"f_m{s}"), 1)
                    dve.wait_ge(*at(f"f_m{s}", i + 1))
                    dve.wait_ge(*at("f_x2", 2 * i + s + 1))
                    v.tensor_tensor(xh, xh, XA["X2"][:, ds(2 * i + s, 1), :].rearrange("p a n -> p (a n)"), ALU.add).then_inc(sem(f"f_o{s}"), 1)


_INS = ["x", "src", "dst"] + ["L0_" + n for n in (
    "gnn_norm_g gnn_norm_b gnn_W1 gnn_a_src1 gnn_a_dst1 gnn_b1 gnn_W2 gnn_a_src2 gnn_a_dst2 gnn_b2 gnn_Wu gnn_bu "
    "mix_qkv_w mix_qkv_b mix_proj_w mix_proj_b mix_fc1_w mix_fc1_b mix_fc2_w mix_fc2_b mix_ln1_w mix_ln1_b "
    "mix_ln2_w mix_ln2_b ffn_router_w ffn_router_b ffn_w1 ffn_b1 ffn_w2 ffn_b2 ffn_ln_g ffn_ln_b").split()]


def kernel(**inputs):
    import numpy as _np
    import concourse.bacc as _bacc
    from concourse import mybir as _mybir
    from concourse.bass_utils import run_bass_kernel_spmd as _run

    nc = _bacc.Bacc("TRN2", target_bir_lowering=False, num_devices=1)
    arrays, args = {}, {}
    for name in _INS:
        a = _np.ascontiguousarray(inputs[name])
        arrays[f"in_{name}"] = a
        args[name.removeprefix("L0_")] = nc.dram_tensor(f"in_{name}", a.shape, _mybir.dt.from_np(a.dtype), kind="ExternalInput").ap()
    out = nc.dram_tensor("out", (N, D), _mybir.dt.from_np(_np.dtype("float32")), kind="ExternalOutput").ap()
    gps_layer(nc, args, out)
    r = _run(nc, [arrays], core_ids=[0])
    return r.results[0]["out"]
```
